# Optimizing a Trainium2 kernel written in Bass

```python
import numpy as np
import jax
import jax.numpy as jnp

def _softmax(x, axis=-1):
    return jax.nn.softmax(x, axis=axis)

def _gelu(x):
    return jax.nn.gelu(x, approximate=True)

def _silu(x):
    return jax.nn.silu(x)

def _sigmoid(x):
    return jax.nn.sigmoid(x)

def _layernorm(x, axis=-1, eps=1e-05):
    m = jnp.mean(x, axis=axis, keepdims=True)
    v = jnp.var(x, axis=axis, keepdims=True)
    return (x - m) / jnp.sqrt(v + eps)

def _scatter_add(tgt, idx, src, axis=0):
    return tgt.at[idx].add(src)

def _segment_sum(src, seg, n):
    return jax.ops.segment_sum(src, seg, n)
kernel_name = 'mk_macaron_d2_jaxref_r8_ed75b5'

def setup_inputs(seed: int=0):
    np.random.seed(seed)
    _w = jnp.asarray

    def _L0_attn_setup():
        import jax, jax.numpy as jnp
        import numpy as np
        NORM_EPS = 1e-06
        QK_SCALE = 1.0 / 128.0
        ROTARY_BASE = 1250
        INFTY_APPROX = 1e+30
        B, T, M, H, D = (2, 256, 128, 8, 128)

        def _rmsnorm(x, eps=NORM_EPS):
            ms = jnp.mean(jnp.square(x), axis=-1, keepdims=True)
            return x / jnp.sqrt(ms + eps)

        def _rope(x, base=ROTARY_BASE):
            length, width = (x.shape[-2], x.shape[-1])
            half = width // 2
            pos = jnp.arange(length, dtype=x.dtype)[:, None]
            freqs = jnp.power(jnp.asarray(base, x.dtype), -jnp.arange(half, dtype=x.dtype) / half)[None, :]
            rad = pos * freqs
            cos = jnp.cos(rad)[None, None]
            sin = jnp.sin(rad)[None, None]
            even, odd = jnp.split(x, 2, axis=-1)
            return jnp.concatenate([even * cos - odd * sin, even * sin + odd * cos], axis=-1)
        key = jax.random.key(seed)
        ks = jax.random.split(key, 5)
        std = M ** (-0.5)
        return {'x': jax.random.normal(ks[0], (B, T, M), jnp.float32), 'wq': jax.random.normal(ks[1], (M, H, D), jnp.float32) * std, 'wk': jax.random.normal(ks[2], (M, H, D), jnp.float32) * std, 'wv': jax.random.normal(ks[3], (M, H, D), jnp.float32) * std, 'wo': jax.random.normal(ks[4], (H, D, M), jnp.float32) * std}
    _L0_attn_in = _L0_attn_setup()

    def _L0_ffn_setup():
        import jax, jax.numpy as jnp
        import numpy as np
        D_MODEL = 128
        N_EXPERTS = 16
        TOP_K = 2
        EXPERT_DIM = 128
        SHARED_DIM = 256
        B, T = (2, 128)
        key = jax.random.key(seed)
        ks = jax.random.split(key, 7)
        std = 0.02
        return {'x': jax.random.normal(ks[0], (B, T, D_MODEL), dtype=jnp.float32), 'router_w': jax.random.normal(ks[1], (N_EXPERTS, D_MODEL), dtype=jnp.float32) * std, 'gate_up_w': jax.random.normal(ks[2], (N_EXPERTS, D_MODEL, 2 * EXPERT_DIM), dtype=jnp.float32) * std, 'down_w': jax.random.normal(ks[3], (N_EXPERTS, EXPERT_DIM, D_MODEL), dtype=jnp.float32) * std, 'shared_gate_w': jax.random.normal(ks[4], (SHARED_DIM, D_MODEL), dtype=jnp.float32) * std, 'shared_up_w': jax.random.normal(ks[5], (SHARED_DIM, D_MODEL), dtype=jnp.float32) * std, 'shared_down_w': jax.random.normal(ks[6], (D_MODEL, SHARED_DIM), dtype=jnp.float32) * std}
    _L0_ffn_in = _L0_ffn_setup()

    def _L1_attn_setup():
        import jax, jax.numpy as jnp
        import numpy as np
        B, L, C = (4, 128, 128)
        H = 8
        D = C // H
        MAX_SAMPLES = 32
        HALF_S = MAX_SAMPLES // 2
        S = 2 * HALF_S + 1
        K = 64
        MAX_FREQ = 16.0
        MIN_FREQ = 1.0

        def _silu(v):
            return v * jax.nn.sigmoid(v)
        key = jax.random.key(seed)
        ks = jax.random.split(key, 6)
        x = jax.random.normal(ks[0], (B, L, C), dtype=jnp.float32)
        wave_w = jax.random.normal(ks[1], (2 * H, C), dtype=jnp.float32) * 0.02
        wave_b = jnp.zeros((2 * H,), dtype=jnp.float32)
        kernel_w = jax.random.normal(ks[2], (H * K, C), dtype=jnp.float32) * (0.1 / np.sqrt(C))
        kernel_b = jnp.zeros((H * K,), dtype=jnp.float32)
        out_w = jax.random.normal(ks[3], (C, C), dtype=jnp.float32) * (0.1 / np.sqrt(C))
        return {'x': x, 'wave_w': wave_w, 'wave_b': wave_b, 'kernel_w': kernel_w, 'kernel_b': kernel_b, 'out_w': out_w}
    _L1_attn_in = _L1_attn_setup()

    def _L1_ffn_setup():
        import jax, jax.numpy as jnp
        import numpy as np
        N_EXPERT_CAPACITY = 2
        key = jax.random.key(seed)
        k1, k2, k3, k4 = jax.random.split(key, 4)
        B, S, D, E, F = (8, 128, 128, 8, 256)
        x = jax.random.normal(k1, (B, S, D), dtype=jnp.float32)
        choice_w = jax.random.uniform(k2, (E, D), dtype=jnp.float32, minval=-1.0, maxval=1.0) * (1.0 / np.sqrt(D))
        w1 = jax.random.uniform(k3, (E, D, F), dtype=jnp.float32, minval=-1.0, maxval=1.0) * (1.0 / np.sqrt(D))
        w2 = jax.random.uniform(k4, (E, F, D), dtype=jnp.float32, minval=-1.0, maxval=1.0) * (1.0 / np.sqrt(F))
        return {'x': x, 'choice_w': choice_w, 'w1': w1, 'w2': w2}
    _L1_ffn_in = _L1_ffn_setup()
    _d = {'L0_attn_x': _L0_attn_in['x'], 'L0_attn_wq': _L0_attn_in['wq'], 'L0_attn_wk': _L0_attn_in['wk'], 'L0_attn_wv': _L0_attn_in['wv'], 'L0_attn_wo': _L0_attn_in['wo'], 'L0_ffn_router_w': _L0_ffn_in['router_w'], 'L0_ffn_gate_up_w': _L0_ffn_in['gate_up_w'], 'L0_ffn_down_w': _L0_ffn_in['down_w'], 'L0_ffn_shared_gate_w': _L0_ffn_in['shared_gate_w'], 'L0_ffn_shared_up_w': _L0_ffn_in['shared_up_w'], 'L0_ffn_shared_down_w': _L0_ffn_in['shared_down_w'], 'L1_attn_wave_w': _L1_attn_in['wave_w'], 'L1_attn_wave_b': _L1_attn_in['wave_b'], 'L1_attn_kernel_w': _L1_attn_in['kernel_w'], 'L1_attn_kernel_b': _L1_attn_in['kernel_b'], 'L1_attn_out_w': _L1_attn_in['out_w'], 'L1_ffn_choice_w': _L1_ffn_in['choice_w'], 'L1_ffn_w1': _L1_ffn_in['w1'], 'L1_ffn_w2': _L1_ffn_in['w2']}
    _x0 = _d['L0_attn_x']
    _d['L0_attn_x'] = jax.random.normal(jax.random.fold_in(jax.random.key(seed), 1), (8, 256, 128), dtype=_x0.dtype)
    del _x0
    return _d

def reference(L0_attn_x, L0_attn_wq, L0_attn_wk, L0_attn_wv, L0_attn_wo, L0_ffn_router_w, L0_ffn_gate_up_w, L0_ffn_down_w, L0_ffn_shared_gate_w, L0_ffn_shared_up_w, L0_ffn_shared_down_w, L1_attn_wave_w, L1_attn_wave_b, L1_attn_kernel_w, L1_attn_kernel_b, L1_attn_out_w, L1_ffn_choice_w, L1_ffn_w1, L1_ffn_w2):

    def _L0_attn_ref(x, wq, wk, wv, wo):
        import jax, jax.numpy as jnp
        import numpy as np
        NORM_EPS = 1e-06
        QK_SCALE = 1.0 / 128.0
        ROTARY_BASE = 1250
        INFTY_APPROX = 1e+30
        B, T, M, H, D = (2, 256, 128, 8, 128)

        def _rmsnorm(x, eps=NORM_EPS):
            ms = jnp.mean(jnp.square(x), axis=-1, keepdims=True)
            return x / jnp.sqrt(ms + eps)

        def _rope(x, base=ROTARY_BASE):
            length, width = (x.shape[-2], x.shape[-1])
            half = width // 2
            pos = jnp.arange(length, dtype=x.dtype)[:, None]
            freqs = jnp.power(jnp.asarray(base, x.dtype), -jnp.arange(half, dtype=x.dtype) / half)[None, :]
            rad = pos * freqs
            cos = jnp.cos(rad)[None, None]
            sin = jnp.sin(rad)[None, None]
            even, odd = jnp.split(x, 2, axis=-1)
            return jnp.concatenate([even * cos - odd * sin, even * sin + odd * cos], axis=-1)
        q = jnp.einsum('bim,mhd->bhid', x, wq)
        k = jnp.einsum('bim,mhd->bhid', x, wk)
        v = jnp.einsum('bim,mhd->bhid', x, wv)
        q = _rmsnorm(q)
        k = _rmsnorm(k)
        q = _rope(q)
        k = _rope(k)
        mult = jnp.asarray(QK_SCALE ** 0.5, q.dtype)
        s = jnp.einsum('bhid,bhjd->bhij', q * mult, k * mult)
        t = s.shape[-1]
        mask = (jnp.arange(t)[:, None] < jnp.arange(t)[None, :]).astype(s.dtype)
        s = s - jnp.asarray(INFTY_APPROX, s.dtype) * mask[None, None]
        p = jax.nn.softmax(s, axis=-1)
        o = jnp.einsum('bhij,bhjd->bhid', p, v)
        return jnp.einsum('bhid,hdm->bim', o, wo)

    def _L0_ffn_ref(x, router_w, gate_up_w, down_w, shared_gate_w, shared_up_w, shared_down_w):
        import jax, jax.numpy as jnp
        import numpy as np
        D_MODEL = 128
        N_EXPERTS = 16
        TOP_K = 2
        EXPERT_DIM = 128
        SHARED_DIM = 256
        B, T = (2, 128)
        Bb, Tt, C = x.shape
        N = Bb * Tt
        E = gate_up_w.shape[0]
        logits = jnp.einsum('btc,ec->bte', x, router_w)
        top_vals, top_idx = jax.lax.top_k(logits, TOP_K)
        gates = jax.nn.sigmoid(top_vals)
        xf = x.reshape(N, C)
        sel = top_idx.reshape(N, TOP_K)
        gw = gates.reshape(N, TOP_K)
        w_full = jnp.zeros((N, E), dtype=x.dtype).at[jnp.arange(N)[:, None], sel].add(gw)
        gu = jnp.einsum('nc,ech->neh', xf, gate_up_w)
        gate, up = jnp.split(gu, 2, axis=-1)
        h = jax.nn.silu(gate) * up
        out_all = jnp.einsum('neh,ehc->nec', h, down_w)
        moe = jnp.einsum('ne,nec->nc', w_full, out_all).reshape(Bb, Tt, C)
        sg = jnp.einsum('btc,sc->bts', x, shared_gate_w)
        su = jnp.einsum('btc,sc->bts', x, shared_up_w)
        shared = jnp.einsum('bts,cs->btc', jax.nn.silu(sg) * su, shared_down_w)
        return moe + shared

    def _L1_attn_ref(x, wave_w, wave_b, kernel_w, kernel_b, out_w):
        import jax, jax.numpy as jnp
        import numpy as np
        B, L, C = (4, 128, 128)
        H = 8
        D = C // H
        MAX_SAMPLES = 32
        HALF_S = MAX_SAMPLES // 2
        S = 2 * HALF_S + 1
        K = 64
        MAX_FREQ = 16.0
        MIN_FREQ = 1.0

        def _silu(v):
            return v * jax.nn.sigmoid(v)
        Bb, Ll, Cc = x.shape
        wave = _silu(x @ wave_w.T + wave_b).reshape(Bb, Ll, 2, H)
        freq = jax.nn.sigmoid(wave[:, :, 0, :]) * (MAX_FREQ - MIN_FREQ) + MIN_FREQ
        phase = jnp.tanh(wave[:, :, 1, :]) * MAX_FREQ
        freq_avg = freq.mean(axis=-1)
        phase_avg = phase.mean(axis=-1)
        kernel = _silu(x @ kernel_w.T + kernel_b).reshape(Bb, Ll, H, K)
        w = kernel[:, :, :, :S]
        s_idx = jnp.arange(S, dtype=x.dtype) - HALF_S
        base = jnp.arange(Ll, dtype=x.dtype)
        pos = base[None, :, None] + s_idx[None, None, :] * freq_avg[:, :, None] + phase_avg[:, :, None]
        pos = jnp.clip(pos, 0.0, Ll - 1.0)
        lo = jnp.floor(pos).astype(jnp.int32)
        hi = jnp.minimum(lo + 1, Ll - 1)
        frac = pos - lo.astype(x.dtype)
        xh = x.reshape(Bb, Ll, H, D)
        b_ix = jnp.arange(Bb)[:, None, None]
        g_lo = xh[b_ix, lo]
        g_hi = xh[b_ix, hi]
        g = g_lo + frac[..., None, None] * (g_hi - g_lo)
        out_h = jnp.einsum('blshd,blhs->blhd', g, w)
        out = out_h.reshape(Bb, Ll, Cc)
        return _silu(out @ out_w.T)

    def _L1_ffn_ref(x, choice_w, w1, w2):
        import jax, jax.numpy as jnp
        import numpy as np
        N_EXPERT_CAPACITY = 2
        B, S, D = x.shape
        E = choice_w.shape[0]
        k = S * N_EXPERT_CAPACITY // E
        probs = jax.nn.softmax(jnp.einsum('bsd,ed->bse', x, choice_w), axis=-1)
        G, I = jax.lax.top_k(jnp.swapaxes(probs, -1, -2), k)
        x_in = jnp.take_along_axis(x[:, None, :, :], I[..., None], axis=2)
        h = jax.nn.silu(jnp.einsum('bekd,edf->bekf', x_in, w1))
        x_mlp = jnp.einsum('bekf,efd->bekd', h, w2)
        b_idx = jnp.arange(B)[:, None, None]
        out = jnp.zeros_like(x).at[b_idx, I].add(G[..., None] * x_mlp)
        return out
    x = L0_attn_x
    x = x + 0.5 * _L0_ffn_ref(_layernorm(x, axis=-1), L0_ffn_router_w, L0_ffn_gate_up_w, L0_ffn_down_w, L0_ffn_shared_gate_w, L0_ffn_shared_up_w, L0_ffn_shared_down_w)
    x = x + _L0_attn_ref(_layernorm(x, axis=-1), L0_attn_wq, L0_attn_wk, L0_attn_wv, L0_attn_wo)
    x = x + 0.5 * _L0_ffn_ref(_layernorm(x, axis=-1), L0_ffn_router_w, L0_ffn_gate_up_w, L0_ffn_down_w, L0_ffn_shared_gate_w, L0_ffn_shared_up_w, L0_ffn_shared_down_w)
    x = x + 0.5 * _L1_ffn_ref(_layernorm(x, axis=-1), L1_ffn_choice_w, L1_ffn_w1, L1_ffn_w2)
    x = x + _L1_attn_ref(_layernorm(x, axis=-1), L1_attn_wave_w, L1_attn_wave_b, L1_attn_kernel_w, L1_attn_kernel_b, L1_attn_out_w)
    x = x + 0.5 * _L1_ffn_ref(_layernorm(x, axis=-1), L1_ffn_choice_w, L1_ffn_w1, L1_ffn_w2)
    return x

_drawn_inputs = setup_inputs


def setup_inputs(seed=0):
    import zlib

    import numpy as np

    out = dict(_drawn_inputs(seed))
    spreads = {'L1_attn_wave_b': (0.0, 0.8), 'L1_attn_kernel_b': (0.0, 0.684)}
    factors = {'L0_ffn_router_w': 8.0,
     'L0_ffn_gate_up_w': 8.0,
     'L0_ffn_down_w': 8.0,
     'L0_ffn_shared_gate_w': 7.055,
     'L0_ffn_shared_up_w': 6.977,
     'L0_ffn_shared_down_w': 6.978,
     'L1_attn_wave_w': 5.459,
     'L1_attn_kernel_w': 4.781,
     'L1_attn_out_w': 3.419,
     'L1_ffn_choice_w': 4.558,
     'L1_ffn_w1': 4.205,
     'L1_ffn_w2': 4.078}
    for name, (base, spread) in spreads.items():
        noise = np.random.default_rng([zlib.crc32(name.encode()), seed]).standard_normal(out[name].shape)
        drawn = base * np.exp(spread * noise) if base else spread * noise
        out[name] = jnp.asarray(drawn.astype(out[name].dtype))
    for name, factor in factors.items():
        out[name] = (out[name] * factor).astype(out[name].dtype)
    return out
```

```python
import numpy as np
import concourse.bass as bass
from concourse import mybir
from contextlib import ExitStack

F32 = mybir.dt.float32
F16 = mybir.dt.float16
BF16 = mybir.dt.bfloat16
ALU = mybir.AluOpType
ACT = mybir.ActivationFunctionType
AX = mybir.AxisListType.X
ds = bass.ds

BATCH, SEQ, C = 8, 256, 128
P = 128
NT = BATCH * SEQ // P
TPB = SEQ // P
CHUNK = 512
NC = BATCH * SEQ // CHUNK
TPC = CHUNK // P
BPC = CHUNK // SEQ
LN_EPS = 1e-5
HALF = 0.5
E0, HID = 16, 128
U0 = E0 + 2
NH, HD = 8, 128
HG = 4
NG = NH // HG
RMS_EPS = 1e-6
ROPE_BASE = 1250
E1, FF = 8, 256
F1 = FF // P
U1 = E1 * F1
TOPK = SEQ * 2 // E1
WH, WK, WS = 8, 64, 33
WD = C // WH
MAX_FREQ, MIN_FREQ = 16.0, 1.0
SU = P // (2 * WH)
SG = -(-WS // SU)
UR = 4
PIECES = 3
POSK = PIECES * WS + 1
WSCALE = 64.0


def macaron_kernel(nc, a, out):
    ctx = ExitStack()
    with ctx:
        def sb(name, shape, dt=F32):
            return ctx.enter_context(nc.sbuf_tensor(name, shape, dt))

        def sem(name):
            return ctx.enter_context(nc.semaphore(name))

        psum = ctx.enter_context(nc.psum_tensor("psum", [P, 8, CHUNK], F32))

        def bank(i):
            return psum[:, i, :]

        x = sb("x", [P, NT, C])
        xn = sb("xn", [P, NT, C])
        xTh = sb("xTh", [P, NT * P], F16)
        xTl = sb("xTl", [P, NT * P], F16)
        ident = sb("ident", [P, P])
        neghalf = sb("neghalf", [P, NT])
        stats = sb("stats", [P, NT, 6])
        mv = sb("mv", [P, NT, 2])
        rstd = sb("rstd", [P, NT])
        rvar = sb("rvar", [P, NT])

        guh = sb("guh", [P, U0, 2 * HID], F16)
        gul = sb("gul", [P, U0, 2 * HID], F16)
        wdn = sb("wdn", [P, U0, C])
        rwh = sb("rwh", [P, E0], F16)
        rwl = sb("rwl", [P, E0], F16)
        rwr = sb("rwr", [P, E0])
        sel0 = sb("sel0", [64, U0, P], F16)
        gT0 = sb("gT0", [64, NT * P], F16)
        w1h = sb("w1h", [P, E1, FF], F16)
        w1l = sb("w1l", [P, E1, FF], F16)
        w2 = sb("w2", [P, U1, C])
        cwh = sb("cwh", [P, E1], F16)
        cwl = sb("cwl", [P, E1], F16)
        cwr = sb("cwr", [P, E1])
        sel1 = sb("sel1", [P, BATCH * E1, P], F16)
        gT1 = sb("gT1", [P, SEQ], F16)
        qkh = sb("qkh", [P, 2, NH * HD], F16)
        qkl = sb("qkl", [P, 2, NH * HD], F16)
        voh = sb("voh", [P, NH * C], F16)
        vol = sb("vol", [P, NH * C], F16)
        rawqk = sb("rawqk", [P, 2, NH * HD])
        rawvo = sb("rawvo", [P, 2, NH * HD])
        raww1 = rawqk[:, :, :].rearrange("p a (e f) -> p (a e) f", f=FF)
        work = sb("work", [P, 6, CHUNK])
        sg, su, hT = work[:, 0:2, :], work[:, 2:4, :], work[:, 4:6, :]
        zrow = sb("zrow", [1, CHUNK], F16)
        rt = sb("rt", [P, 6, NT, E0])
        rs = sb("rs", [P, 6, NT])
        g16 = sb("g16", [P, NT, E0], F16)
        revidx = sb("revidx", [P, E0])
        gst = sb("gst", [P, NT, 64])
        ARENA = 12032
        arena = sb("arena", [P, ARENA])
        off = [0]

        def part(n):
            off[0] += n
            assert off[0] <= ARENA, off[0]
            return arena[:, off[0] - n:off[0]]

        rawgu = part(U0 * 2 * HID).rearrange("p (u h) -> p u h", u=U0)
        off[0] = 0
        sq, rpA = sg, hT
        rpB = part(2 * CHUNK).rearrange("p (r c) -> p r c", r=2)
        qr = part(4 * CHUNK).rearrange("p (r c) -> p r c", r=4)
        qT = part(2 * HG * SEQ).rearrange("p (g h t) -> p g h t", g=2, h=HG)
        kT = part(2 * HG * SEQ).rearrange("p (g h t) -> p g h t", g=2, h=HG)
        VW = C + 1
        vb = part(2 * TPB * HG * VW).rearrange("p (g t h c) -> p g t h c", g=2, t=TPB, h=HG)
        pt = part(HG * 3 * P).rearrange("p (r c) -> p r c", r=HG)
        qn = sel1[:, :, :].rearrange("p a b -> p (a b)").bitcast(F32).rearrange("p (g u c) -> p g u c", g=2, u=4)
        cosd = part(TPB * HD).rearrange("p (t c) -> p t c", t=TPB)
        sind = part(TPB * HD).rearrange("p (t c) -> p t c", t=TPB)
        ss = sb("ss", [P, 4, HG])
        rms = sb("rms", [P, 4, HG])
        rq = sb("rq", [P, BATCH * NG, 4 * HG])
        rl = sb("rl", [P, 2, TPB])
        off[0] = 0
        selS = part(WS * 2 * P // 2).bitcast(F16).rearrange("p (s j l) -> p s j l", s=WS, j=2)
        kwt = part(SG * NT * P // 2).bitcast(F16).rearrange("p (g t) -> p g t", g=SG)
        selW = part(SU * P // 2).bitcast(F16).rearrange("p (s c) -> p s c", s=SU)
        uu = part(UR * CHUNK).rearrange("p (r c) -> p r c", r=UR)
        wsm, prod = work[:, 0:2, :], work[:, 2:6, :]
        sil = work[:, 0:2, :]
        wacc = rt[:, 0:2].rearrange("p a t e -> p (a t e)")
        yw = rt[:, 2:4].rearrange("p a t e -> p (a t e)")
        rawkw = sb("rawkw", [P, WK // SU, SU * WH])
        kb = sb("kb", [P, WK // SU])
        wwh = sb("wwh", [P, 2 * WH], F16)
        wwl = sb("wwl", [P, 2 * WH], F16)
        wwr = sb("wwr", [P, 2 * WH])
        wb = sb("wb", [P, 2 * WH])
        ow = sb("ow", [P, C])
        sgrid = sb("sgrid", [P, WS])
        tokpos = sb("tokpos", [P, NT])
        diffm = sb("diffm", [P, 4, P])
        wdnf = wdn[:, :, :].rearrange("p u c -> p (u c)")
        posT = wdnf[:, 0:NT * P // 2].bitcast(BF16)
        dxs = wdnf[:, NT * P // 2:NT * P // 2 + 2 * BPC * TPB * C].rearrange("p (r b t c) -> p r b t c", r=2, b=BPC, t=TPB)
        guf = guh[:, :, :].rearrange("p a b -> p (a b)")
        kwh = guf[:, 0:SG * P].rearrange("p (g d r) -> p g d r", g=SG, d=2)
        kwl = guf[:, SG * P:2 * SG * P].rearrange("p (g d r) -> p g d r", g=SG, d=2)
        pos = sb("pos", [P, NT, WS])
        posr = sb("posr", [P, NT, WS])
        pos16 = sb("pos16", [P, NT, WS], BF16)
        stag = gul[:, :, :].rearrange("p a b -> p (a b)")[:, 0:2 * NT * POSK].bitcast(F32).rearrange("p (t k) -> p t k", t=NT)
        wz = sb("wz", [P, NT, 2, WH])
        wav = sb("wav", [P, 4, NT])
        pT = work[0:64, 0, 0:SEQ]
        pW = work[0:64, 1:3, 0:SEQ]
        pD = work[0:64, 3, 0:SEQ]
        top8 = sb("top8", [64, 8])

        S = {}

        def s(name):
            if name not in S:
                S[name] = sem(name)
            return S[name]

        block = ctx.enter_context(nc.Block())
        stage_order = a["_stages"]

        def nth(i, per, j=0):
            return i * per + j + 1

        def wait_apart(eng, sem_, value):
            eng.wait_ge(sem_, value)
            eng.sem_inc(s("waited"), 1)

        def matmul3(pe, o, lh, ll, rh, rl_, last=None):
            nc.tensor.matmul(o, ll, rh, start=True, stop=False)
            nc.tensor.matmul(o, lh, rl_, start=False, stop=False)
            return nc.tensor.matmul(o, lh, rh, start=False, stop=True)

        @block.sync
        def _(sp):
            def ld(dst, src, name):
                sp.dma_start(dst, src).then_inc(s(name), 16)
            xv = a["L0_attn_x"].rearrange("b (t p) c -> p (b t) c", p=P)
            ld(x[:, :, :], xv, "ld_x")
            ld(ident[:, :], a["ident"], "ld_ident")
            ld(rwr[:, :], a["L0_ffn_router_w"], "ld_rw")
            ld(rawgu[:, 0:E0, :], a["L0_ffn_gate_up_w"].rearrange("e c h -> c e h"), "ld_gu")
            ld(rawgu[:, E0:U0, 0:HID], a["L0_ffn_shared_gate_w"].rearrange("c (u h) -> c u h", u=2), "ld_gu")
            ld(rawgu[:, E0:U0, HID:], a["L0_ffn_shared_up_w"].rearrange("c (u h) -> c u h", u=2), "ld_gu")
            ld(sel0[:, :, :], a["sel0"], "ld_sel0")
            ld(wdn[:, 0:E0, :], a["L0_ffn_down_w"].rearrange("e h c -> h e c"), "ld_dn")
            ld(wdn[:, E0:U0, :], a["L0_ffn_shared_down_w"].rearrange("(u h) c -> h u c", h=P), "ld_dn")
            ld(rawqk[:, 0, :], a["L0_attn_wq"].rearrange("m h d -> m (h d)"), "ld_qk")
            ld(rawqk[:, 1, :], a["L0_attn_wk"].rearrange("m h d -> m (h d)"), "ld_qk")
            ld(rawvo[:, 0, :], a["L0_attn_wv"].rearrange("d h m -> d (h m)"), "ld_vo")
            ld(rawvo[:, 1, :].rearrange("d (h m) -> d h m", h=NH), a["L0_attn_wo"].rearrange("h d m -> d h m"), "ld_vo")
            ld(w2[:, :, :], a["L1_ffn_w2"].rearrange("e (f p) d -> p (e f) d", p=P), "ld_w2")
            ld(cwr[:, :], a["L1_ffn_choice_w"], "ld_cw")
            ld(rawkw[:, :, :], a["L1_attn_kernel_w"], "ld_kw")
            ld(wwr[:, :], a["L1_attn_wave_w"], "ld_ww")
            ld(wb[:, :], a["L1_attn_wave_b"].rearrange("(o w) -> o w", o=1).broadcast_to([P, 2 * WH]), "ld_wb")
            ld(ow[:, :], a["L1_attn_out_w"], "ld_ow")
            ld(sgrid[:, :], a["sgrid"], "ld_sg")
            ld(tokpos[:, :], a["tokpos"], "ld_sg")
            ld(diffm[:, :, :], a["diffm"], "ld_df")
            for d in range(2):
                ld(kb[d * P // 2:(d + 1) * P // 2, :], a["L1_attn_kernel_b"], "ld_kb")
            if "AT" in stage_order:
                sp.wait_ge(s("gu_split"), 1)
                ld(cosd[:, :, :], a["cosd"], "ld_cos")
                ld(sind[:, :, :], a["sind"], "ld_cos")
            if "F1" in stage_order:
                if "AT" in stage_order:
                    sp.wait_ge(s("qk_split"), 1)
                else:
                    sp.wait_ge(s("ld_qk"), 32)
                ld(raww1, a["L1_ffn_w1"].rearrange("e d f -> d e f"), "ld_w1")
            if "AT" in stage_order:
                sp.wait_ge(s("at_done"), 1)
            if "F1" in stage_order:
                ld(sel1[:, :, :], a["sel1"], "ld_sel1")
            if "LA" in stage_order:
                ld(selS[0:POSK, :, :, :], a["selS"], "ld_selS")
                ld(selW, a["selW"], "ld_selS")
            sp.wait_ge(s("x_final"), 1)
            sp.dma_start(out.rearrange("b (t p) c -> p (b t) c", p=P), x[:, :, :]).then_inc(s("stored"), 16)
            sp.wait_ge(s("stored"), 16)

        def prep_vector(dve, use):
            def statistics(c):
                for k in range(TPC):
                    t = c * TPC + k
                    nc.vector.bn_stats(stats[:, t, :], x[:, t, :]).then_inc(s("stats"), 1)

            def moments(c):
                dve.wait_ge(s("stats"), nth(use, NT, (c + 1) * TPC - 1))
                for k in range(TPC):
                    last = nc.vector.bn_aggr(mv[:, c * TPC + k, :], stats[:, c * TPC + k, :])
                last.then_inc(s("moments"), 1)

            def normalise(c):
                dve.wait_ge(s("rstd"), nth(use, NC, c))
                for k in range(TPC):
                    t = c * TPC + k
                    last = nc.vector.tensor_scalar(xn[:, t, :], x[:, t, :], mv[:, t, 0:1], rstd[:, t:t + 1],
                                                   ALU.subtract, ALU.mult)
                last.then_inc(s("xn_ready"), 1)

            def low(c):
                dve.wait_ge(s("xh_ready"), nth(use, NC, c))
                cs = slice(c * CHUNK, (c + 1) * CHUNK)
                nc.vector.tensor_tensor(xTl[:, cs], bank(6 + c % 2), xTh[:, cs], ALU.subtract).then_inc(s("xT_ready"), 1)
            statistics(0)
            for c in range(NC + 3):
                if c + 1 < NC:
                    statistics(c + 1)
                if c < NC:
                    moments(c)
                if 0 <= c - 1 < NC:
                    normalise(c - 1)
                if 0 <= c - 3 < NC:
                    low(c - 3)

        def prep_gpsimd(pool, use):
            for c in range(NC):
                ts = slice(c * TPC, (c + 1) * TPC)
                pool.wait_ge(s("moments"), nth(use, NC, c))
                nc.gpsimd.tensor_scalar(rvar[:, ts], mv[:, ts, 1], LN_EPS, None, ALU.add).then_inc(s("rvar"), 1)
                pool.wait_ge(s("rvar"), nth(use, NC, c))
                nc.gpsimd.tensor_tensor(rstd[:, ts], rvar[:, ts], neghalf[:, ts], ALU.pow).then_inc(s("rstd"), 1)

        def prep_tensor(pe, use):
            for c in range(NC):
                pe.wait_ge(s("xn_ready"), nth(use, NC, c))
                pe.wait_ge(s("xT_ready"), nth(use, NC, c))
                for k in range(TPC):
                    last = nc.tensor.transpose(bank(6 + c % 2)[:, k * P:(k + 1) * P], xn[:, c * TPC + k, :],
                                               ident[:, :])
                last.then_inc(s("tp_ready"), 1)

        def prep_scalar(act, use):
            for c in range(NC):
                act.wait_ge(s("tp_ready"), nth(use, NC, c))
                nc.scalar.activation(xTh[:, c * CHUNK:(c + 1) * CHUNK], bank(6 + c % 2),
                                     ACT.Copy).then_inc(s("xh_ready"), 1)

        XT0 = 2

        def all_xT(eng, use):
            eng.wait_ge(s("xT_ready"), XT0 + NC * (use + 1))

        def route0_tensor(pe, use, puse):
            all_xT(pe, puse)
            if use == 0:
                pe.wait_ge(s("rw_split"), 1)
            for t in range(NT):
                last = matmul3(pe, bank(0)[:, t * E0:(t + 1) * E0], xTh[:, t * P:(t + 1) * P],
                               xTl[:, t * P:(t + 1) * P], rwh[:, :], rwl[:, :])
            last.then_inc(s("logit0"), 1)
            pe.wait_ge(s("gate0"), use + 1)
            for c in range(NC):
                for k in range(TPC):
                    last = nc.tensor.transpose(psum[0:64, 1 + c, k * P:(k + 1) * P], gst[:, c * TPC + k, :], ident[:, :])
                last.then_inc(s("gT0_psum"), 1)

        def route0_scalar(act, use):
            act.wait_ge(s("top2"), use + 1)
            nc.scalar.activation(rs[:, 4:6, :], rs[:, 2:4, :], ACT.Sigmoid, scale=1.0 / WSCALE).then_inc(s("sig2"), 1)
            for c in range(NC):
                act.wait_ge(s("gT0_psum"), nth(use, NC, c))
                nc.scalar.activation(gT0[:, c * CHUNK:(c + 1) * CHUNK], psum[0:64, 1 + c, :],
                                     ACT.Copy).then_inc(s("gT0"), 1)

        def route0_vector(dve, use):
            n = [0]

            def step(ins):
                n[0] += 1
                ins.then_inc(s("route0_step"), 1)
                dve.wait_ge(s("route0_step"), ROUTE0_STEPS * use + n[0])

            def eachtile(v):
                return v.unsqueeze(2).broadcast_to([P, NT, E0])
            L = rt[:, 0]
            dve.wait_ge(s("logit0"), use + 1)
            step(nc.vector.tensor_copy(L, bank(0)[:, 0:NT * E0].rearrange("p (t e) -> p t e", t=NT)))
            for r in range(2):
                m = rs[:, 2 + r, :]
                k = rs[:, r, :]
                key, one = rt[:, 1], rt[:, 2 + r]
                step(nc.vector.tensor_reduce(m, L, AX, ALU.max))
                step(nc.vector.tensor_tensor(key, L, eachtile(m), ALU.is_equal))
                step(nc.vector.tensor_tensor(key, key, revidx[:, :].unsqueeze(1).broadcast_to([P, NT, E0]), ALU.mult))
                step(nc.vector.tensor_reduce(k, key, AX, ALU.max))
                step(nc.vector.tensor_tensor(one, key, eachtile(k), ALU.is_equal))
                if r == 0:
                    step(nc.vector.scalar_tensor_tensor(L, one, -1e30, L, ALU.mult, ALU.add))
            nc.vector.tensor_copy(rs[:, 0, 0:1], rs[:, 2, 0:1]).then_inc(s("top2"), 1)
            dve.wait_ge(s("sig2"), use + 1)
            step(nc.vector.tensor_tensor(rt[:, 4], rt[:, 2], eachtile(rs[:, 4, :]), ALU.mult))
            step(nc.vector.tensor_tensor(rt[:, 5], rt[:, 3], eachtile(rs[:, 5, :]), ALU.mult))
            step(nc.vector.tensor_tensor(rt[:, 1], rt[:, 4], rt[:, 5], ALU.add))
            step(nc.vector.tensor_copy(g16[:, :, :], rt[:, 1]))
            step(nc.vector.tensor_copy(gst[:, :, 0:E0], g16[:, :, :]))
            nc.vector.tensor_tensor(gst[:, :, 32:32 + E0], rt[:, 1], g16[:, :, :],
                                    ALU.subtract).then_inc(s("gate0"), 1)

        ROUTE0_STEPS = 1 + 6 + 5 + 5

        def ffn0_tensor(pe, use, puse):
            if use == 0:
                pe.wait_ge(s("gu_split"), 1)
                pe.wait_ge(s("ld_sel0"), 16)
                pe.wait_ge(s("ld_dn"), 32)
            pe.wait_ge(s("gT0"), NC * (use + 1))

            def up(c, u, r, i):
                cs = ds(c * CHUNK, CHUNK)
                pe.wait_ge(s("hT_ready"), nth(i, 2, r))
                for half, b in ((0, 0), (1, 2)):
                    ws = ds(half * HID, HID)
                    last = matmul3(pe, bank(b + r), guh[:, u, ws], gul[:, u, ws], xTh[:, cs], xTl[:, cs])
                    if half == 0:
                        last.then_inc(s("g_ready"), 1)
                nc.tensor.matmul(bank(4 + r), sel0[:, u, :], gT0[:, cs], start=True, stop=True).then_inc(s("u_ready"), 1)

            def down(u, r, i):
                pe.wait_ge(s("hT_ready"), H0 + nth(i, 2, r))
                for k in range(TPC):
                    last = nc.tensor.matmul(bank(6)[:, k * P:(k + 1) * P], hT[:, r, k * P:(k + 1) * P],
                                            wdn[:, u, :], start=False, stop=True, skip_group_check=True)
                last.then_inc(s("down_done"), 1)

            NP = U0 // 2
            with pe.Fori(0, NC) as c:
                base = (use * NC + c) * NP
                up(c, ds(0, 1), 0, base)
                pe.wait_ge(s("acc_free"), nth(use * NC + c, 1))
                nc.tensor.matmul(bank(6), zrow[:, 0:P], zrow[:, :], start=True, stop=False, skip_group_check=True)
                with pe.Fori(0, NP - 1) as k:
                    up(c, ds(k * 2 + 1, 1), 1, base + k)
                    down(ds(k * 2, 1), 0, base + k)
                    up(c, ds(k * 2 + 2, 1), 0, base + k + 1)
                    down(ds(k * 2 + 1, 1), 1, base + k)
                up(c, ds(U0 - 1, 1), 1, base + (NP - 1))
                down(ds(U0 - 2, 1), 0, base + (NP - 1))
                down(ds(U0 - 1, 1), 1, base + (NP - 1))

        H0 = 2

        def ffn0_scalar(act, use):
            with act.Fori(0, NC * U0 // 2) as i:
                for r in range(2):
                    act.wait_ge(s("g_ready"), nth(use * (NC * U0 // 2) + i, 2, r))
                    act.wait_ge(s("su_ready"), nth(use * (NC * U0 // 2) + i, 2, r))
                    nc.scalar.activation(sg[:, r, :], bank(r), ACT.Silu, scale=1.0 / WSCALE).then_inc(s("sg_ready"), 1)

        def ffn0_vector(dve, use):
            NP = U0 // 2
            with dve.Fori(0, NC) as c:
                with dve.Fori(0, NP) as k:
                    i = (use * NC + c) * NP + k
                    for r in range(2):
                        dve.wait_ge(s("sg_ready"), nth(i, 2, r))
                        dve.wait_ge(s("u_ready"), nth(i, 2, r))
                        nc.vector.tensor_tensor(su[:, r, :], sg[:, r, :], bank(2 + r), ALU.mult).then_inc(s("su_ready"), 1)
                        dve.wait_ge(s("su_ready"), H0 + nth(i, 2, r))
                        dve.wait_ge(s("down_done"), nth(i, 2, r))
                        nc.vector.tensor_tensor(hT[:, r, :], su[:, r, :], bank(4 + r), ALU.mult).then_inc(s("hT_ready"), 1)
                dve.wait_ge(s("down_done"), H0 + nth(use * NC + c, U0, U0 - 1))
                xc = x[:, ds(c * TPC, TPC), :].rearrange("p t c -> p (t c)")
                nc.vector.scalar_tensor_tensor(xc, bank(6), HALF / WSCALE, xc, ALU.mult, ALU.add).then_inc(s("acc_free"), 1)
            dve.wait_ge(s("acc_free"), 1 + NC * (use + 1))

        QKU = 2 * TPB
        AT_ROUNDS = BATCH * NG
        R0 = 2 * QKU

        def at_loop(eng, emit):
            def rd(b, k):
                return (b + k // NG, k % NG, b * NG + k)
            emit(None, None, None, rd(0, 0))
            emit(None, None, rd(0, 0), rd(0, 1))
            emit(None, rd(0, 0), rd(0, 1), rd(0, 2))
            with eng.Fori(0, BATCH - 2) as b:
                for k in range(NG):
                    emit(rd(b, k), rd(b, k + 1), rd(b, k + 2), rd(b, k + 3))
            b = BATCH - 2
            emit(rd(b, 0), rd(b, 1), rd(b, 2), rd(b, 3))
            emit(rd(b, 1), rd(b, 2), rd(b, 3), None)
            emit(rd(b, 2), rd(b, 3), None, None)
            emit(rd(b, 3), None, None, None)

        def behind(last, core, h):
            rnd, hh = (last, h + 2) if h < 2 else (core, h - 2)
            return (rnd, hh) if rnd else None

        def at_tensor(pe, puse):
            pe.wait_ge(s("ld_vo"), 32)
            for h in range(NH):
                hs = slice(h * HD, (h + 1) * HD)
                last = nc.tensor.matmul(psum[:, h // HG, (h % HG) * C:(h % HG + 1) * C], rawvo[:, 0, hs],
                                        rawvo[:, 1, hs], start=True, stop=True)
            last.then_inc(s("vo_psum"), 1)
            prep_tensor(pe, puse)
            all_xT(pe, puse)
            pe.wait_ge(s("qk_split"), 1)
            pe.wait_ge(s("vo_split"), 1)

            def emit(last_, core, turn_, proj_):
                def project(u):
                    b, g, j = proj_
                    pe.wait_ge(s("qn_ready"), nth(j, QKU, u))
                    tok = ds(b * SEQ + (u // 2) * P, P)
                    cols = slice(g * CHUNK, (g + 1) * CHUNK)
                    matmul3(pe, bank(u % 2), xTh[:, tok], xTl[:, tok], qkh[:, u % 2, cols],
                            qkl[:, u % 2, cols]).then_inc(s("pj_ready"), 1)

                def project_v(t):
                    b, g, j = turn_
                    pe.wait_ge(s("vb_ready"), nth(j, TPB, t))
                    tok = ds(b * SEQ + t * P, P)
                    cols = slice(g * CHUNK, (g + 1) * CHUNK)
                    matmul3(pe, bank(2), xTh[:, tok], xTl[:, tok], voh[:, cols], vol[:, cols]).then_inc(s("v_ready"), 1)

                def turn(u):
                    j = turn_[2]
                    pe.wait_ge(s("rot_ready"), R0 + nth(j, QKU, u))
                    pe.wait_ge(s("qkT_ready"), nth(j, QKU, u))
                    for h in range(HG):
                        last = nc.tensor.transpose(bank(3)[:, h * P:(h + 1) * P], qr[:, u, h * HD:(h + 1) * HD], ident[:, :])
                    last.then_inc(s("tr_ready"), 1)

                def scores(h):
                    b, g, i = core
                    pe.wait_ge(s("qkT_ready"), 1 + nth(i, QKU, QKU - 1))
                    pe.wait_ge(s("exp_ready"), nth(i, HG, h))
                    nc.tensor.matmul(bank(4 + h % 2)[:, 0:SEQ], kT[:, g, h, 0:P], qT[:, g, h, :], start=True, stop=True)
                    nc.tensor.matmul(bank(4 + h % 2)[:, SEQ:SEQ + P], kT[:, g, h, P:SEQ], qT[:, g, h, P:SEQ],
                                     start=True, stop=True).then_inc(s("sc_ready"), 1)

                def values(due):
                    (b, g, i), h = due
                    pe.wait_ge(s("mask_ready"), nth(i, HG, h))
                    pe.wait_ge(s("vb_ready"), 1 + nth(i, TPB, TPB - 1))
                    pe.wait_ge(s("pv_taken"), nth(i, HG, h))
                    o = bank(6 + h % 2)
                    nc.tensor.matmul(o[:, 0:VW], pt[:, h, 0:P], vb[:, g, 0, h, :], start=True, stop=True)
                    nc.tensor.matmul(o[:, SEQ:SEQ + VW], pt[:, h, P:SEQ], vb[:, g, 0, h, :], start=True, stop=False)
                    nc.tensor.matmul(o[:, SEQ:SEQ + VW], pt[:, h, SEQ:SEQ + P], vb[:, g, 1, h, :],
                                     start=False, stop=True).then_inc(s("pv_ready"), 1)
                for h in range(HG):
                    if proj_ and h % 2 == 0:
                        project(h)
                    if core:
                        scores(h)
                    if proj_ and h % 2 == 0:
                        project(h + 1)
                    if turn_ and h == 1:
                        turn(0)
                        project_v(0)
                    if turn_ and h == 2:
                        turn(1)
                    if turn_ and h == 3:
                        turn(3)
                    if behind(last_, core, h):
                        values(behind(last_, core, h))
                    if turn_ and h == 2:
                        turn(2)
                        project_v(1)
            at_loop(pe, emit)

        def at_scalar(act, puse):
            split_act(act, qkh[:, :, :].rearrange("p a b -> p (a b)"), rawqk[:, :, :].rearrange("p a b -> p (a b)"), "ld_qk", 32)
            act.wait_ge(s("vo_psum"), 1)
            nc.scalar.activation(voh[:, :], psum[:, 0:2, :].rearrange("p a b -> p (a b)"), ACT.Copy,
                                 scale=WSCALE).then_inc(s("hi_vo"), 1)
            prep_scalar(act, puse)
            act.preload_act_table(ACT.Exp)
            act.wait_ge(s("vb_ones"), 1)

            def emit(last_, core, turn_, proj_):
                def exps(h):
                    b, g, i = core
                    act.wait_ge(s("sc_ready"), nth(i, HG, h))
                    act.wait_ge(s("pv_ready"), nth(i, HG, h))
                    act.wait_ge(s("rq_ready"), nth(i, TPB, TPB - 1))
                    nc.scalar.activation(pt[:, h, 0:SEQ], bank(4 + h % 2)[:, 0:SEQ], ACT.Exp,
                                         scale=rq[:, ds(i, 1), HG + h])
                    nc.scalar.activation(pt[:, h, SEQ:SEQ + P], bank(4 + h % 2)[:, SEQ:SEQ + P], ACT.Exp,
                                         scale=rq[:, ds(i, 1), 3 * HG + h]).then_inc(s("exp_ready"), 1)

                def squares(u):
                    j = proj_[2]
                    act.wait_ge(s("pj_ready"), nth(j, QKU, u))
                    act.wait_ge(s("ss_ready"), nth(j, QKU, u))
                    nc.scalar.activation(sq[:, u % 2, :], bank(u % 2), ACT.Square).then_inc(s("sq_ready"), 1)

                def copy_out(u):
                    b, g, j = proj_
                    act.wait_ge(s("rot_ready"), nth(j, QKU, u))
                    if u % 2 == 0:
                        act.wait_ge(s("rq_ready"), nth(j, TPB, u // 2))
                        for h in range(HG):
                            hs = slice(h * HD, (h + 1) * HD)
                            last = nc.scalar.activation(qn[:, g, u, hs], bank(0)[:, hs], ACT.Copy,
                                                        scale=rq[:, ds(j, 1), u * HG + h])
                    else:
                        last = nc.scalar.activation(qn[:, g, u, :], bank(1), ACT.Copy)
                    last.then_inc(s("qn_ready"), 1)

                def turned(u):
                    b, g, j = turn_
                    act.wait_ge(s("tr_ready"), QKU + nth(j, QKU, u))
                    dst = (qT, kT)[u % 2][:, g, :, (u // 2) * P:(u // 2 + 1) * P]
                    nc.scalar.activation(dst, bank(3).rearrange("p (h t) -> p h t", h=HG),
                                         ACT.Copy).then_inc(s("qkT_ready"), 1)

                def values_out(t):
                    b, g, j = turn_
                    act.wait_ge(s("v_ready"), nth(j, TPB, t))
                    if last_:
                        act.wait_ge(s("pv_ready"), HG + nth(last_[2], HG, HG - 1))
                    nc.scalar.activation(vb[:, g, t, :, 0:C], bank(2).rearrange("p (h c) -> p h c", h=HG),
                                         ACT.Copy).then_inc(s("vb_ready"), 1)
                for h in range(HG):
                    if core:
                        exps(h)
                    if proj_ and h % 2 == 0:
                        squares(h)
                        squares(h + 1)
                    if turn_ and h == 1:
                        turned(0)
                    if turn_ and h == 2:
                        turned(1)
                        values_out(0)
                    if turn_ and h == 3:
                        turned(2)
                    if proj_ and h % 2 == 1:
                        copy_out(h - 1)
                        copy_out(h)
                    if turn_ and h == 3:
                        turned(3)
                        values_out(1)
            at_loop(act, emit)

        def at_vector(dve, puse):
            split_dve(dve, qkl[:, :, :].rearrange("p a b -> p (a b)"), rawqk[:, :, :].rearrange("p a b -> p (a b)"),
                      qkh[:, :, :].rearrange("p a b -> p (a b)"), "ld_qk", "qk_split")
            dve.wait_ge(s("hi_vo"), 1)
            nc.vector.scalar_tensor_tensor(vol[:, :], psum[:, 0:2, :].rearrange("p a b -> p (a b)"), WSCALE, voh[:, :],
                                           ALU.mult, ALU.subtract).then_inc(s("vo_split"), 1)
            prep_vector(dve, puse)
            dve.wait_ge(s("ld_cos"), 32)
            nc.vector.memset(vb[:, :, :, :, C:VW].rearrange("p g t h c -> p (g t h) c"), WSCALE).then_inc(s("vb_ones"), 1)

            def emit(last_, core, turn_, proj_):
                def sums(u):
                    j = proj_[2]
                    dve.wait_ge(s("sq_ready"), nth(j, QKU, u))
                    nc.vector.tensor_reduce(ss[:, u, :], sq[:, u % 2, :].rearrange("p (h d) -> p h d", h=HG), AX,
                                            ALU.add).then_inc(s("ss_ready"), 1)

                def cosines(u):
                    b, g, j = turn_
                    dve.wait_ge(s("qn_ready"), 2 + nth(j, QKU, u))
                    dve.wait_ge(s("rot_ready"), R0 - 2 + nth(j, QKU, u))
                    cs = cosd[:, u // 2, :].unsqueeze(1).broadcast_to([P, HG, HD])
                    nc.vector.tensor_tensor(rpA[:, u % 2, :].rearrange("p (h d) -> p h d", h=HG),
                                            qn[:, g, u, :].rearrange("p (h d) -> p h d", h=HG), cs,
                                            ALU.mult).then_inc(s("cos_ready"), 1)

                def rotated(u):
                    b, g, j = turn_
                    dve.wait_ge(s("cos_ready"), nth(j, QKU, u))
                    dve.wait_ge(s("sin_ready"), nth(j, QKU, u))
                    dve.wait_ge(s("tr_ready"), nth(j, QKU, u))
                    nc.vector.tensor_tensor(qr[:, u, :], rpA[:, u % 2, :], rpB[:, u % 2, :],
                                            ALU.add).then_inc(s("rot_ready"), 1)

                def add_values(due):
                    (b, g, i), h = due
                    o = bank(6 + h % 2)
                    dve.wait_ge(s("pv_ready"), HG + nth(i, HG, h))
                    nc.vector.reciprocal(rl[:, h % 2, :], o.rearrange("p (t c) -> p t c", t=TPB)[:, :, C]).then_inc(s("rl_ready"), 1)
                    dve.wait_ge(s("rl_ready"), nth(i, HG, h))
                    dve.wait_ge(s("pv_taken"), 1 + nth(i, HG, h))
                    for t in range(TPB):
                        xt = x[:, ds(b * TPB + t, 1), :].rearrange("p o c -> p (o c)")
                        last = nc.vector.scalar_tensor_tensor(xt, o[:, t * SEQ:t * SEQ + C], rl[:, h % 2, t:t + 1], xt,
                                                              ALU.mult, ALU.add)
                    last.then_inc(s("pv_taken"), 1)
                for h in range(HG):
                    if turn_ and h == 0:
                        cosines(0)
                    if turn_ and h == 1:
                        cosines(1)
                    if turn_ and h == 2:
                        cosines(3)
                    if proj_ and h % 2 == 0:
                        sums(h)
                        sums(h + 1)
                    if turn_ and h == 0:
                        rotated(0)
                    if turn_ and h == 1:
                        rotated(1)
                        cosines(2)
                        rotated(2)
                    if turn_ and h == 2:
                        rotated(3)
                    if behind(last_, core, h):
                        add_values(behind(last_, core, h))
            at_loop(dve, emit)
            dve.wait_ge(s("pv_taken"), 2 + AT_ROUNDS * HG)
            dve.sem_inc(s("at_done"), 1)

        def at_gpsimd(pool, puse):
            prep_gpsimd(pool, puse)

            def emit(last_, core, turn_, proj_):
                def scale(t):
                    b, g, j = proj_
                    wait_apart(pool, s("ss_ready"), 2 + nth(j, QKU, 2 * t + 1))
                    nc.gpsimd.tensor_scalar(rms[:, 2 * t:2 * t + 2, :], ss[:, 2 * t:2 * t + 2, :], RMS_EPS * HD * WSCALE ** 2,
                                            None, ALU.add).then_inc(s("rms_ready"), 1)
                    pool.wait_ge(s("rms_ready"), nth(j, TPB, t))
                    nc.gpsimd.tensor_tensor(rq[:, ds(j, 1), 2 * t * HG:(2 * t + 2) * HG],
                                            rms[:, 2 * t:2 * t + 2, :].rearrange("p u h -> p (u h)"), neghalf[:, 0:2 * HG],
                                            ALU.pow).then_inc(s("rq_ready"), 1)

                def sines(u):
                    b, g, j = turn_
                    pool.wait_ge(s("qn_ready"), 2 + nth(j, QKU, u))
                    pool.wait_ge(s("rot_ready"), R0 - 2 + nth(j, QKU, u))
                    sn = sind[:, u // 2, :].unsqueeze(1).broadcast_to([P, HG, HD])
                    half = HD // 2
                    for k in range(2):
                        last = nc.gpsimd.tensor_tensor(
                            rpB[:, u % 2, :].rearrange("p (h d) -> p h d", h=HG)[:, :, k * half:(k + 1) * half],
                            qn[:, g, u, :].rearrange("p (h d) -> p h d", h=HG)[:, :, (1 - k) * half:(2 - k) * half],
                            sn[:, :, k * half:(k + 1) * half], ALU.mult)
                    last.then_inc(s("sin_ready"), 1)

                def mask(h):
                    b, g, i = core
                    wait_apart(pool, s("exp_ready"), 2 + nth(i, HG, h))
                    v = pt[:, h, :].rearrange("p (n t) -> p n t", t=P)[:, 0:3:2, :]
                    nc.gpsimd.affine_select(out=v, in_=v, compare_op=ALU.is_ge, fill=0.0, base=0,
                                            pattern=[[0, 2], [1, P]], channel_multiplier=-1).then_inc(s("mask_ready"), 1)
                for h in range(HG):
                    if turn_ and h < 3:
                        sines((0, 1, 3)[h])
                    if turn_ and h == 1:
                        sines(2)
                    if proj_ and h % 2 == 0:
                        scale(h // 2)
                    if core:
                        mask(h)
            at_loop(pool, emit)

        probs = rt[:, 1].rearrange("p t e -> p (t e)")[:, 0:NT * E1]

        def route1_tensor(pe, use, puse):
            all_xT(pe, puse)
            if use == 0:
                pe.wait_ge(s("cw_split"), 1)
            for t in range(NT):
                last = matmul3(pe, bank(0)[:, t * E1:(t + 1) * E1], xTh[:, t * P:(t + 1) * P],
                               xTl[:, t * P:(t + 1) * P], cwh[:, :], cwl[:, :])
            last.then_inc(s("logit1"), 1)
            pe.wait_ge(s("prob1"), use + 1)
            for t in range(TPB):
                last = nc.tensor.transpose(psum[0:64, 1, t * P:(t + 1) * P], probs[:, t * 64:(t + 1) * 64], ident[:, :])
            last.then_inc(s("probT"), 1)

        def route1_scalar(act, use):
            act.wait_ge(s("shift1"), use + 1)
            v = rt[:, 0].rearrange("p t e -> p (t e)")[:, 0:NT * E1]
            nc.scalar.activation(v, v, ACT.Exp, scale=1.0 / WSCALE).then_inc(s("exp1"), 1)
            act.preload_act_table(ACT.Silu)

        ROUTE1_STEPS = 1 + 3 + 1 + 16 + 2

        def route1_vector(dve, use):
            n = [0]

            def step(ins):
                n[0] += 1
                ins.then_inc(s("route1_step"), 1)
                dve.wait_ge(s("route1_step"), ROUTE1_STEPS * use + n[0])

            def tiles(v):
                return v.rearrange("p t e -> p (t e)")[:, 0:NT * E1].rearrange("p (t e) -> p t e", e=E1)

            def eachtile(v):
                return v.unsqueeze(2).broadcast_to([P, NT, E1])
            L = bank(0)[:, 0:NT * E1].rearrange("p (t e) -> p t e", t=NT)
            dve.wait_ge(s("logit1"), use + 1)
            step(nc.vector.tensor_reduce(rs[:, 0, :], L, AX, ALU.max))
            nc.vector.tensor_tensor(tiles(rt[:, 0]), L, eachtile(rs[:, 0, :]), ALU.subtract).then_inc(s("shift1"), 1)
            dve.wait_ge(s("exp1"), use + 1)
            step(nc.vector.tensor_reduce(rs[:, 1, :], tiles(rt[:, 0]), AX, ALU.add))
            step(nc.vector.reciprocal(rs[:, 2, :], rs[:, 1, :]))
            nc.vector.tensor_tensor(probs.rearrange("p (t b e) -> p b t e", t=TPB, b=BATCH),
                                    tiles(rt[:, 0]).rearrange("p (b t) e -> p b t e", t=TPB),
                                    eachtile(rs[:, 2, :]).rearrange("p (b t) e -> p b t e", t=TPB),
                                    ALU.mult).then_inc(s("prob1"), 1)
            dve.wait_ge(s("probT"), use + 1)
            step(nc.vector.tensor_copy(pT, psum[0:64, 1, 0:SEQ]))
            for k in range(TOPK // 8):
                src = pT if k == 0 else pW[:, (k - 1) % 2]
                step(nc.vector.max(top8[:, :], src))
                step(nc.vector.match_replace(pW[:, k % 2], top8[:, :], src, 0.0))
            step(nc.vector.tensor_tensor(pD, pT, pW[:, (TOPK // 8 - 1) % 2], ALU.subtract))
            step(nc.vector.tensor_copy(gT1[0:64, :], pD))
            step(nc.vector.tensor_tensor(pD, pD, gT1[0:64, :], ALU.subtract))
            nc.vector.tensor_copy(gT1[64:128, :], pD).then_inc(s("gate1"), 1)

        def ffn1_tensor(pe, use, puse):
            if use == 0:
                pe.wait_ge(s("w1_split"), 1)
                pe.wait_ge(s("ld_sel1"), 16)
                pe.wait_ge(s("ld_w2"), 16)
            pe.wait_ge(s("gate1"), use + 1)

            def up(c, e, f, i):
                cs = ds(c * CHUNK, CHUNK)
                pe.wait_ge(s("h1_ready"), nth(i, F1, f))
                ws = slice(f * P, (f + 1) * P)
                matmul3(pe, bank(f), w1h[:, ds(e, 1), ws], w1l[:, ds(e, 1), ws], xTh[:, cs], xTl[:, cs]).then_inc(s("g1_ready"), 1)
                for k in range(BPC):
                    last = nc.tensor.matmul(bank(4 + f)[:, k * SEQ:(k + 1) * SEQ],
                                            sel1[:, ds((c * BPC + k) * E1 + e, 1), :], gT1[:, :], start=True, stop=True)
                last.then_inc(s("w1_ready"), 1)

            def down(e, f, i):
                pe.wait_ge(s("h1_ready"), H0 + nth(i, F1, f))
                for k in range(TPC):
                    last = nc.tensor.matmul(bank(6)[:, k * P:(k + 1) * P], hT[:, f, k * P:(k + 1) * P],
                                            w2[:, ds(e * F1 + f, 1), :], start=False, stop=True, skip_group_check=True)
                last.then_inc(s("down1"), 1)

            with pe.Fori(0, NC) as c:
                base = (use * NC + c) * E1
                up(c, 0, 0, base)
                pe.wait_ge(s("acc1_free"), nth(use * NC + c, 1))
                nc.tensor.matmul(bank(6), zrow[:, 0:P], zrow[:, :], start=True, stop=False, skip_group_check=True)
                with pe.Fori(0, E1 - 1) as e:
                    up(c, e, 1, base + e)
                    down(e, 0, base + e)
                    up(c, e + 1, 0, base + e + 1)
                    down(e, 1, base + e)
                up(c, E1 - 1, 1, base + (E1 - 1))
                down(E1 - 1, 0, base + (E1 - 1))
                down(E1 - 1, 1, base + (E1 - 1))

        def ffn1_scalar(act, use):
            with act.Fori(0, NC * E1) as i:
                for f in range(F1):
                    act.wait_ge(s("g1_ready"), nth(use * NC * E1 + i, F1, f))
                    act.wait_ge(s("h1_ready"), nth(use * NC * E1 + i, F1, f))
                    nc.scalar.activation(sg[:, f, :], bank(f), ACT.Silu, scale=1.0 / WSCALE).then_inc(s("sg1_ready"), 1)

        def ffn1_vector(dve, use):
            with dve.Fori(0, NC) as c:
                with dve.Fori(0, E1) as e:
                    i = (use * NC + c) * E1 + e
                    for f in range(F1):
                        dve.wait_ge(s("sg1_ready"), nth(i, F1, f))
                        dve.wait_ge(s("w1_ready"), nth(i, F1, f))
                        dve.wait_ge(s("down1"), nth(i, F1, f))
                        nc.vector.tensor_tensor(hT[:, f, :], sg[:, f, :], bank(4 + f), ALU.mult).then_inc(s("h1_ready"), 1)
                dve.wait_ge(s("down1"), H0 + nth(use * NC + c, U1, U1 - 1))
                xc = x[:, ds(c * TPC, TPC), :].rearrange("p t c -> p (t c)")
                nc.vector.scalar_tensor_tensor(xc, bank(6), HALF, xc, ALU.mult, ALU.add).then_inc(s("acc1_free"), 1)
            dve.wait_ge(s("acc1_free"), 1 + NC * (use + 1))

        def sample(c, k, q):
            return c * WS + k * SU + q + 1

        def half(c, k, q, jt):
            return (c * WS + k * SU + q) * 2 + jt + 1

        def kernel_groups():
            return [(r * SG + g, g, r) for r in range(2) for g in range(SG)]

        def la_tensor(pe, puse):
            prep_tensor(pe, puse)
            all_xT(pe, puse)
            pe.wait_ge(s("ww_split"), 1)
            for t in range(NT):
                last = matmul3(pe, bank(0)[:, t * 2 * WH:(t + 1) * 2 * WH], xTh[:, t * P:(t + 1) * P],
                               xTl[:, t * P:(t + 1) * P], wwh[:, :], wwl[:, :])
            last.then_inc(s("wave_ready"), 1)
            pe.wait_ge(s("kw_split"), 2)
            with pe.Fori(0, NC // 2) as c2:
                for i, g, r in kernel_groups():
                    cs = ds(c2 * 2 * CHUNK + r * CHUNK, CHUNK)
                    pe.wait_ge(s("sil_ready"), nth(c2, 2 * SG, i))
                    matmul3(pe, bank(6 + i % 2), kwh[:, g].rearrange("p d r -> p (d r)"),
                            kwl[:, g].rearrange("p d r -> p (d r)"), xTh[:, cs], xTl[:, cs]).then_inc(s("kp_ready"), 1)
            pe.wait_ge(s("stag_ready"), 1)
            for c in range(NC):
                for k in range(TPC):
                    last = nc.tensor.transpose(psum[0:POSK, 1 + c, k * P:(k + 1) * P], stag[:, c * TPC + k, :], ident[:, :])
                last.then_inc(s("posT_psum"), 1)
            pe.wait_ge(s("ld_df"), 16)
            pe.wait_ge(s("kwt_ready"), 2 + NC * SG)
            pe.wait_ge(s("ld_selS"), 32)
            pe.wait_ge(s("ld_ow"), 16)
            pe.wait_ge(s("posT"), NC)
            with pe.Fori(0, NC // 2) as c2:
                for r in range(2):
                    c = c2 * 2 + r
                    cs = ds(c2 * 2 * CHUNK + r * CHUNK, CHUNK)

                    def positions(n, g, k, q):
                        for jt in range(2):
                            v = (2 * (r + q) + jt) % UR
                            pe.wait_ge(s("clip_ready"), half(c, k, q, jt))
                            nc.tensor.matmul(bank(v), selS[0:POSK, n, jt, :], posT[0:POSK, cs],
                                             start=True, stop=True).then_inc(s("pos_ready"), 1)
                        pe.wait_ge(s("ws_ready"), sample(c, k, q))
                        nc.tensor.matmul(bank(6), selW[:, q % SU, :], kwt[:, g, cs], start=True,
                                         stop=True).then_inc(s("w_ready"), 1)

                    def samples(k, q):
                        pe.wait_ge(s("prod_ready"), sample(c, k, q))
                        for jt in range(2):
                            v = (2 * (r + q) + jt) % UR
                            pe.wait_ge(s("clip_ready"), UR + half(c, k, q, jt))
                            for b in range(BPC):
                                last = nc.tensor.matmul(bank(4 + (r + q) % 2)[:, b * SEQ:(b + 1) * SEQ], dxs[:, r, b, jt, :],
                                                        uu[:, v, b * SEQ:(b + 1) * SEQ], start=(jt == 0 and b == 0),
                                                        stop=(jt == 1), skip_group_check=True)
                            last.then_inc(s("uu_used"), 1)

                    pe.wait_ge(s("yw_ready"), nth(c, 1))
                    for b in range(BPC):
                        x0 = xn[:, ds((c2 * 2 + r) * TPC + b * TPB, 1), :].rearrange("p o c -> p (o c)")
                        x1 = xn[:, ds((c2 * 2 + r) * TPC + b * TPB + 1, 1), :].rearrange("p o c -> p (o c)")
                        for jt, (m0, m1) in enumerate(((0, 1), (3, 2))):
                            o = bank(7)[:, (b * TPB + jt) * C:(b * TPB + jt + 1) * C]
                            nc.tensor.matmul(o, diffm[:, m0, :], x0, start=True, stop=False)
                            last = nc.tensor.matmul(o, diffm[:, m1, :], x1, start=False, stop=True)
                    last.then_inc(s("dx_psum"), 1)
                    positions(ds(0, 1), ds(0, 1), 0, 0)
                    wait_apart(pe, s("dx_ready"), nth(c, 1))
                    with pe.Fori(0, SG - 1) as k:
                        for q in range(SU):
                            positions(ds(k * SU + q + 1, 1), ds(k, 1) if q < SU - 1 else ds(k + 1, 1), k, q + 1)
                            samples(k, q)
                    samples(SG - 1, 0)
                    pe.wait_ge(s("acc_sum"), 4 + nth(c, WS, WS - 1))
                    for k in range(TPC):
                        last = nc.tensor.matmul(bank(7)[:, k * P:(k + 1) * P], wacc[:, k * P:(k + 1) * P], ow[:, :],
                                                start=True, stop=True)
                    last.then_inc(s("y_psum"), 1)

        def la_scalar(act, puse):
            act.wait_ge(s("ld_kw"), 16)
            for d in range(2):
                nc.scalar.activation(kwh[:, :, d, :], rawkw[:, 0:SG, :], ACT.Copy, scale=WSCALE).then_inc(s("hi_kw"), 1)
            split_act(act, wwh[:, :], wwr[:, :], "ld_ww", 16)
            prep_scalar(act, puse)
            act.wait_ge(s("wz_ready"), 1)
            wzf = wz[:, :, :, :].rearrange("p t a h -> p (t a h)")
            nc.scalar.activation(wzf, wzf, ACT.Silu).then_inc(s("wave_act"), 1)
            act.wait_ge(s("wave_act"), 1)
            nc.scalar.activation(wz[:, :, 1, :], wz[:, :, 1, :], ACT.Tanh).then_inc(s("wave_act"), 1)
            nc.scalar.activation(wz[:, :, 0, :], wz[:, :, 0, :], ACT.Sigmoid).then_inc(s("wave_act"), 1)
            act.preload_act_table(ACT.Silu)
            act.wait_ge(s("ld_kb"), 32)
            with act.Fori(0, NC // 2) as c2:
                for i, g, r in kernel_groups():
                    act.wait_ge(s("kp_ready"), nth(c2, 2 * SG, i))
                    nc.scalar.activation(kwt[:, g, ds(c2 * 2 * CHUNK + r * CHUNK, CHUNK)], bank(6 + i % 2), ACT.Silu,
                                         bias=kb[:, g:g + 1], scale=1.0 / WSCALE)
                    act.wait_ge(s("kwt_ready"), nth(c2, 2 * SG, i))
                    nc.scalar.activation(sil[:, i % 2, :], bank(6 + i % 2), ACT.Silu, bias=kb[:, g:g + 1],
                                         scale=1.0 / WSCALE).then_inc(s("sil_ready"), 1)
            for c in range(NC):
                act.wait_ge(s("posT_psum"), c + 1)
                nc.scalar.activation(posT[0:POSK, c * CHUNK:(c + 1) * CHUNK], psum[0:POSK, 1 + c, :],
                                     ACT.Copy).then_inc(s("posT"), 1)
            with act.Fori(0, NC // 2) as c2:
                for r in range(2):
                    c = c2 * 2 + r
                    act.wait_ge(s("dx_psum"), nth(c, 1))
                    nc.scalar.activation(dxs[:, r].rearrange("p b t c -> p (b t c)"), bank(7), ACT.Copy).then_inc(s("dx_ready"), 1)

                    def copy_weights(k, q):
                        act.wait_ge(s("w_ready"), sample(c, k, q))
                        act.wait_ge(s("prod_ready"), sample(c, k, q))
                        nc.scalar.activation(wsm[:, (r + q) % 2, :], bank(6), ACT.Copy).then_inc(s("ws_ready"), 1)
                    with act.Fori(0, SG - 1) as k:
                        for q in range(SU):
                            copy_weights(k, q)
                    copy_weights(SG - 1, 0)
                    act.wait_ge(s("y_psum"), nth(c, 1))
                    act.wait_ge(s("res_done"), nth(c, 1))
                    nc.scalar.activation(yw, bank(7), ACT.Silu).then_inc(s("yw_ready"), 1)

        def la_vector(dve, puse):
            dve.wait_ge(s("hi_kw"), 2)
            for d in range(2):
                nc.vector.scalar_tensor_tensor(kwl[:, :, d, :], rawkw[:, 0:SG, :], WSCALE, kwh[:, :, d, :],
                                               ALU.mult, ALU.subtract).then_inc(s("kw_split"), 1)
            split_dve(dve, wwl[:, :], wwr[:, :], wwh[:, :], "ld_ww", "ww_split")
            prep_vector(dve, puse)
            n = [0]

            def step(ins):
                n[0] += 1
                ins.then_inc(s("wave_step"), 1)
                dve.wait_ge(s("wave_step"), n[0])
            dve.wait_ge(s("wave_ready"), 1)
            dve.wait_ge(s("ld_wb"), 16)
            wzf = wz[:, :, :, :].rearrange("p t a h -> p t (a h)")
            nc.vector.scalar_tensor_tensor(wzf, bank(0)[:, 0:NT * 2 * WH].rearrange("p (t w) -> p t w", t=NT), 1.0 / WSCALE,
                                           wb[:, :].unsqueeze(1).broadcast_to([P, NT, 2 * WH]),
                                           ALU.mult, ALU.add).then_inc(s("wz_ready"), 1)
            dve.wait_ge(s("wave_act"), 3)
            dve.wait_ge(s("ld_sg"), 32)
            nc.vector.tensor_reduce(wav[:, 0, :], wz[:, :, 0, :], AX, ALU.add)
            step(nc.vector.tensor_reduce(wav[:, 1, :], wz[:, :, 1, :], AX, ALU.add))
            nc.vector.tensor_scalar(wav[:, 2, :], wav[:, 0, :], (MAX_FREQ - MIN_FREQ) / WH, MIN_FREQ, ALU.mult, ALU.add)
            step(nc.vector.scalar_tensor_tensor(wav[:, 3, :], wav[:, 1, :], MAX_FREQ / WH, tokpos[:, :], ALU.mult, ALU.add))
            step(nc.vector.tensor_tensor(pos[:, :, :], sgrid[:, :].unsqueeze(1).broadcast_to([P, NT, WS]),
                                         wav[:, 2, :].unsqueeze(2).broadcast_to([P, NT, WS]), ALU.mult))
            step(nc.vector.tensor_tensor(pos[:, :, :], pos[:, :, :], wav[:, 3, :].unsqueeze(2).broadcast_to([P, NT, WS]), ALU.add))
            step(nc.vector.tensor_scalar(pos[:, :, :], pos[:, :, :], 0.0, SEQ - 1.0, ALU.max, ALU.min))
            step(nc.vector.tensor_copy(pos16[:, :, :], pos[:, :, :]))
            nc.vector.tensor_copy(stag[:, :, 0:WS], pos16[:, :, :])
            step(nc.vector.tensor_tensor(posr[:, :, :], pos[:, :, :], pos16[:, :, :], ALU.subtract))
            step(nc.vector.tensor_copy(pos16[:, :, :], posr[:, :, :]))
            nc.vector.tensor_copy(stag[:, :, WS:2 * WS], pos16[:, :, :])
            nc.vector.tensor_tensor(stag[:, :, 2 * WS:3 * WS], posr[:, :, :], pos16[:, :, :], ALU.subtract)
            nc.vector.memset(stag[:, :, 3 * WS:POSK], 1.0).then_inc(s("stag_ready"), 1)

            with dve.Fori(0, NC // 2) as c2:
                for r in range(2):
                    c = c2 * 2 + r
                    def clips(k, q):
                        for jt in range(2):
                            v = (2 * (r + q) + jt) % UR
                            dve.wait_ge(s("pos_ready"), half(c, k, q, jt))
                            dve.wait_ge(s("uu_used"), half(c, k, q, jt))
                            nc.vector.tensor_scalar(uu[:, v, :], bank(v), 0.0, 1.0, ALU.max, ALU.min).then_inc(s("clip_ready"), 1)

                    def weigh(k, q):
                        dve.wait_ge(s("uu_used"), UR + half(c, k, q, 1))
                        dve.wait_ge(s("ws_ready"), 1 + sample(c, k, q))
                        dve.wait_ge(s("acc_sum"), sample(c, k, q))
                        nc.vector.tensor_tensor(prod[:, (r + q) % 4, :], wsm[:, (r + q) % 2, :], bank(4 + (r + q) % 2),
                                                ALU.mult).then_inc(s("prod_ready"), 1)
                    clips(0, 0)
                    with dve.Fori(0, SG - 1) as k:
                        for q in range(SU):
                            clips(k, q + 1)
                            weigh(k, q)
                    weigh(SG - 1, 0)
                    dve.wait_ge(s("yw_ready"), 1 + nth(c, 1))
                    xc = x[:, ds(c * TPC, TPC), :].rearrange("p t c -> p (t c)")
                    nc.vector.tensor_tensor(xc, xc, yw, ALU.add).then_inc(s("res_done"), 1)
            dve.wait_ge(s("res_done"), 1 + NC)

        def la_gpsimd(pool, puse):
            prep_gpsimd(pool, puse)
            with pool.Fori(0, NC // 2) as c2:
                for i, g, r in kernel_groups():
                    pool.wait_ge(s("sil_ready"), 2 + nth(c2, 2 * SG, i))
                    lo = kwt[P // 2:P, g, ds(c2 * 2 * CHUNK + r * CHUNK, CHUNK)]
                    nc.gpsimd.tensor_tensor(lo, sil[P // 2:P, i % 2, :], lo, ALU.subtract).then_inc(s("kwt_ready"), 1)
            pool.wait_ge(s("kwt_ready"), 2 + NC * SG)
            with pool.Fori(0, NC // 2) as c2:
                for r in range(2):
                    c = c2 * 2 + r
                    wait_apart(pool, s("yw_ready"), nth(c, 1))
                    nc.gpsimd.memset(wacc, 0.0).then_inc(s("wacc0"), 1)
                    wait_apart(pool, s("wacc0"), nth(c, 1))

                    def add(k, q):
                        pool.wait_ge(s("prod_ready"), 2 + sample(c, k, q))
                        pool.wait_ge(s("acc_sum"), 3 + sample(c, k, q))
                        nc.gpsimd.tensor_tensor(wacc, wacc, prod[:, (r + q) % 4, :], ALU.add).then_inc(s("acc_sum"), 1)
                    with pool.Fori(0, SG - 1) as k:
                        for q in range(SU):
                            add(k, q)
                    add(SG - 1, 0)

        def split_act(act, dst, src, wait, n):
            act.wait_ge(s(wait), n)
            nc.scalar.activation(dst, src, ACT.Copy, scale=WSCALE).then_inc(s("hi_" + wait), 1)

        def split_dve(dve, dst, src, hi, wait, done):
            dve.wait_ge(s("hi_" + wait), 1)
            nc.vector.scalar_tensor_tensor(dst, src, WSCALE, hi, ALU.mult, ALU.subtract).then_inc(s(done), 1)

        def flat(v):
            return v.rearrange("p a b -> p (a b)")

        @block.gpsimd
        def _(pool):
            pool.sem_inc(s("acc_sum"), 4)
            pool.sem_inc(s("kwt_ready"), 2)
            nc.gpsimd.memset(neghalf[:, :], -0.5)
            nc.gpsimd.memset(zrow[:, :], 0.0).then_inc(s("consts"), 1)
            nc.gpsimd.memset(gst[:, :, :], 0.0).then_inc(s("gst0"), 1)
            pool.wait_ge(s("gst0"), 1)
            nc.gpsimd.memset(gst[:, :, E0:U0], 1.0).then_inc(s("consts"), 1)
            nc.gpsimd.iota(revidx[:, :], pattern=[[-1, E0]], base=E0, channel_multiplier=0,
                           allow_small_or_imprecise_dtypes=True).then_inc(s("consts"), 1)
            pool.wait_ge(s("consts"), 3)
            for pu, st in enumerate(stage_order):
                if st == "AT":
                    at_gpsimd(pool, pu)
                elif st == "LA":
                    la_gpsimd(pool, pu)
                else:
                    prep_gpsimd(pool, pu)

        @block.scalar
        def _(act):
            act.sem_inc(s("vb_ready"), 1)
            act.sem_inc(s("qkT_ready"), 1)
            act.sem_inc(s("qn_ready"), 2)
            act.sem_inc(s("exp_ready"), 2)
            act.sem_inc(s("ws_ready"), 1)
            act.sem_inc(s("sil_ready"), 2)
            act.sem_inc(s("yw_ready"), 1)
            split_act(act, rwh[:, :], rwr[:, :], "ld_rw", 16)
            split_act(act, flat(guh[:, :, :]), flat(rawgu), "ld_gu", 48)
            uses = {}
            for pu, st in enumerate(stage_order):
                use = uses.get(st, 0)
                uses[st] = use + 1
                if st == "AT":
                    at_scalar(act, pu)
                    continue
                if st == "LA":
                    la_scalar(act, pu)
                    continue
                if st == "F1" and use == 0:
                    split_act(act, cwh[:, :], cwr[:, :], "ld_cw", 16)
                    split_act(act, flat(w1h[:, :, :]), flat(raww1), "ld_w1", 16)
                prep_scalar(act, pu)
                if st == "F1":
                    route1_scalar(act, use)
                    ffn1_scalar(act, use)
                if st == "F0":
                    route0_scalar(act, use)
                    act.preload_act_table(ACT.Silu)
                    ffn0_scalar(act, use)

        @block.vector
        def _(dve):
            dve.sem_inc(s("xT_ready"), XT0)
            dve.sem_inc(s("hT_ready"), H0)
            dve.sem_inc(s("su_ready"), H0)
            dve.sem_inc(s("acc_free"), 1)
            dve.sem_inc(s("ss_ready"), 2)
            dve.sem_inc(s("rot_ready"), R0)
            dve.sem_inc(s("pv_taken"), 2)
            dve.sem_inc(s("h1_ready"), H0)
            dve.sem_inc(s("acc1_free"), 1)
            dve.sem_inc(s("clip_ready"), UR)
            dve.sem_inc(s("prod_ready"), 2)
            dve.sem_inc(s("res_done"), 1)
            split_dve(dve, rwl[:, :], rwr[:, :], rwh[:, :], "ld_rw", "rw_split")
            dve.wait_ge(s("ld_x"), 16)
            dve.wait_ge(s("consts"), 3)
            uses = {}
            for pu, st in enumerate(stage_order):
                use = uses.get(st, 0)
                uses[st] = use + 1
                if st == "AT":
                    at_vector(dve, pu)
                    continue
                if st == "LA":
                    la_vector(dve, pu)
                    continue
                if st == "F1" and use == 0:
                    split_dve(dve, cwl[:, :], cwr[:, :], cwh[:, :], "ld_cw", "cw_split")
                    split_dve(dve, flat(w1l[:, :, :]), flat(raww1), flat(w1h[:, :, :]), "ld_w1", "w1_split")
                prep_vector(dve, pu)
                if st == "F1":
                    route1_vector(dve, use)
                    ffn1_vector(dve, use)
                if st == "F0":
                    route0_vector(dve, use)
                    if use == 0:
                        split_dve(dve, flat(gul[:, :, :]), flat(rawgu), flat(guh[:, :, :]), "ld_gu", "gu_split")
                    ffn0_vector(dve, use)
            dve.sem_inc(s("x_final"), 1)

        @block.tensor
        def _(pe):
            pe.wait_ge(s("ld_ident"), 16)
            pe.sem_inc(s("down_done"), H0)
            pe.sem_inc(s("down1"), H0)
            pe.sem_inc(s("tr_ready"), 4)
            pe.sem_inc(s("pv_ready"), HG)
            pe.sem_inc(s("uu_used"), UR)
            pe.wait_ge(s("consts"), 3)
            uses = {}
            for pu, st in enumerate(stage_order):
                use = uses.get(st, 0)
                uses[st] = use + 1
                if st == "AT":
                    at_tensor(pe, pu)
                    continue
                if st == "LA":
                    la_tensor(pe, pu)
                    continue
                prep_tensor(pe, pu)
                if st == "F1":
                    route1_tensor(pe, use, pu)
                    ffn1_tensor(pe, use, pu)
                if st == "F0":
                    route0_tensor(pe, use, pu)
                    ffn0_tensor(pe, use, pu)


def _constants():
    ident = np.eye(P, dtype=np.float32)
    sel0 = np.zeros((64, U0, P), np.float16)
    for u in range(U0):
        sel0[u, u] = 1
        sel0[32 + u, u] = 1
    sel1 = np.zeros((P, BATCH * E1, P), np.float16)
    for i in range(BATCH * E1):
        sel1[i, i] = 1
        sel1[64 + i, i] = 1
    j = np.arange(HD // 2, dtype=np.float32)
    freqs = np.power(np.float32(ROPE_BASE), -j / np.float32(HD // 2)).astype(np.float32)
    rad = (np.arange(SEQ, dtype=np.float32)[:, None] * freqs[None, :]).astype(np.float32).astype(np.float64)
    cos, sin = np.cos(rad).astype(np.float32), np.sin(rad).astype(np.float32)
    cosd = np.concatenate([cos, cos], 1).reshape(TPB, P, HD).transpose(1, 0, 2).copy()
    sind = np.concatenate([-sin, sin], 1).reshape(TPB, P, HD).transpose(1, 0, 2).copy()
    selS = np.zeros((POSK, WS, 2, P), np.float32)
    for t in range(WS):
        selS[[p * WS + t for p in range(PIECES)], t] = 1
    selS[POSK - 1] = -np.arange(SEQ, dtype=np.float32).reshape(2, P)
    selS[POSK - 1, :, 1, P - 1] = 1
    d = np.zeros((P, 4, P), np.float32)
    for k in range(P):
        d[k, 0, k] = -1
        if k:
            d[k, 0, k - 1] = 1
            d[k, 2, k - 1] = 1
        if k < P - 1:
            d[k, 2, k] = -1
    d[0, 1, P - 1] = 1
    d[0, 3, P - 1] = 1
    selW = np.zeros((2, SU, WH, SU, WH, WD), np.float16)
    for t in range(SU):
        for h in range(WH):
            selW[:, t, h, t, h, :] = 1
    sgrid = np.tile(np.arange(WS, dtype=np.float32) - (WS // 2), (P, 1))
    tokpos = np.zeros((P, NT), np.float32)
    for t in range(NT):
        tokpos[:, t] = np.arange(P) + (t % TPB) * P
    return {"ident": ident, "sel0": sel0, "sel1": sel1, "cosd": cosd, "sind": sind,
            "selS": selS.astype(np.float16), "diffm": d, "selW": selW.reshape(P, SU, P), "sgrid": sgrid, "tokpos": tokpos}


_TRANSPOSED = {"L0_ffn_router_w": (1, 0), "L0_ffn_shared_gate_w": (1, 0), "L0_ffn_shared_up_w": (1, 0),
               "L0_ffn_shared_down_w": (1, 0), "L0_attn_wv": (2, 1, 0), "L1_attn_wave_w": (1, 0),
               "L1_attn_kernel_w": (3, 1, 2, 0), "L1_attn_kernel_b": (2, 0, 1),
               "L1_attn_out_w": (1, 0), "L1_ffn_choice_w": (1, 0)}
_SHAPED = {"L1_attn_kernel_w": (WH, WK // SU, SU, C), "L1_attn_kernel_b": (WH, WK // SU, SU)}
_MERGED = {"L1_attn_kernel_w": (C, WK // SU, SU * WH), "L1_attn_kernel_b": (SU * WH, WK // SU)}
_STAGES = ["F0", "AT", "F0", "F1", "LA", "F1"]


def _laid_out(name, v):
    v = v.reshape(_SHAPED.get(name, v.shape))
    v = v.transpose(_TRANSPOSED.get(name, range(v.ndim)))
    return np.ascontiguousarray(v.reshape(_MERGED.get(name, v.shape)))


def kernel(**inputs):
    import concourse.bacc as _bacc
    from concourse.bass_utils import run_bass_kernel_spmd as _run

    nc = _bacc.Bacc("TRN2", target_bir_lowering=False, num_devices=1)
    host = dict(_constants())
    for name, v in inputs.items():
        v = np.asarray(v)
        host[name] = _laid_out(name, v)
    arrays, aps = {}, {"_stages": _STAGES}
    for name, v in host.items():
        arrays[f"in_{name}"] = v
        aps[name] = nc.dram_tensor(f"in_{name}", v.shape, mybir.dt.from_np(v.dtype), kind="ExternalInput").ap()
    out = nc.dram_tensor("out_x", (BATCH, SEQ, C), F32, kind="ExternalOutput").ap()
    macaron_kernel(nc, aps, out)
    r = _run(nc, [arrays], core_ids=[0])
    return r.results[0]["out_x"]
```

```python
import numpy as np
import concourse.bass as bass
from concourse import mybir
from contextlib import ExitStack

F32 = mybir.dt.float32
F16 = mybir.dt.float16
BF16 = mybir.dt.bfloat16
ALU = mybir.AluOpType
ACT = mybir.ActivationFunctionType
AX = mybir.AxisListType.X
ds = bass.ds

BATCH, SEQ, C = 8, 256, 128
P = 128
NT = BATCH * SEQ // P
TPB = SEQ // P
CHUNK = 512
NC = BATCH * SEQ // CHUNK
TPC = CHUNK // P
BPC = CHUNK // SEQ
LN_EPS = 1e-5
HALF = 0.5
E0, HID = 16, 128
U0 = E0 + 2
NH, HD = 8, 128
HG = 4
NG = NH // HG
RMS_EPS = 1e-6
ROPE_BASE = 1250
E1, FF = 8, 256
F1 = FF // P
U1 = E1 * F1
TOPK = SEQ * 2 // E1
WH, WK, WS = 8, 64, 33
WD = C // WH
MAX_FREQ, MIN_FREQ = 16.0, 1.0
SU = P // (2 * WH)
SG = -(-WS // SU)
UR = 4
PIECES = 3
POSK = PIECES * WS + 1
WSCALE = 64.0


def macaron_kernel(nc, a, out):
    ctx = ExitStack()
    with ctx:
        def sb(name, shape, dt=F32):
            return ctx.enter_context(nc.sbuf_tensor(name, shape, dt))

        def sem(name):
            return ctx.enter_context(nc.semaphore(name))

        psum = ctx.enter_context(nc.psum_tensor("psum", [P, 8, CHUNK], F32))

        def bank(i):
            return psum[:, i, :]

        x = sb("x", [P, NT, C])
        xn = sb("xn", [P, NT, C])
        xTh = sb("xTh", [P, NT * P], F16)
        xTl = sb("xTl", [P, NT * P], F16)
        ident = sb("ident", [P, P])
        neghalf = sb("neghalf", [P, NT])
        stats = sb("stats", [P, NT, 6])
        mv = sb("mv", [P, NT, 2])
        rstd = sb("rstd", [P, NT])
        rvar = sb("rvar", [P, NT])

        guh = sb("guh", [P, U0, 2 * HID], F16)
        gul = sb("gul", [P, U0, 2 * HID], F16)
        wd16 = sb("wd16", [P, 2, U0, C], F16)
        rwh = sb("rwh", [P, E0], F16)
        rwl = sb("rwl", [P, E0], F16)
        rwr = sb("rwr", [P, E0])
        sel0 = sb("sel0", [64, U0, P], F16)
        gT0 = sb("gT0", [64, NT * P], F16)
        w1h = sb("w1h", [P, E1, FF], F16)
        w1l = sb("w1l", [P, E1, FF], F16)
        w216 = sb("w216", [P, 2, U1, C], F16)
        cwh = sb("cwh", [P, E1], F16)
        cwl = sb("cwl", [P, E1], F16)
        cwr = sb("cwr", [P, E1])
        sel1 = sb("sel1", [P, BATCH * E1, P], F16)
        gT1 = sb("gT1", [P, SEQ], F16)
        qkh = sb("qkh", [P, 2, NH * HD], F16)
        qkl = sb("qkl", [P, 2, NH * HD], F16)
        voh = sb("voh", [P, NH * C], F16)
        vol = sb("vol", [P, NH * C], F16)
        rawqk = sb("rawqk", [P, 2, NH * HD])
        rawvo = sb("rawvo", [P, 2, NH * HD])
        raww1 = rawqk[:, :, :].rearrange("p a (e f) -> p (a e) f", f=FF)
        work = sb("work", [P, 6, CHUNK])
        sg, su, hT = work[:, 0:2, :], work[:, 2:4, :], work[:, 4:6, :]
        zrow = sb("zrow", [1, CHUNK], F16)
        rt = sb("rt", [P, 6, NT, E0])
        rs = sb("rs", [P, 6, NT])
        g16 = sb("g16", [P, NT, E0], F16)
        hh = rt[:, 0:2].rearrange("p a t e -> p (a t e)").bitcast(F16).rearrange("p (r c) -> p r c", r=2)
        hl = rt[:, 2:4].rearrange("p a t e -> p (a t e)").bitcast(F16).rearrange("p (r c) -> p r c", r=2)
        outT = rt[:, 4:6].rearrange("p a t e -> p (a t e)")
        revidx = sb("revidx", [P, E0])
        gst = sb("gst", [P, NT, 64])
        ARENA = 12032
        arena = sb("arena", [P, ARENA])
        off = [0]

        def part(n):
            off[0] += n
            assert off[0] <= ARENA, off[0]
            return arena[:, off[0] - n:off[0]]

        rawgu = part(U0 * 2 * HID).rearrange("p (u h) -> p u h", u=U0)
        rawdn = part(U0 * C).rearrange("p (u c) -> p u c", u=U0)
        off[0] = 0
        sq, rpA = sg, hT
        rpB = part(2 * CHUNK).rearrange("p (r c) -> p r c", r=2)
        qr = part(4 * CHUNK).rearrange("p (r c) -> p r c", r=4)
        qT = part(2 * HG * SEQ).rearrange("p (g h t) -> p g h t", g=2, h=HG)
        kT = part(2 * HG * SEQ).rearrange("p (g h t) -> p g h t", g=2, h=HG)
        VW = C + 1
        vb = part(2 * TPB * HG * VW).rearrange("p (g t h c) -> p g t h c", g=2, t=TPB, h=HG)
        pt = part(HG * 3 * P).rearrange("p (r c) -> p r c", r=HG)
        qn = sel1[:, :, :].rearrange("p a b -> p (a b)").bitcast(F32).rearrange("p (g u c) -> p g u c", g=2, u=4)
        cosd = part(TPB * HD).rearrange("p (t c) -> p t c", t=TPB)
        sind = part(TPB * HD).rearrange("p (t c) -> p t c", t=TPB)
        ss = sb("ss", [P, 4, HG])
        rms = sb("rms", [P, 4, HG])
        rq = sb("rq", [P, BATCH * NG, 4 * HG])
        rl = sb("rl", [P, 2, TPB])
        off[0] = 0
        selS = part(WS * 2 * P // 2).bitcast(F16).rearrange("p (s j l) -> p s j l", s=WS, j=2)
        kwt = part(SG * NT * P // 2).bitcast(F16).rearrange("p (g t) -> p g t", g=SG)
        selW = part(SU * P // 2).bitcast(F16).rearrange("p (s c) -> p s c", s=SU)
        uu = part(UR * CHUNK).rearrange("p (r c) -> p r c", r=UR)
        raww2 = uu.rearrange("p r (u c) -> p (r u) c", c=C)
        wsm, prod = work[:, 0:2, :], work[:, 2:6, :]
        sil = work[:, 0:2, :]
        wacc = rt[:, 0:2].rearrange("p a t e -> p (a t e)")
        yw = rt[:, 2:4].rearrange("p a t e -> p (a t e)")
        rawkw = sb("rawkw", [P, WK // SU, SU * WH])
        kb = sb("kb", [P, WK // SU])
        wwh = sb("wwh", [P, 2 * WH], F16)
        wwl = sb("wwl", [P, 2 * WH], F16)
        wwr = sb("wwr", [P, 2 * WH])
        wb = sb("wb", [P, 2 * WH])
        ow = sb("ow", [P, C])
        sgrid = sb("sgrid", [P, WS])
        tokpos = sb("tokpos", [P, NT])
        diffm = sb("diffm", [P, 4, P])
        wdnf = wd16[:, :, :, :].rearrange("p a u c -> p (a u c)").bitcast(F32)
        posT = wdnf[:, 0:NT * P // 2].bitcast(BF16)
        dxs = wdnf[:, NT * P // 2:NT * P // 2 + 2 * BPC * TPB * C].rearrange("p (r b t c) -> p r b t c", r=2, b=BPC, t=TPB)
        guf = guh[:, :, :].rearrange("p a b -> p (a b)")
        kwh = guf[:, 0:SG * P].rearrange("p (g d r) -> p g d r", g=SG, d=2)
        kwl = guf[:, SG * P:2 * SG * P].rearrange("p (g d r) -> p g d r", g=SG, d=2)
        pos = sb("pos", [P, NT, WS])
        xnc = pos[:, :, :].rearrange("p t k -> p (t k)")[:, 0:CHUNK].rearrange("p (t c) -> p t c", t=TPC)
        posr = sb("posr", [P, NT, WS])
        pos16 = sb("pos16", [P, NT, WS], BF16)
        stag = gul[:, :, :].rearrange("p a b -> p (a b)")[:, 0:2 * NT * POSK].bitcast(F32).rearrange("p (t k) -> p t k", t=NT)
        wz = sb("wz", [P, NT, 2, WH])
        wav = sb("wav", [P, 4, NT])
        pT = work[0:64, 0, 0:SEQ]
        pW = work[0:64, 1:3, 0:SEQ]
        pD = work[0:64, 3, 0:SEQ]
        top8 = sb("top8", [64, 8])

        S = {}

        def s(name):
            if name not in S:
                S[name] = sem(name)
            return S[name]

        block = ctx.enter_context(nc.Block())
        stage_order = a["_stages"]

        def nth(i, per, j=0):
            return i * per + j + 1

        def wait_apart(eng, sem_, value):
            eng.wait_ge(sem_, value)
            eng.sem_inc(s("waited"), 1)

        def matmul3(pe, o, lh, ll, rh, rl_, last=None):
            nc.tensor.matmul(o, ll, rh, start=True, stop=False)
            nc.tensor.matmul(o, lh, rl_, start=False, stop=False)
            return nc.tensor.matmul(o, lh, rh, start=False, stop=True)

        @block.sync
        def _(sp):
            def ld(dst, src, name):
                sp.dma_start(dst, src).then_inc(s(name), 16)
            xv = a["L0_attn_x"].rearrange("b (t p) c -> p (b t) c", p=P)
            ld(x[:, :, :], xv, "ld_x")
            ld(ident[:, :], a["ident"], "ld_ident")
            ld(rwr[:, :], a["L0_ffn_router_w"], "ld_rw")
            ld(rawgu[:, 0:E0, :], a["L0_ffn_gate_up_w"].rearrange("e c h -> c e h"), "ld_gu")
            ld(rawgu[:, E0:U0, 0:HID], a["L0_ffn_shared_gate_w"].rearrange("c (u h) -> c u h", u=2), "ld_gu")
            ld(rawgu[:, E0:U0, HID:], a["L0_ffn_shared_up_w"].rearrange("c (u h) -> c u h", u=2), "ld_gu")
            ld(sel0[:, :, :], a["sel0"], "ld_sel0")
            ld(rawdn[:, 0:E0, :], a["L0_ffn_down_w"].rearrange("e h c -> h e c"), "ld_dn")
            ld(rawdn[:, E0:U0, :], a["L0_ffn_shared_down_w"].rearrange("(u h) c -> h u c", h=P), "ld_dn")
            ld(rawqk[:, 0, :], a["L0_attn_wq"].rearrange("m h d -> m (h d)"), "ld_qk")
            ld(rawqk[:, 1, :], a["L0_attn_wk"].rearrange("m h d -> m (h d)"), "ld_qk")
            ld(rawvo[:, 0, :], a["L0_attn_wv"].rearrange("d h m -> d (h m)"), "ld_vo")
            ld(rawvo[:, 1, :].rearrange("d (h m) -> d h m", h=NH), a["L0_attn_wo"].rearrange("h d m -> d h m"), "ld_vo")
            ld(cwr[:, :], a["L1_ffn_choice_w"], "ld_cw")
            ld(rawkw[:, :, :], a["L1_attn_kernel_w"], "ld_kw")
            ld(wwr[:, :], a["L1_attn_wave_w"], "ld_ww")
            ld(wb[:, :], a["L1_attn_wave_b"].rearrange("(o w) -> o w", o=1).broadcast_to([P, 2 * WH]), "ld_wb")
            ld(ow[:, :], a["L1_attn_out_w"], "ld_ow")
            ld(sgrid[:, :], a["sgrid"], "ld_sg")
            ld(tokpos[:, :], a["tokpos"], "ld_sg")
            ld(diffm[:, :, :], a["diffm"], "ld_df")
            for d in range(2):
                ld(kb[d * P // 2:(d + 1) * P // 2, :], a["L1_attn_kernel_b"], "ld_kb")
            if "AT" in stage_order:
                sp.wait_ge(s("gu_split"), 1)
                sp.wait_ge(s("dn_split"), 1)
                ld(cosd[:, :, :], a["cosd"], "ld_cos")
                ld(sind[:, :, :], a["sind"], "ld_cos")
            if "F1" in stage_order:
                if "AT" in stage_order:
                    sp.wait_ge(s("qk_split"), NC)
                else:
                    sp.wait_ge(s("ld_qk"), 32)
                ld(raww1, a["L1_ffn_w1"].rearrange("e d f -> d e f"), "ld_w1")
            if "AT" in stage_order:
                sp.wait_ge(s("at_done"), 1)
            if "F1" in stage_order:
                ld(sel1[:, :, :], a["sel1"], "ld_sel1")
                ld(raww2, a["L1_ffn_w2"].rearrange("e (f p) d -> p (e f) d", p=P), "ld_w2")
            if "LA" in stage_order:
                ld(selS[0:POSK, :, :, :], a["selS"], "ld_selS")
                ld(selW, a["selW"], "ld_selS")
            sp.wait_ge(s("x_final"), 1)
            sp.dma_start(out.rearrange("b (t p) c -> p (b t) c", p=P), x[:, :, :]).then_inc(s("stored"), 16)
            sp.wait_ge(s("stored"), 16)

        def chunks_left(puse):
            before = stage_order[puse - 1] if puse else None
            return [(puse * NC + c, c) for c in ([NC - 1] if before in ("F0", "F1") else range(NC))]

        def tile(v, c, k):
            return v[:, ds(c * TPC + k, 1), :].rearrange("p o c -> p (o c)")

        def slots(c):
            c = c if isinstance(c, int) else 0
            return range(c * TPC, (c + 1) * TPC)

        def statistics(dve, i, c):
            for k, t in enumerate(slots(c)):
                nc.vector.bn_stats(stats[:, t:t + 1, :], x[:, ds(c * TPC + k, 1), :]).then_inc(s("stats"), 1)

        def moments(dve, i, c):
            wait_apart(dve, s("stats"), nth(i, TPC, TPC - 1))
            for t in slots(c):
                last = nc.vector.bn_aggr(mv[:, t, :], stats[:, t, :])
            last.then_inc(s("moments"), 1)

        def normalise(dve, i, c, dsts):
            dve.wait_ge(s("rstd"), nth(i, 1))
            for dst in dsts:
                for k, t in enumerate(slots(c)):
                    last = nc.vector.tensor_scalar(dst(k), tile(x, c, k), mv[:, t, 0:1], rstd[:, t:t + 1],
                                                   ALU.subtract, ALU.mult)
            last.then_inc(s("xn_ready"), 1)

        def low(dve, i, c, b):
            dve.wait_ge(s("xh_ready"), nth(i, 1))
            cs = ds(c * CHUNK, CHUNK)
            nc.vector.tensor_tensor(xTl[:, cs], bank(b), xTh[:, cs], ALU.subtract).then_inc(s("xT_ready"), 1)

        def inverse_deviation(pool, i, c):
            ts = slice(slots(c)[0], slots(c)[-1] + 1)
            wait_apart(pool, s("moments"), nth(i, 1))
            nc.gpsimd.tensor_scalar(rvar[:, ts], mv[:, ts, 1], LN_EPS, None, ALU.add).then_inc(s("rvar"), 1)
            pool.wait_ge(s("rvar"), nth(i, 1))
            nc.gpsimd.tensor_tensor(rstd[:, ts], rvar[:, ts], neghalf[:, 0:TPC], ALU.pow).then_inc(s("rstd"), 1)

        def turn_rows(pe, i, b, src, busy):
            pe.wait_ge(s("xn_ready"), nth(i, 1))
            pe.wait_ge(s("xT_ready"), XT0 + i - busy)
            for k in range(TPC):
                last = nc.tensor.transpose(bank(b)[:, k * P:(k + 1) * P], src(k), ident[:, :])
            last.then_inc(s("tp_ready"), 1)

        def high(act, i, c, b):
            act.wait_ge(s("tp_ready"), nth(i, 1))
            nc.scalar.activation(xTh[:, ds(c * CHUNK, CHUNK)], bank(b), ACT.Copy).then_inc(s("xh_ready"), 1)

        def prep_vector(dve, puse):
            left = chunks_left(puse)
            n = len(left)
            statistics(dve, *left[0])
            for m in range(n + 3):
                if m + 1 < n:
                    statistics(dve, *left[m + 1])
                if m < n:
                    moments(dve, *left[m])
                if 0 <= m - 1 < n:
                    i, c = left[m - 1]
                    normalise(dve, i, c, [lambda k: xn[:, c * TPC + k, :]])
                if 0 <= m - 3 < n:
                    low(dve, *left[m - 3], 6 + left[m - 3][1] % 2)

        def prep_gpsimd(pool, puse):
            for i, c in chunks_left(puse):
                inverse_deviation(pool, i, c)

        def prep_tensor(pe, puse):
            for i, c in chunks_left(puse):
                turn_rows(pe, i, 6 + c % 2, lambda k: xn[:, c * TPC + k, :], 1)

        def prep_scalar(act, puse):
            for i, c in chunks_left(puse):
                high(act, i, c, 6 + c % 2)

        XT0 = 2

        def all_xT(eng, use):
            eng.wait_ge(s("xT_ready"), XT0 + NC * (use + 1))

        def route0_tensor(pe, use, puse):
            all_xT(pe, puse)
            if use == 0:
                pe.wait_ge(s("rw_split"), 1)
            for t in range(NT):
                last = matmul3(pe, bank(0)[:, t * E0:(t + 1) * E0], xTh[:, t * P:(t + 1) * P],
                               xTl[:, t * P:(t + 1) * P], rwh[:, :], rwl[:, :])
            last.then_inc(s("logit0"), 1)
            pe.wait_ge(s("gate0"), use + 1)
            for c in range(NC):
                for k in range(TPC):
                    last = nc.tensor.transpose(psum[0:64, 1 + c, k * P:(k + 1) * P], gst[:, c * TPC + k, :], ident[:, :])
                last.then_inc(s("gT0_psum"), 1)

        def route0_scalar(act, use):
            act.wait_ge(s("top2"), use + 1)
            nc.scalar.activation(rs[:, 4:6, :], rs[:, 2:4, :], ACT.Sigmoid, scale=1.0 / WSCALE).then_inc(s("sig2"), 1)
            for c in range(NC):
                act.wait_ge(s("gT0_psum"), nth(use, NC, c))
                nc.scalar.activation(gT0[:, c * CHUNK:(c + 1) * CHUNK], psum[0:64, 1 + c, :],
                                     ACT.Copy).then_inc(s("gT0"), 1)

        def route0_vector(dve, use):
            n = [0]

            def step(ins):
                n[0] += 1
                ins.then_inc(s("route0_step"), 1)
                dve.wait_ge(s("route0_step"), ROUTE0_STEPS * use + n[0])

            def eachtile(v):
                return v.unsqueeze(2).broadcast_to([P, NT, E0])
            L = rt[:, 0]
            dve.wait_ge(s("logit0"), use + 1)
            step(nc.vector.tensor_copy(L, bank(0)[:, 0:NT * E0].rearrange("p (t e) -> p t e", t=NT)))
            for r in range(2):
                m = rs[:, 2 + r, :]
                k = rs[:, r, :]
                key, one = rt[:, 1], rt[:, 2 + r]
                step(nc.vector.tensor_reduce(m, L, AX, ALU.max))
                step(nc.vector.tensor_tensor(key, L, eachtile(m), ALU.is_equal))
                step(nc.vector.tensor_tensor(key, key, revidx[:, :].unsqueeze(1).broadcast_to([P, NT, E0]), ALU.mult))
                step(nc.vector.tensor_reduce(k, key, AX, ALU.max))
                step(nc.vector.tensor_tensor(one, key, eachtile(k), ALU.is_equal))
                if r == 0:
                    step(nc.vector.scalar_tensor_tensor(L, one, -1e30, L, ALU.mult, ALU.add))
            nc.vector.tensor_copy(rs[:, 0, 0:1], rs[:, 2, 0:1]).then_inc(s("top2"), 1)
            dve.wait_ge(s("sig2"), use + 1)
            step(nc.vector.tensor_tensor(rt[:, 4], rt[:, 2], eachtile(rs[:, 4, :]), ALU.mult))
            step(nc.vector.tensor_tensor(rt[:, 5], rt[:, 3], eachtile(rs[:, 5, :]), ALU.mult))
            step(nc.vector.tensor_tensor(rt[:, 1], rt[:, 4], rt[:, 5], ALU.add))
            step(nc.vector.tensor_copy(g16[:, :, :], rt[:, 1]))
            step(nc.vector.tensor_copy(gst[:, :, 0:E0], g16[:, :, :]))
            nc.vector.tensor_tensor(gst[:, :, 32:32 + E0], rt[:, 1], g16[:, :, :],
                                    ALU.subtract).then_inc(s("gate0"), 1)

        ROUTE0_STEPS = 1 + 6 + 5 + 5

        H0 = 2
        LAG0, LAG1 = 2, 3
        PREP_AT = 3

        def by_chunk(eng, emit):
            emit(0, True)
            with eng.Fori(1, NC) as c:
                emit(c, False)
            emit(None, False)

        def experts_tensor(pe, n, use, puse, units, lag, up, down_w):
            def down(u, r, i):
                pe.wait_ge(s(n + "_hl"), H0 + nth(i, 2, r))
                nc.tensor.matmul(bank(6), down_w[:, 0, u, :], hl[:, r, :], start=False, stop=True, skip_group_check=True)
                nc.tensor.matmul(bank(6), down_w[:, 1, u, :], hh[:, r, :], start=False, stop=True, skip_group_check=True)
                nc.tensor.matmul(bank(6), down_w[:, 0, u, :], hh[:, r, :], start=False, stop=True,
                                 skip_group_check=True).then_inc(s(n + "_down"), 1)

            def turn_result(count):
                pe.wait_ge(s(n + "_out"), 1 + count)
                pe.wait_ge(s(n + "_added"), count)
                for k in range(TPC):
                    last = nc.tensor.transpose(bank(7)[:, k * P:(k + 1) * P], outT[:, k * P:(k + 1) * P], ident[:, :])
                last.then_inc(s(n + "_turned"), 1)

            def emit(c, first):
                base = (use * NC + (NC if c is None else c)) * (units // 2)

                def unit(step, pair, slot):
                    if isinstance(pair, int) and pair < 0:
                        step(ds(units + 2 * pair + slot, 1), None, slot, base + pair)
                    else:
                        step(ds(pair * 2 + slot, 1), pair, slot, base + pair)

                def up_(u, pair, slot, i):
                    up(c, u, pair, slot, i)

                def down_(u, pair, slot, i):
                    down(u, slot, i)

                def behind_(n):
                    return -((n + 1) // 2), n % 2
                for u in range(lag):
                    if c is not None:
                        unit(up_, u // 2, u % 2)
                    if not first:
                        unit(down_, *behind_(lag - u))
                if c is not None:
                    unit(up_, lag // 2, lag % 2)
                    pe.wait_ge(s(n + "_out"), nth(use * NC + c, 1))
                    nc.tensor.matmul(bank(6), zrow[:, 0:P], zrow[:, :], start=True, stop=False, skip_group_check=True)
                    unit(down_, 0, 0)
                    unit(up_, (lag + 1) // 2, (lag + 1) % 2)
                if not first:
                    turn_result(use * NC + (NC if c is None else c))
                if c is not None:
                    unit(down_, 0, 1)

                    def pairs(k0, k1):
                        with pe.Fori(k0, k1) as k:
                            for r in range(2):
                                unit(up_, k + (lag + r) // 2, (lag + r) % 2)
                                unit(down_, k, r)
                    end = units // 2 - (lag + 1) // 2
                    if not first and puse + 1 < len(stage_order):
                        pairs(1, PREP_AT + 1)
                        turn_rows(pe, (puse + 1) * NC + c - 1, 7, lambda k: xnc[:, k, :], 0)
                        pairs(PREP_AT + 1, end)
                    else:
                        pairs(1, end)
                    if lag % 2:
                        unit(up_, units // 2 - 1, 1)
                        unit(down_, end, 0)
            by_chunk(pe, emit)

        def experts_scalar(act, n, use, puse, units, lag, sg_read, side):
            def silu(r, i):
                act.wait_ge(s(n + "_g"), nth(i, 2, r))
                act.wait_ge(s(sg_read), nth(i, 2, r))
                nc.scalar.activation(sg[:, r, :], bank(r), ACT.Silu, scale=1.0 / WSCALE).then_inc(s(n + "_sg"), 1)

            def high_part(r, i):
                act.wait_ge(s(n + "_hT"), H0 + nth(i, 2, r))
                act.wait_ge(s(n + "_down"), nth(i, 2, r))
                nc.scalar.activation(hh[:, r, :], hT[:, r, :], ACT.Copy).then_inc(s(n + "_hh"), 1)

            def emit(c, first):
                base = (use * NC + (NC if c is None else c)) * (units // 2)
                count = use * NC + (NC if c is None else c)
                def copy_result():
                    act.wait_ge(s(n + "_down"), H0 + count * units)
                    act.wait_ge(s(n + "_turned"), count)
                    nc.scalar.activation(outT, bank(6), ACT.Copy).then_inc(s(n + "_out"), 1)
                if c is None:
                    high_part(1, base - 1)
                    copy_result()
                else:
                    for u in range(4):
                        silu(u % 2, base + u // 2)
                        if u == 2 and lag == 3 and not first:
                            copy_result()
                        if u or not first:
                            high_part((u - 1) % 2, base + (u - 1) // 2)
                        if u == 1 and lag == 2 and not first:
                            copy_result()

                    def pairs(k0, k1):
                        with act.Fori(k0, k1) as k:
                            silu(0, base + k)
                            high_part(1, base + k - 1)
                            silu(1, base + k)
                            high_part(0, base + k)
                    pairs(2, PREP_AT + 2)
                    if not first and puse + 1 < len(stage_order):
                        high(act, (puse + 1) * NC + c - 1, c - 1, 7)
                    pairs(PREP_AT + 2, units // 2 - 1)
                    side(c)
                    pairs(units // 2 - 1, units // 2)
            by_chunk(act, emit)

        def experts_vector(dve, n, use, puse, units, hidden):
            def emit(c, first):
                base = (use * NC + (NC if c is None else c)) * (units // 2)
                if c is not None:
                    for k in range(2):
                        for r in range(2):
                            hidden(r, base + k)
                if not first:
                    count = use * NC + (NC if c is None else c)
                    dve.wait_ge(s(n + "_turned"), 1 + count)
                    xc = x[:, ds(((NC if c is None else c) - 1) * TPC, TPC), :].rearrange("p t c -> p (t c)")
                    nc.vector.scalar_tensor_tensor(xc, bank(7), HALF / WSCALE, xc, ALU.mult, ALU.add).then_inc(s(n + "_added"), 1)
                if c is not None:
                    def pairs(k0, k1):
                        with dve.Fori(k0, k1) as k:
                            for r in range(2):
                                hidden(r, base + k)
                    if not first and puse + 1 < len(stage_order):
                        i = (puse + 1) * NC + c - 1
                        wait_apart(dve, s(n + "_added"), 1 + use * NC + c)
                        statistics(dve, i, c - 1)
                        hidden(0, base + 2)
                        moments(dve, i, c - 1)
                        hidden(1, base + 2)
                        dsts = [lambda k: xnc[:, k, :]]
                        if stage_order[puse + 1] == "LA":
                            dsts.insert(0, lambda k: tile(xn, c - 1, k))
                        normalise(dve, i, c - 1, dsts)
                        pairs(3, PREP_AT + 3)
                        low(dve, i, c - 1, 7)
                        pairs(PREP_AT + 3, units // 2)
                    else:
                        pairs(2, units // 2)
            by_chunk(dve, emit)
            dve.wait_ge(s(n + "_added"), 1 + NC * (use + 1))

        def experts_gpsimd(pool, n, use, puse, units, side):
            def emit(c, first):
                def pairs(k0, k1):
                    with pool.Fori(k0, k1) as k:
                        for r in range(2):
                            pool.wait_ge(s(n + "_hh"), nth((use * NC + c) * (units // 2) + k, 2, r))
                            nc.gpsimd.tensor_tensor(hl[:, r, :], hT[:, r, :], hh[:, r, :], ALU.subtract).then_inc(s(n + "_hl"), 1)
                if c is None:
                    return
                pairs(0, 2)
                if not first and puse + 1 < len(stage_order):
                    inverse_deviation(pool, (puse + 1) * NC + c - 1, c - 1)
                pairs(2, units // 2 - 1)
                side(c)
                pairs(units // 2 - 1, units // 2)
            by_chunk(pool, emit)

        def pieces(use, n):
            def flat(v):
                return v.rearrange("p a b -> p (a b)")
            if n == "F0" and use == 0 and "AT" in stage_order:
                return [(flat(rawqk[:, :, :]), flat(qkh[:, :, :]), flat(qkl[:, :, :]), "qk", 32)]
            if n == "F0" and use == 1:
                return [(flat(raww1), flat(w1h[:, :, :]), flat(w1l[:, :, :]), "w1", 16),
                        (flat(raww2), flat(w216[:, 0]), flat(w216[:, 1]), "w2", 16)]
            return []

        def scale_pieces(act, use, n):
            def side(c):
                cs = ds(c * CHUNK, CHUNK)
                for raw, hi, lo, name, loads in pieces(use, n):
                    if isinstance(c, int):
                        act.wait_ge(s("ld_" + name), loads)
                    nc.scalar.activation(hi[:, cs], raw[:, cs], ACT.Copy, scale=WSCALE)
                    nc.scalar.activation(raw[:, cs], raw[:, cs], ACT.Copy, scale=WSCALE).then_inc(s("hi_" + name), 1)
            return side

        def low_pieces(pool, use, n):
            def side(c):
                cs = ds(c * CHUNK, CHUNK)
                for raw, hi, lo, name, loads in pieces(use, n):
                    pool.wait_ge(s("hi_" + name), nth(c, 1))
                    nc.gpsimd.tensor_tensor(lo[:, cs], raw[:, cs], hi[:, cs], ALU.subtract).then_inc(s(name + "_split"), 1)
            return side

        def ffn0_tensor(pe, use, puse):
            if use == 0:
                pe.wait_ge(s("gu_split"), 1)
                pe.wait_ge(s("ld_sel0"), 16)
                pe.wait_ge(s("dn_split"), 1)
            pe.wait_ge(s("gT0"), NC * (use + 1))

            def up(c, u, pair, r, i):
                cs = ds(c * CHUNK, CHUNK)
                pe.wait_ge(s("f0_hT"), nth(i, 2, r))
                for half_, b in ((0, 0), (1, 2)):
                    ws = ds(half_ * HID, HID)
                    last = matmul3(pe, bank(b + r), guh[:, u, ws], gul[:, u, ws], xTh[:, cs], xTl[:, cs])
                    if half_ == 0:
                        last.then_inc(s("f0_g"), 1)
                nc.tensor.matmul(bank(4 + r), sel0[:, u, :], gT0[:, cs], start=True, stop=True).then_inc(s("f0_u"), 1)
            experts_tensor(pe, "f0", use, puse, U0, LAG0, up, wd16)

        def ffn0_scalar(act, use, puse):
            experts_scalar(act, "f0", use, puse, U0, LAG0, "f0_su", scale_pieces(act, use, "F0"))

        def ffn0_vector(dve, use, puse):
            def hidden(r, i):
                dve.wait_ge(s("f0_sg"), nth(i, 2, r))
                dve.wait_ge(s("f0_u"), nth(i, 2, r))
                nc.vector.tensor_tensor(su[:, r, :], sg[:, r, :], bank(2 + r), ALU.mult).then_inc(s("f0_su"), 1)
                dve.wait_ge(s("f0_su"), H0 + nth(i, 2, r))
                dve.wait_ge(s("f0_hl"), nth(i, 2, r))
                nc.vector.tensor_tensor(hT[:, r, :], su[:, r, :], bank(4 + r), ALU.mult).then_inc(s("f0_hT"), 1)
            experts_vector(dve, "f0", use, puse, U0, hidden)

        QKU = 2 * TPB
        AT_ROUNDS = BATCH * NG
        R0 = 2 * QKU

        def at_loop(eng, emit):
            def rd(b, k):
                return (b + k // NG, k % NG, b * NG + k)
            emit(None, None, None, rd(0, 0))
            emit(None, None, rd(0, 0), rd(0, 1))
            emit(None, rd(0, 0), rd(0, 1), rd(0, 2))
            with eng.Fori(0, BATCH - 2) as b:
                for k in range(NG):
                    emit(rd(b, k), rd(b, k + 1), rd(b, k + 2), rd(b, k + 3))
            b = BATCH - 2
            emit(rd(b, 0), rd(b, 1), rd(b, 2), rd(b, 3))
            emit(rd(b, 1), rd(b, 2), rd(b, 3), None)
            emit(rd(b, 2), rd(b, 3), None, None)
            emit(rd(b, 3), None, None, None)

        def behind(last, core, h):
            rnd, hh = (last, h + 2) if h < 2 else (core, h - 2)
            return (rnd, hh) if rnd else None

        def rotation(turn_, proj_, h):
            rnd, u = (turn_, h + 1) if h < HG - 1 else (proj_, 0)
            return (rnd, u) if rnd else None

        def at_tensor(pe, puse):
            pe.wait_ge(s("ld_vo"), 32)
            for h in range(NH):
                hs = slice(h * HD, (h + 1) * HD)
                last = nc.tensor.matmul(psum[:, h // HG, (h % HG) * C:(h % HG + 1) * C], rawvo[:, 0, hs],
                                        rawvo[:, 1, hs], start=True, stop=True)
            last.then_inc(s("vo_psum"), 1)
            prep_tensor(pe, puse)
            all_xT(pe, puse)
            pe.wait_ge(s("qk_split"), NC)
            pe.wait_ge(s("vo_split"), 1)

            def emit(last_, core, turn_, proj_):
                def project(u):
                    b, g, j = proj_
                    pe.wait_ge(s("qn_ready"), nth(j, QKU, u))
                    tok = ds(b * SEQ + (u // 2) * P, P)
                    cols = slice(g * CHUNK, (g + 1) * CHUNK)
                    matmul3(pe, bank(u % 2), xTh[:, tok], xTl[:, tok], qkh[:, u % 2, cols],
                            qkl[:, u % 2, cols]).then_inc(s("pj_ready"), 1)

                def project_v(t):
                    b, g, j = turn_
                    pe.wait_ge(s("vb_ready"), nth(j, TPB, t))
                    tok = ds(b * SEQ + t * P, P)
                    cols = slice(g * CHUNK, (g + 1) * CHUNK)
                    matmul3(pe, bank(2), xTh[:, tok], xTl[:, tok], voh[:, cols], vol[:, cols]).then_inc(s("v_ready"), 1)

                def turn(u):
                    j = turn_[2]
                    pe.wait_ge(s("rot_ready"), R0 + nth(j, QKU, u))
                    pe.wait_ge(s("qkT_ready"), nth(j, QKU, u))
                    for h in range(HG):
                        last = nc.tensor.transpose(bank(3)[:, h * P:(h + 1) * P], qr[:, u, h * HD:(h + 1) * HD], ident[:, :])
                    last.then_inc(s("tr_ready"), 1)

                def scores(h):
                    b, g, i = core
                    pe.wait_ge(s("qkT_ready"), 1 + nth(i, QKU, QKU - 1))
                    pe.wait_ge(s("exp_ready"), nth(i, HG, h))
                    nc.tensor.matmul(bank(4 + h % 2)[:, 0:SEQ], kT[:, g, h, 0:P], qT[:, g, h, :], start=True, stop=True)
                    nc.tensor.matmul(bank(4 + h % 2)[:, SEQ:SEQ + P], kT[:, g, h, P:SEQ], qT[:, g, h, P:SEQ],
                                     start=True, stop=True).then_inc(s("sc_ready"), 1)

                def values(due):
                    (b, g, i), h = due
                    pe.wait_ge(s("mask_ready"), nth(i, HG, h))
                    pe.wait_ge(s("vb_ready"), 1 + nth(i, TPB, TPB - 1))
                    pe.wait_ge(s("pv_taken"), nth(i, HG, h))
                    o = bank(6 + h % 2)
                    nc.tensor.matmul(o[:, 0:VW], pt[:, h, 0:P], vb[:, g, 0, h, :], start=True, stop=True)
                    nc.tensor.matmul(o[:, SEQ:SEQ + VW], pt[:, h, P:SEQ], vb[:, g, 0, h, :], start=True, stop=False)
                    nc.tensor.matmul(o[:, SEQ:SEQ + VW], pt[:, h, SEQ:SEQ + P], vb[:, g, 1, h, :],
                                     start=False, stop=True).then_inc(s("pv_ready"), 1)
                for h in range(HG):
                    if proj_:
                        project(h)
                    if turn_ and h % 2 == 1:
                        project_v(h // 2)
                    if core:
                        scores(h)
                    if behind(last_, core, h):
                        values(behind(last_, core, h))
                    if turn_:
                        turn(h)
            at_loop(pe, emit)

        def at_scalar(act, puse):
            act.wait_ge(s("vo_psum"), 1)
            nc.scalar.activation(voh[:, :], psum[:, 0:2, :].rearrange("p a b -> p (a b)"), ACT.Copy,
                                 scale=WSCALE).then_inc(s("hi_vo"), 1)
            prep_scalar(act, puse)
            act.preload_act_table(ACT.Exp)
            act.wait_ge(s("vb_ones"), 1)

            def emit(last_, core, turn_, proj_):
                def exps(h):
                    b, g, i = core
                    act.wait_ge(s("sc_ready"), nth(i, HG, h))
                    act.wait_ge(s("pv_ready"), nth(i, HG, h))
                    act.wait_ge(s("rq_ready"), nth(i, TPB, TPB - 1))
                    nc.scalar.activation(pt[:, h, 0:SEQ], bank(4 + h % 2)[:, 0:SEQ], ACT.Exp,
                                         scale=rq[:, ds(i, 1), HG + h])
                    nc.scalar.activation(pt[:, h, SEQ:SEQ + P], bank(4 + h % 2)[:, SEQ:SEQ + P], ACT.Exp,
                                         scale=rq[:, ds(i, 1), 3 * HG + h]).then_inc(s("exp_ready"), 1)

                def squares(u):
                    j = proj_[2]
                    act.wait_ge(s("pj_ready"), nth(j, QKU, u))
                    act.wait_ge(s("ss_ready"), nth(j, QKU, u))
                    nc.scalar.activation(sq[:, u % 2, :], bank(u % 2), ACT.Square).then_inc(s("sq_ready"), 1)

                def copy_out(u):
                    b, g, j = proj_
                    act.wait_ge(s("rot_ready"), nth(j, QKU, u))
                    nc.scalar.activation(qn[:, g, u, :], bank(u % 2), ACT.Copy).then_inc(s("qn_ready"), 1)

                def scale_q(rnd, t):
                    b, g, j = rnd
                    act.wait_ge(s("qn_ready"), 2 + nth(j, QKU, 2 * t))
                    act.wait_ge(s("rq_ready"), nth(j, TPB, t))
                    for h in range(HG):
                        hs = slice(h * HD, (h + 1) * HD)
                        last = nc.scalar.activation(qn[:, g, 2 * t, hs], qn[:, g, 2 * t, hs], ACT.Copy,
                                                    scale=rq[:, ds(j, 1), 2 * t * HG + h])
                    last.then_inc(s("qs_ready"), 1)

                def turned(u):
                    b, g, j = turn_
                    act.wait_ge(s("tr_ready"), QKU + nth(j, QKU, u))
                    dst = (qT, kT)[u % 2][:, g, :, (u // 2) * P:(u // 2 + 1) * P]
                    nc.scalar.activation(dst, bank(3).rearrange("p (h t) -> p h t", h=HG),
                                         ACT.Copy).then_inc(s("qkT_ready"), 1)

                def values_out(t):
                    b, g, j = turn_
                    act.wait_ge(s("v_ready"), nth(j, TPB, t))
                    if last_:
                        act.wait_ge(s("pv_ready"), HG + nth(last_[2], HG, HG - 1))
                    nc.scalar.activation(vb[:, g, t, :, 0:C], bank(2).rearrange("p (h c) -> p h c", h=HG),
                                         ACT.Copy).then_inc(s("vb_ready"), 1)
                for h in range(HG):
                    if proj_:
                        squares(h)
                        copy_out(h)
                    if core:
                        exps(h)
                    if turn_ and h >= 2:
                        values_out(h - 2)
                    if turn_:
                        turned(h)
                    if turn_ and h == 0:
                        scale_q(turn_, 1)
                    if proj_ and h == 2:
                        scale_q(proj_, 0)
            at_loop(act, emit)

        def at_vector(dve, puse):
            prep_vector(dve, puse)
            dve.wait_ge(s("hi_vo"), 1)
            nc.vector.scalar_tensor_tensor(vol[:, :], psum[:, 0:2, :].rearrange("p a b -> p (a b)"), WSCALE, voh[:, :],
                                           ALU.mult, ALU.subtract).then_inc(s("vo_split"), 1)
            dve.wait_ge(s("ld_cos"), 32)
            nc.vector.memset(vb[:, :, :, :, C:VW].rearrange("p g t h c -> p (g t h) c"), WSCALE).then_inc(s("vb_ones"), 1)

            def emit(last_, core, turn_, proj_):
                def sums(u):
                    j = proj_[2]
                    dve.wait_ge(s("rms_ready"), nth(j, TPB, u // 2))
                    dve.wait_ge(s("sq_ready"), nth(j, QKU, u))
                    nc.vector.tensor_reduce(ss[:, u, :], sq[:, u % 2, :].rearrange("p (h d) -> p h d", h=HG), AX,
                                            ALU.add).then_inc(s("ss_ready"), 1)

                def cosines(rnd, u):
                    b, g, j = rnd
                    if u % 2 == 0:
                        dve.wait_ge(s("qs_ready"), nth(j, TPB, u // 2))
                    else:
                        dve.wait_ge(s("qn_ready"), 2 + nth(j, QKU, u))
                    dve.wait_ge(s("rot_ready"), R0 - 2 + nth(j, QKU, u))
                    cs = cosd[:, u // 2, :].unsqueeze(1).broadcast_to([P, HG, HD])
                    nc.vector.tensor_tensor(rpA[:, u % 2, :].rearrange("p (h d) -> p h d", h=HG),
                                            qn[:, g, u, :].rearrange("p (h d) -> p h d", h=HG), cs,
                                            ALU.mult).then_inc(s("cos_ready"), 1)

                def rotated(rnd, u):
                    b, g, j = rnd
                    dve.wait_ge(s("cos_ready"), nth(j, QKU, u))
                    dve.wait_ge(s("sin_ready"), nth(j, QKU, u))
                    dve.wait_ge(s("tr_ready"), nth(j, QKU, u))
                    nc.vector.tensor_tensor(qr[:, u, :], rpA[:, u % 2, :], rpB[:, u % 2, :],
                                            ALU.add).then_inc(s("rot_ready"), 1)

                def add_values(due):
                    (b, g, i), h = due
                    o = bank(6 + h % 2)
                    dve.wait_ge(s("pv_ready"), HG + nth(i, HG, h))
                    nc.vector.reciprocal(rl[:, h % 2, :], o.rearrange("p (t c) -> p t c", t=TPB)[:, :, C]).then_inc(s("rl_ready"), 1)
                    dve.wait_ge(s("rl_ready"), nth(i, HG, h))
                    dve.wait_ge(s("pv_taken"), 1 + nth(i, HG, h))
                    for t in range(TPB):
                        xt = x[:, ds(b * TPB + t, 1), :].rearrange("p o c -> p (o c)")
                        last = nc.vector.scalar_tensor_tensor(xt, o[:, t * SEQ:t * SEQ + C], rl[:, h % 2, t:t + 1], xt,
                                                              ALU.mult, ALU.add)
                    last.then_inc(s("pv_taken"), 1)
                for h in range(HG):
                    if rotation(turn_, proj_, h):
                        cosines(*rotation(turn_, proj_, h))
                    if proj_:
                        sums(h)
                    if behind(last_, core, h):
                        add_values(behind(last_, core, h))
                    if rotation(turn_, proj_, h):
                        rotated(*rotation(turn_, proj_, h))
            at_loop(dve, emit)
            dve.wait_ge(s("pv_taken"), 2 + AT_ROUNDS * HG)
            dve.sem_inc(s("at_done"), 1)

        def at_gpsimd(pool, puse):
            prep_gpsimd(pool, puse)

            def emit(last_, core, turn_, proj_):
                def scale(rnd, t):
                    b, g, j = rnd
                    wait_apart(pool, s("ss_ready"), 2 + nth(j, QKU, 2 * t + 1))
                    nc.gpsimd.tensor_scalar(rms[:, 2 * t:2 * t + 2, :], ss[:, 2 * t:2 * t + 2, :], RMS_EPS * HD * WSCALE ** 2,
                                            None, ALU.add).then_inc(s("rms_ready"), 1)
                    pool.wait_ge(s("rms_ready"), TPB + nth(j, TPB, t))
                    nc.gpsimd.tensor_tensor(rq[:, ds(j, 1), 2 * t * HG:(2 * t + 2) * HG],
                                            rms[:, 2 * t:2 * t + 2, :].rearrange("p u h -> p (u h)"), neghalf[:, 0:2 * HG],
                                            ALU.pow).then_inc(s("rq_ready"), 1)

                def sines(rnd, u):
                    b, g, j = rnd
                    if u % 2 == 0:
                        pool.wait_ge(s("qs_ready"), nth(j, TPB, u // 2))
                    else:
                        pool.wait_ge(s("qn_ready"), 2 + nth(j, QKU, u))
                    pool.wait_ge(s("rot_ready"), R0 - 2 + nth(j, QKU, u))
                    sn = sind[:, u // 2, :].unsqueeze(1).broadcast_to([P, HG, HD])
                    half = HD // 2
                    for k in range(2):
                        last = nc.gpsimd.tensor_tensor(
                            rpB[:, u % 2, :].rearrange("p (h d) -> p h d", h=HG)[:, :, k * half:(k + 1) * half],
                            qn[:, g, u, :].rearrange("p (h d) -> p h d", h=HG)[:, :, (1 - k) * half:(2 - k) * half],
                            sn[:, :, k * half:(k + 1) * half], ALU.mult)
                    last.then_inc(s("sin_ready"), 1)

                def mask(h):
                    b, g, i = core
                    wait_apart(pool, s("exp_ready"), 2 + nth(i, HG, h))
                    v = pt[:, h, :].rearrange("p (n t) -> p n t", t=P)[:, 0:3:2, :]
                    nc.gpsimd.affine_select(out=v, in_=v, compare_op=ALU.is_ge, fill=0.0, base=0,
                                            pattern=[[0, 2], [1, P]], channel_multiplier=-1).then_inc(s("mask_ready"), 1)
                for h in range(HG):
                    if proj_ and h == 2:
                        scale(proj_, 0)
                    if turn_ and h == 0:
                        scale(turn_, 1)
                    if rotation(turn_, proj_, h):
                        sines(*rotation(turn_, proj_, h))
                    if core:
                        mask(h)
            at_loop(pool, emit)

        probs = rt[:, 1].rearrange("p t e -> p (t e)")[:, 0:NT * E1]

        def route1_tensor(pe, use, puse):
            all_xT(pe, puse)
            if use == 0:
                pe.wait_ge(s("cw_split"), 1)
            for t in range(NT):
                last = matmul3(pe, bank(0)[:, t * E1:(t + 1) * E1], xTh[:, t * P:(t + 1) * P],
                               xTl[:, t * P:(t + 1) * P], cwh[:, :], cwl[:, :])
            last.then_inc(s("logit1"), 1)
            pe.wait_ge(s("prob1"), use + 1)
            for t in range(TPB):
                last = nc.tensor.transpose(psum[0:64, 1, t * P:(t + 1) * P], probs[:, t * 64:(t + 1) * 64], ident[:, :])
            last.then_inc(s("probT"), 1)

        def route1_scalar(act, use):
            act.wait_ge(s("shift1"), use + 1)
            v = rt[:, 0].rearrange("p t e -> p (t e)")[:, 0:NT * E1]
            nc.scalar.activation(v, v, ACT.Exp, scale=1.0 / WSCALE).then_inc(s("exp1"), 1)
            act.preload_act_table(ACT.Silu)

        ROUTE1_STEPS = 1 + 3 + 1 + 16 + 2

        def route1_vector(dve, use):
            n = [0]

            def step(ins):
                n[0] += 1
                ins.then_inc(s("route1_step"), 1)
                dve.wait_ge(s("route1_step"), ROUTE1_STEPS * use + n[0])

            def tiles(v):
                return v.rearrange("p t e -> p (t e)")[:, 0:NT * E1].rearrange("p (t e) -> p t e", e=E1)

            def eachtile(v):
                return v.unsqueeze(2).broadcast_to([P, NT, E1])
            L = bank(0)[:, 0:NT * E1].rearrange("p (t e) -> p t e", t=NT)
            dve.wait_ge(s("logit1"), use + 1)
            step(nc.vector.tensor_reduce(rs[:, 0, :], L, AX, ALU.max))
            nc.vector.tensor_tensor(tiles(rt[:, 0]), L, eachtile(rs[:, 0, :]), ALU.subtract).then_inc(s("shift1"), 1)
            dve.wait_ge(s("exp1"), use + 1)
            step(nc.vector.tensor_reduce(rs[:, 1, :], tiles(rt[:, 0]), AX, ALU.add))
            step(nc.vector.reciprocal(rs[:, 2, :], rs[:, 1, :]))
            nc.vector.tensor_tensor(probs.rearrange("p (t b e) -> p b t e", t=TPB, b=BATCH),
                                    tiles(rt[:, 0]).rearrange("p (b t) e -> p b t e", t=TPB),
                                    eachtile(rs[:, 2, :]).rearrange("p (b t) e -> p b t e", t=TPB),
                                    ALU.mult).then_inc(s("prob1"), 1)
            dve.wait_ge(s("probT"), use + 1)
            step(nc.vector.tensor_copy(pT, psum[0:64, 1, 0:SEQ]))
            for k in range(TOPK // 8):
                src = pT if k == 0 else pW[:, (k - 1) % 2]
                step(nc.vector.max(top8[:, :], src))
                step(nc.vector.match_replace(pW[:, k % 2], top8[:, :], src, 0.0))
            step(nc.vector.tensor_tensor(pD, pT, pW[:, (TOPK // 8 - 1) % 2], ALU.subtract))
            step(nc.vector.tensor_copy(gT1[0:64, :], pD))
            step(nc.vector.tensor_tensor(pD, pD, gT1[0:64, :], ALU.subtract))
            nc.vector.tensor_copy(gT1[64:128, :], pD).then_inc(s("gate1"), 1)

        def ffn1_tensor(pe, use, puse):
            if use == 0:
                pe.wait_ge(s("w1_split"), NC)
                pe.wait_ge(s("ld_sel1"), 16)
                pe.wait_ge(s("w2_split"), NC)
            pe.wait_ge(s("gate1"), use + 1)
            w1hu = w1h[:, :, :].rearrange("p e (f c) -> p (e f) c", c=P)
            w1lu = w1l[:, :, :].rearrange("p e (f c) -> p (e f) c", c=P)

            def up(c, u, e, r, i):
                cs = ds(c * CHUNK, CHUNK)
                pe.wait_ge(s("f1_hT"), nth(i, 2, r))
                matmul3(pe, bank(r), w1hu[:, u, :], w1lu[:, u, :], xTh[:, cs], xTl[:, cs]).then_inc(s("f1_g"), 1)
                for k in range(BPC):
                    last = nc.tensor.matmul(bank(4 + r)[:, k * SEQ:(k + 1) * SEQ],
                                            sel1[:, ds((c * BPC + k) * E1 + e, 1), :], gT1[:, :], start=True, stop=True)
                last.then_inc(s("f1_w"), 1)
            experts_tensor(pe, "f1", use, puse, U1, LAG1, up, w216)

        def ffn1_scalar(act, use, puse):
            experts_scalar(act, "f1", use, puse, U1, LAG1, "f1_hT", scale_pieces(act, use, "F1"))

        def ffn1_vector(dve, use, puse):
            def hidden(r, i):
                dve.wait_ge(s("f1_sg"), nth(i, 2, r))
                dve.wait_ge(s("f1_w"), nth(i, 2, r))
                dve.wait_ge(s("f1_hl"), nth(i, 2, r))
                nc.vector.tensor_tensor(hT[:, r, :], sg[:, r, :], bank(4 + r), ALU.mult).then_inc(s("f1_hT"), 1)
            experts_vector(dve, "f1", use, puse, U1, hidden)

        def sample(c, k, q):
            return c * WS + k * SU + q + 1

        def half(c, k, q, jt):
            return (c * WS + k * SU + q) * 2 + jt + 1

        def kernel_groups():
            return [(r * SG + g, g, r) for r in range(2) for g in range(SG)]

        def la_tensor(pe, puse):
            prep_tensor(pe, puse)
            all_xT(pe, puse)
            pe.wait_ge(s("ww_split"), 1)
            for t in range(NT):
                last = matmul3(pe, bank(0)[:, t * 2 * WH:(t + 1) * 2 * WH], xTh[:, t * P:(t + 1) * P],
                               xTl[:, t * P:(t + 1) * P], wwh[:, :], wwl[:, :])
            last.then_inc(s("wave_ready"), 1)
            pe.wait_ge(s("kw_split"), 2)
            with pe.Fori(0, NC // 2) as c2:
                for i, g, r in kernel_groups():
                    cs = ds(c2 * 2 * CHUNK + r * CHUNK, CHUNK)
                    pe.wait_ge(s("sil_ready"), nth(c2, 2 * SG, i))
                    matmul3(pe, bank(6 + i % 2), kwh[:, g].rearrange("p d r -> p (d r)"),
                            kwl[:, g].rearrange("p d r -> p (d r)"), xTh[:, cs], xTl[:, cs]).then_inc(s("kp_ready"), 1)
            pe.wait_ge(s("stag_ready"), 1)
            for c in range(NC):
                for k in range(TPC):
                    last = nc.tensor.transpose(psum[0:POSK, 1 + c, k * P:(k + 1) * P], stag[:, c * TPC + k, :], ident[:, :])
                last.then_inc(s("posT_psum"), 1)
            pe.wait_ge(s("ld_df"), 16)
            pe.wait_ge(s("kwt_ready"), 2 + NC * SG)
            pe.wait_ge(s("ld_selS"), 32)
            pe.wait_ge(s("ld_ow"), 16)
            pe.wait_ge(s("posT"), NC)
            with pe.Fori(0, NC // 2) as c2:
                for r in range(2):
                    c = c2 * 2 + r
                    cs = ds(c2 * 2 * CHUNK + r * CHUNK, CHUNK)

                    def positions(n, g, k, q):
                        for jt in range(2):
                            v = (2 * (r + q) + jt) % UR
                            pe.wait_ge(s("clip_ready"), half(c, k, q, jt))
                            nc.tensor.matmul(bank(v), selS[0:POSK, n, jt, :], posT[0:POSK, cs],
                                             start=True, stop=True).then_inc(s("pos_ready"), 1)
                        pe.wait_ge(s("ws_ready"), sample(c, k, q))
                        nc.tensor.matmul(bank(6), selW[:, q % SU, :], kwt[:, g, cs], start=True,
                                         stop=True).then_inc(s("w_ready"), 1)

                    def samples(k, q):
                        pe.wait_ge(s("prod_ready"), sample(c, k, q))
                        for jt in range(2):
                            v = (2 * (r + q) + jt) % UR
                            pe.wait_ge(s("clip_ready"), UR + half(c, k, q, jt))
                            for b in range(BPC):
                                last = nc.tensor.matmul(bank(4 + (r + q) % 2)[:, b * SEQ:(b + 1) * SEQ], dxs[:, r, b, jt, :],
                                                        uu[:, v, b * SEQ:(b + 1) * SEQ], start=(jt == 0 and b == 0),
                                                        stop=(jt == 1), skip_group_check=True)
                            last.then_inc(s("uu_used"), 1)

                    pe.wait_ge(s("yw_ready"), nth(c, 1))
                    for b in range(BPC):
                        x0 = xn[:, ds((c2 * 2 + r) * TPC + b * TPB, 1), :].rearrange("p o c -> p (o c)")
                        x1 = xn[:, ds((c2 * 2 + r) * TPC + b * TPB + 1, 1), :].rearrange("p o c -> p (o c)")
                        for jt, (m0, m1) in enumerate(((0, 1), (3, 2))):
                            o = bank(7)[:, (b * TPB + jt) * C:(b * TPB + jt + 1) * C]
                            nc.tensor.matmul(o, diffm[:, m0, :], x0, start=True, stop=False)
                            last = nc.tensor.matmul(o, diffm[:, m1, :], x1, start=False, stop=True)
                    last.then_inc(s("dx_psum"), 1)
                    positions(ds(0, 1), ds(0, 1), 0, 0)
                    wait_apart(pe, s("dx_ready"), nth(c, 1))
                    with pe.Fori(0, SG - 1) as k:
                        for q in range(SU):
                            positions(ds(k * SU + q + 1, 1), ds(k, 1) if q < SU - 1 else ds(k + 1, 1), k, q + 1)
                            samples(k, q)
                    samples(SG - 1, 0)
                    pe.wait_ge(s("acc_sum"), 4 + nth(c, WS, WS - 1))
                    for k in range(TPC):
                        last = nc.tensor.matmul(bank(7)[:, k * P:(k + 1) * P], wacc[:, k * P:(k + 1) * P], ow[:, :],
                                                start=True, stop=True)
                    last.then_inc(s("y_psum"), 1)

        def la_scalar(act, puse):
            act.wait_ge(s("ld_kw"), 16)
            for d in range(2):
                nc.scalar.activation(kwh[:, :, d, :], rawkw[:, 0:SG, :], ACT.Copy, scale=WSCALE).then_inc(s("hi_kw"), 1)
            split_act(act, wwh[:, :], wwr[:, :], "ld_ww", 16)
            prep_scalar(act, puse)
            act.wait_ge(s("wz_ready"), 1)
            wzf = wz[:, :, :, :].rearrange("p t a h -> p (t a h)")
            nc.scalar.activation(wzf, wzf, ACT.Silu).then_inc(s("wave_act"), 1)
            act.wait_ge(s("wave_act"), 1)
            nc.scalar.activation(wz[:, :, 1, :], wz[:, :, 1, :], ACT.Tanh).then_inc(s("wave_act"), 1)
            nc.scalar.activation(wz[:, :, 0, :], wz[:, :, 0, :], ACT.Sigmoid).then_inc(s("wave_act"), 1)
            act.preload_act_table(ACT.Silu)
            act.wait_ge(s("ld_kb"), 32)
            with act.Fori(0, NC // 2) as c2:
                for i, g, r in kernel_groups():
                    act.wait_ge(s("kp_ready"), nth(c2, 2 * SG, i))
                    nc.scalar.activation(kwt[:, g, ds(c2 * 2 * CHUNK + r * CHUNK, CHUNK)], bank(6 + i % 2), ACT.Silu,
                                         bias=kb[:, g:g + 1], scale=1.0 / WSCALE)
                    act.wait_ge(s("kwt_ready"), nth(c2, 2 * SG, i))
                    nc.scalar.activation(sil[:, i % 2, :], bank(6 + i % 2), ACT.Silu, bias=kb[:, g:g + 1],
                                         scale=1.0 / WSCALE).then_inc(s("sil_ready"), 1)
            for c in range(NC):
                act.wait_ge(s("posT_psum"), c + 1)
                nc.scalar.activation(posT[0:POSK, c * CHUNK:(c + 1) * CHUNK], psum[0:POSK, 1 + c, :],
                                     ACT.Copy).then_inc(s("posT"), 1)
            with act.Fori(0, NC // 2) as c2:
                for r in range(2):
                    c = c2 * 2 + r
                    act.wait_ge(s("dx_psum"), nth(c, 1))
                    nc.scalar.activation(dxs[:, r].rearrange("p b t c -> p (b t c)"), bank(7), ACT.Copy).then_inc(s("dx_ready"), 1)

                    def copy_weights(k, q):
                        act.wait_ge(s("w_ready"), sample(c, k, q))
                        act.wait_ge(s("prod_ready"), sample(c, k, q))
                        nc.scalar.activation(wsm[:, (r + q) % 2, :], bank(6), ACT.Copy).then_inc(s("ws_ready"), 1)
                    with act.Fori(0, SG - 1) as k:
                        for q in range(SU):
                            copy_weights(k, q)
                    copy_weights(SG - 1, 0)
                    act.wait_ge(s("y_psum"), nth(c, 1))
                    act.wait_ge(s("res_done"), nth(c, 1))
                    nc.scalar.activation(yw, bank(7), ACT.Silu).then_inc(s("yw_ready"), 1)

        def la_vector(dve, puse):
            dve.wait_ge(s("hi_kw"), 2)
            for d in range(2):
                nc.vector.scalar_tensor_tensor(kwl[:, :, d, :], rawkw[:, 0:SG, :], WSCALE, kwh[:, :, d, :],
                                               ALU.mult, ALU.subtract).then_inc(s("kw_split"), 1)
            split_dve(dve, wwl[:, :], wwr[:, :], wwh[:, :], "ld_ww", "ww_split")
            prep_vector(dve, puse)
            n = [0]

            def step(ins):
                n[0] += 1
                ins.then_inc(s("wave_step"), 1)
                dve.wait_ge(s("wave_step"), n[0])
            dve.wait_ge(s("wave_ready"), 1)
            dve.wait_ge(s("ld_wb"), 16)
            wzf = wz[:, :, :, :].rearrange("p t a h -> p t (a h)")
            nc.vector.scalar_tensor_tensor(wzf, bank(0)[:, 0:NT * 2 * WH].rearrange("p (t w) -> p t w", t=NT), 1.0 / WSCALE,
                                           wb[:, :].unsqueeze(1).broadcast_to([P, NT, 2 * WH]),
                                           ALU.mult, ALU.add).then_inc(s("wz_ready"), 1)
            dve.wait_ge(s("wave_act"), 3)
            dve.wait_ge(s("ld_sg"), 32)
            nc.vector.tensor_reduce(wav[:, 0, :], wz[:, :, 0, :], AX, ALU.add)
            step(nc.vector.tensor_reduce(wav[:, 1, :], wz[:, :, 1, :], AX, ALU.add))
            nc.vector.tensor_scalar(wav[:, 2, :], wav[:, 0, :], (MAX_FREQ - MIN_FREQ) / WH, MIN_FREQ, ALU.mult, ALU.add)
            step(nc.vector.scalar_tensor_tensor(wav[:, 3, :], wav[:, 1, :], MAX_FREQ / WH, tokpos[:, :], ALU.mult, ALU.add))
            step(nc.vector.tensor_tensor(pos[:, :, :], sgrid[:, :].unsqueeze(1).broadcast_to([P, NT, WS]),
                                         wav[:, 2, :].unsqueeze(2).broadcast_to([P, NT, WS]), ALU.mult))
            step(nc.vector.tensor_tensor(pos[:, :, :], pos[:, :, :], wav[:, 3, :].unsqueeze(2).broadcast_to([P, NT, WS]), ALU.add))
            step(nc.vector.tensor_scalar(pos[:, :, :], pos[:, :, :], 0.0, SEQ - 1.0, ALU.max, ALU.min))
            step(nc.vector.tensor_copy(pos16[:, :, :], pos[:, :, :]))
            nc.vector.tensor_copy(stag[:, :, 0:WS], pos16[:, :, :])
            step(nc.vector.tensor_tensor(posr[:, :, :], pos[:, :, :], pos16[:, :, :], ALU.subtract))
            step(nc.vector.tensor_copy(pos16[:, :, :], posr[:, :, :]))
            nc.vector.tensor_copy(stag[:, :, WS:2 * WS], pos16[:, :, :])
            nc.vector.tensor_tensor(stag[:, :, 2 * WS:3 * WS], posr[:, :, :], pos16[:, :, :], ALU.subtract)
            nc.vector.memset(stag[:, :, 3 * WS:POSK], 1.0).then_inc(s("stag_ready"), 1)

            with dve.Fori(0, NC // 2) as c2:
                for r in range(2):
                    c = c2 * 2 + r
                    def clips(k, q):
                        for jt in range(2):
                            v = (2 * (r + q) + jt) % UR
                            dve.wait_ge(s("pos_ready"), half(c, k, q, jt))
                            dve.wait_ge(s("uu_used"), half(c, k, q, jt))
                            nc.vector.tensor_scalar(uu[:, v, :], bank(v), 0.0, 1.0, ALU.max, ALU.min).then_inc(s("clip_ready"), 1)

                    def weigh(k, q):
                        dve.wait_ge(s("uu_used"), UR + half(c, k, q, 1))
                        dve.wait_ge(s("ws_ready"), 1 + sample(c, k, q))
                        dve.wait_ge(s("acc_sum"), sample(c, k, q))
                        nc.vector.tensor_tensor(prod[:, (r + q) % 4, :], wsm[:, (r + q) % 2, :], bank(4 + (r + q) % 2),
                                                ALU.mult).then_inc(s("prod_ready"), 1)
                    clips(0, 0)
                    with dve.Fori(0, SG - 1) as k:
                        for q in range(SU):
                            clips(k, q + 1)
                            weigh(k, q)
                    weigh(SG - 1, 0)
                    dve.wait_ge(s("yw_ready"), 1 + nth(c, 1))
                    xc = x[:, ds(c * TPC, TPC), :].rearrange("p t c -> p (t c)")
                    nc.vector.tensor_tensor(xc, xc, yw, ALU.add).then_inc(s("res_done"), 1)
            dve.wait_ge(s("res_done"), 1 + NC)

        def la_gpsimd(pool, puse):
            prep_gpsimd(pool, puse)
            with pool.Fori(0, NC // 2) as c2:
                for i, g, r in kernel_groups():
                    pool.wait_ge(s("sil_ready"), 2 + nth(c2, 2 * SG, i))
                    lo = kwt[P // 2:P, g, ds(c2 * 2 * CHUNK + r * CHUNK, CHUNK)]
                    nc.gpsimd.tensor_tensor(lo, sil[P // 2:P, i % 2, :], lo, ALU.subtract).then_inc(s("kwt_ready"), 1)
            pool.wait_ge(s("kwt_ready"), 2 + NC * SG)
            with pool.Fori(0, NC // 2) as c2:
                for r in range(2):
                    c = c2 * 2 + r
                    wait_apart(pool, s("yw_ready"), nth(c, 1))
                    nc.gpsimd.memset(wacc, 0.0).then_inc(s("wacc0"), 1)
                    wait_apart(pool, s("wacc0"), nth(c, 1))

                    def add(k, q):
                        pool.wait_ge(s("prod_ready"), 2 + sample(c, k, q))
                        pool.wait_ge(s("acc_sum"), 3 + sample(c, k, q))
                        nc.gpsimd.tensor_tensor(wacc, wacc, prod[:, (r + q) % 4, :], ALU.add).then_inc(s("acc_sum"), 1)
                    with pool.Fori(0, SG - 1) as k:
                        for q in range(SU):
                            add(k, q)
                    add(SG - 1, 0)

        def split_act(act, dst, src, wait, n):
            act.wait_ge(s(wait), n)
            nc.scalar.activation(dst, src, ACT.Copy, scale=WSCALE).then_inc(s("hi_" + wait), 1)

        def split_dve(dve, dst, src, hi, wait, done):
            dve.wait_ge(s("hi_" + wait), 1)
            nc.vector.scalar_tensor_tensor(dst, src, WSCALE, hi, ALU.mult, ALU.subtract).then_inc(s(done), 1)

        def flat(v):
            return v.rearrange("p a b -> p (a b)")

        @block.gpsimd
        def _(pool):
            pool.sem_inc(s("acc_sum"), 4)
            pool.sem_inc(s("f0_hl"), H0)
            pool.sem_inc(s("f1_hl"), H0)
            pool.sem_inc(s("rms_ready"), TPB)
            pool.sem_inc(s("kwt_ready"), 2)
            nc.gpsimd.memset(neghalf[:, :], -0.5)
            nc.gpsimd.memset(zrow[:, :], 0.0).then_inc(s("consts"), 1)
            nc.gpsimd.memset(gst[:, :, :], 0.0).then_inc(s("gst0"), 1)
            pool.wait_ge(s("gst0"), 1)
            nc.gpsimd.memset(gst[:, :, E0:U0], 1.0).then_inc(s("consts"), 1)
            nc.gpsimd.iota(revidx[:, :], pattern=[[-1, E0]], base=E0, channel_multiplier=0,
                           allow_small_or_imprecise_dtypes=True).then_inc(s("consts"), 1)
            pool.wait_ge(s("consts"), 3)
            uses = {}
            for pu, st in enumerate(stage_order):
                use = uses.get(st, 0)
                uses[st] = use + 1
                if st == "AT":
                    at_gpsimd(pool, pu)
                elif st == "LA":
                    la_gpsimd(pool, pu)
                else:
                    prep_gpsimd(pool, pu)
                    if st == "F0":
                        experts_gpsimd(pool, "f0", use, pu, U0, low_pieces(pool, use, st))
                    else:
                        experts_gpsimd(pool, "f1", use, pu, U1, low_pieces(pool, use, st))

        @block.scalar
        def _(act):
            act.sem_inc(s("f0_out"), 1)
            act.sem_inc(s("f1_out"), 1)
            act.sem_inc(s("vb_ready"), 1)
            act.sem_inc(s("qkT_ready"), 1)
            act.sem_inc(s("qn_ready"), 2)
            act.sem_inc(s("exp_ready"), 2)
            act.sem_inc(s("ws_ready"), 1)
            act.sem_inc(s("sil_ready"), 2)
            act.sem_inc(s("yw_ready"), 1)
            split_act(act, rwh[:, :], rwr[:, :], "ld_rw", 16)
            split_act(act, flat(guh[:, :, :]), flat(rawgu), "ld_gu", 48)
            split_act(act, flat(wd16[:, 0]), flat(rawdn), "ld_dn", 32)
            uses = {}
            for pu, st in enumerate(stage_order):
                use = uses.get(st, 0)
                uses[st] = use + 1
                if st == "AT":
                    at_scalar(act, pu)
                    continue
                if st == "LA":
                    la_scalar(act, pu)
                    continue
                if st == "F1" and use == 0:
                    split_act(act, cwh[:, :], cwr[:, :], "ld_cw", 16)
                prep_scalar(act, pu)
                if st == "F1":
                    route1_scalar(act, use)
                    ffn1_scalar(act, use, pu)
                if st == "F0":
                    route0_scalar(act, use)
                    act.preload_act_table(ACT.Silu)
                    ffn0_scalar(act, use, pu)

        @block.vector
        def _(dve):
            dve.sem_inc(s("xT_ready"), XT0)
            dve.sem_inc(s("f0_hT"), H0)
            dve.sem_inc(s("f0_su"), H0)
            dve.sem_inc(s("f0_added"), 1)
            dve.sem_inc(s("f1_hT"), H0)
            dve.sem_inc(s("f1_added"), 1)
            dve.sem_inc(s("ss_ready"), 2)
            dve.sem_inc(s("rot_ready"), R0)
            dve.sem_inc(s("pv_taken"), 2)
            dve.sem_inc(s("clip_ready"), UR)
            dve.sem_inc(s("prod_ready"), 2)
            dve.sem_inc(s("res_done"), 1)
            split_dve(dve, rwl[:, :], rwr[:, :], rwh[:, :], "ld_rw", "rw_split")
            dve.wait_ge(s("ld_x"), 16)
            dve.wait_ge(s("consts"), 3)
            uses = {}
            for pu, st in enumerate(stage_order):
                use = uses.get(st, 0)
                uses[st] = use + 1
                if st == "AT":
                    at_vector(dve, pu)
                    continue
                if st == "LA":
                    la_vector(dve, pu)
                    continue
                if st == "F1" and use == 0:
                    split_dve(dve, cwl[:, :], cwr[:, :], cwh[:, :], "ld_cw", "cw_split")
                prep_vector(dve, pu)
                if st == "F1":
                    route1_vector(dve, use)
                    ffn1_vector(dve, use, pu)
                if st == "F0":
                    route0_vector(dve, use)
                    if use == 0:
                        split_dve(dve, flat(gul[:, :, :]), flat(rawgu), flat(guh[:, :, :]), "ld_gu", "gu_split")
                        split_dve(dve, flat(wd16[:, 1]), flat(rawdn), flat(wd16[:, 0]), "ld_dn", "dn_split")
                    ffn0_vector(dve, use, pu)
            dve.sem_inc(s("x_final"), 1)

        @block.tensor
        def _(pe):
            pe.wait_ge(s("ld_ident"), 16)
            pe.sem_inc(s("f0_down"), H0)
            pe.sem_inc(s("f0_turned"), 1)
            pe.sem_inc(s("f1_down"), H0)
            pe.sem_inc(s("f1_turned"), 1)
            pe.sem_inc(s("tr_ready"), 4)
            pe.sem_inc(s("pv_ready"), HG)
            pe.sem_inc(s("uu_used"), UR)
            pe.wait_ge(s("consts"), 3)
            uses = {}
            for pu, st in enumerate(stage_order):
                use = uses.get(st, 0)
                uses[st] = use + 1
                if st == "AT":
                    at_tensor(pe, pu)
                    continue
                if st == "LA":
                    la_tensor(pe, pu)
                    continue
                prep_tensor(pe, pu)
                if st == "F1":
                    route1_tensor(pe, use, pu)
                    ffn1_tensor(pe, use, pu)
                if st == "F0":
                    route0_tensor(pe, use, pu)
                    ffn0_tensor(pe, use, pu)


def _constants():
    ident = np.eye(P, dtype=np.float32)
    sel0 = np.zeros((64, U0, P), np.float16)
    for u in range(U0):
        sel0[u, u] = 1 / WSCALE
        sel0[32 + u, u] = 1 / WSCALE
    sel1 = np.zeros((P, BATCH * E1, P), np.float16)
    for i in range(BATCH * E1):
        sel1[i, i] = 1
        sel1[64 + i, i] = 1
    j = np.arange(HD // 2, dtype=np.float32)
    freqs = np.power(np.float32(ROPE_BASE), -j / np.float32(HD // 2)).astype(np.float32)
    rad = (np.arange(SEQ, dtype=np.float32)[:, None] * freqs[None, :]).astype(np.float32).astype(np.float64)
    cos, sin = np.cos(rad).astype(np.float32), np.sin(rad).astype(np.float32)
    cosd = np.concatenate([cos, cos], 1).reshape(TPB, P, HD).transpose(1, 0, 2).copy()
    sind = np.concatenate([-sin, sin], 1).reshape(TPB, P, HD).transpose(1, 0, 2).copy()
    selS = np.zeros((POSK, WS, 2, P), np.float32)
    for t in range(WS):
        selS[[p * WS + t for p in range(PIECES)], t] = 1
    selS[POSK - 1] = -np.arange(SEQ, dtype=np.float32).reshape(2, P)
    selS[POSK - 1, :, 1, P - 1] = 1
    d = np.zeros((P, 4, P), np.float32)
    for k in range(P):
        d[k, 0, k] = -1
        if k:
            d[k, 0, k - 1] = 1
            d[k, 2, k - 1] = 1
        if k < P - 1:
            d[k, 2, k] = -1
    d[0, 1, P - 1] = 1
    d[0, 3, P - 1] = 1
    selW = np.zeros((2, SU, WH, SU, WH, WD), np.float16)
    for t in range(SU):
        for h in range(WH):
            selW[:, t, h, t, h, :] = 1
    sgrid = np.tile(np.arange(WS, dtype=np.float32) - (WS // 2), (P, 1))
    tokpos = np.zeros((P, NT), np.float32)
    for t in range(NT):
        tokpos[:, t] = np.arange(P) + (t % TPB) * P
    return {"ident": ident, "sel0": sel0, "sel1": sel1, "cosd": cosd, "sind": sind,
            "selS": selS.astype(np.float16), "diffm": d, "selW": selW.reshape(P, SU, P), "sgrid": sgrid, "tokpos": tokpos}


_TRANSPOSED = {"L0_ffn_router_w": (1, 0), "L0_ffn_shared_gate_w": (1, 0), "L0_ffn_shared_up_w": (1, 0),
               "L0_ffn_shared_down_w": (1, 0), "L0_attn_wv": (2, 1, 0), "L1_attn_wave_w": (1, 0),
               "L1_attn_kernel_w": (3, 1, 2, 0), "L1_attn_kernel_b": (2, 0, 1),
               "L1_attn_out_w": (1, 0), "L1_ffn_choice_w": (1, 0)}
_SHAPED = {"L1_attn_kernel_w": (WH, WK // SU, SU, C), "L1_attn_kernel_b": (WH, WK // SU, SU)}
_MERGED = {"L1_attn_kernel_w": (C, WK // SU, SU * WH), "L1_attn_kernel_b": (SU * WH, WK // SU)}
_STAGES = ["F0", "AT", "F0", "F1", "LA", "F1"]


def _laid_out(name, v):
    v = v.reshape(_SHAPED.get(name, v.shape))
    v = v.transpose(_TRANSPOSED.get(name, range(v.ndim)))
    return np.ascontiguousarray(v.reshape(_MERGED.get(name, v.shape)))


def kernel(**inputs):
    import concourse.bacc as _bacc
    from concourse.bass_utils import run_bass_kernel_spmd as _run

    nc = _bacc.Bacc("TRN2", target_bir_lowering=False, num_devices=1)
    host = dict(_constants())
    for name, v in inputs.items():
        v = np.asarray(v)
        host[name] = _laid_out(name, v)
    arrays, aps = {}, {"_stages": _STAGES}
    for name, v in host.items():
        arrays[f"in_{name}"] = v
        aps[name] = nc.dram_tensor(f"in_{name}", v.shape, mybir.dt.from_np(v.dtype), kind="ExternalInput").ap()
    out = nc.dram_tensor("out_x", (BATCH, SEQ, C), F32, kind="ExternalOutput").ap()
    macaron_kernel(nc, aps, out)
    r = _run(nc, [arrays], core_ids=[0])
    return r.results[0]["out_x"]
```

```python
import numpy as np
import concourse.bass as bass
from concourse import mybir
from contextlib import ExitStack

F32 = mybir.dt.float32
F16 = mybir.dt.float16
BF16 = mybir.dt.bfloat16
ALU = mybir.AluOpType
ACT = mybir.ActivationFunctionType
AX = mybir.AxisListType.X
ds = bass.ds

BATCH, SEQ, C = 8, 256, 128
P = 128
NT = BATCH * SEQ // P
TPB = SEQ // P
CHUNK = 512
NC = BATCH * SEQ // CHUNK
TPC = CHUNK // P
BPC = CHUNK // SEQ
LN_EPS = 1e-5
HALF = 0.5
E0, HID = 16, 128
U0 = E0 + 2
NH, HD = 8, 128
HG = 4
NG = NH // HG
RMS_EPS = 1e-6
ROPE_BASE = 1250
E1, FF = 8, 256
F1 = FF // P
U1 = E1 * F1
TOPK = SEQ * 2 // E1
WH, WK, WS = 8, 64, 33
WD = C // WH
MAX_FREQ, MIN_FREQ = 16.0, 1.0
SU = P // (2 * WH)
SG = -(-WS // SU)
UR = 4
PIECES = 3
POSK = PIECES * WS
PR = 2
WSCALE = 64.0


def macaron_kernel(nc, a, out):
    ctx = ExitStack()
    with ctx:
        def sb(name, shape, dt=F32):
            return ctx.enter_context(nc.sbuf_tensor(name, shape, dt))

        def sem(name):
            return ctx.enter_context(nc.semaphore(name))

        psum = ctx.enter_context(nc.psum_tensor("psum", [P, 8, CHUNK], F32))

        def bank(i):
            return psum[:, i, :]

        x = sb("x", [P, NT, C])
        xn = sb("xn", [P, NT, C])
        xTh = sb("xTh", [P, NT * P], F16)
        xTl = sb("xTl", [P, NT * P], F16)
        ident = sb("ident", [P, P])
        neghalf = sb("neghalf", [P, NT])
        stats = sb("stats", [P, NT, 6])
        mv = sb("mv", [P, NT, 2])
        rstd = sb("rstd", [P, NT])
        rvar = sb("rvar", [P, NT])

        guh = sb("guh", [P, U0, 2 * HID], F16)
        gul = sb("gul", [P, U0, 2 * HID], F16)
        wd16 = sb("wd16", [P, 2, U0, C], F16)
        rwh = sb("rwh", [P, E0], F16)
        rwl = sb("rwl", [P, E0], F16)
        rwr = sb("rwr", [P, E0])
        sel0 = sb("sel0", [64, U0, P], F16)
        gT0 = sb("gT0", [64, NT * P], F16)
        w1h = sb("w1h", [P, E1, FF], F16)
        w1l = sb("w1l", [P, E1, FF], F16)
        w216 = sb("w216", [P, 2, U1, C], F16)
        cwh = sb("cwh", [P, E1], F16)
        cwl = sb("cwl", [P, E1], F16)
        cwr = sb("cwr", [P, E1])
        lent = sb("lent", [P, 4096])
        gT1 = sb("gT1", [P, SEQ], F16)
        qkh = sb("qkh", [P, 2, NH * HD], F16)
        qkl = sb("qkl", [P, 2, NH * HD], F16)
        voh = sb("voh", [P, NH * C], F16)
        vol = sb("vol", [P, NH * C], F16)
        rawqk = sb("rawqk", [P, 2, NH * HD])
        rawvo = sb("rawvo", [P, 2, NH * HD])
        raww1 = rawqk[:, :, :].rearrange("p a (e f) -> p (a e) f", f=FF)
        work = sb("work", [P, 6, CHUNK])
        sg, su, hT = work[:, 0:2, :], work[:, 2:4, :], work[:, 4:6, :]
        zrow = sb("zrow", [1, CHUNK], F16)
        rt = sb("rt", [P, 6, NT, E0])
        rs = sb("rs", [P, 6, NT])
        hh = rt[:, 0:2].rearrange("p a t e -> p (a t e)").bitcast(F16).rearrange("p (r c) -> p r c", r=2)
        hl = rt[:, 2:4].rearrange("p a t e -> p (a t e)").bitcast(F16).rearrange("p (r c) -> p r c", r=2)
        outT = rt[:, 4:6].rearrange("p a t e -> p (a t e)")
        revidx = sb("revidx", [P, E0])
        gst = sb("gst", [P, NT, 64], F16)
        identh = sb("identh", [P, P], F16)
        ARENA = 12032
        arena = sb("arena", [P, ARENA])
        off = [0]

        def part(n):
            off[0] += n
            assert off[0] <= ARENA, off[0]
            return arena[:, off[0] - n:off[0]]

        rawgu = part(U0 * 2 * HID).rearrange("p (u h) -> p u h", u=U0)
        rawdn = part(U0 * C).rearrange("p (u c) -> p u c", u=U0)
        off[0] = 0
        sq, rpA = sg, hT
        rpB = part(2 * CHUNK).rearrange("p (r c) -> p r c", r=2)
        qr = part(4 * CHUNK).rearrange("p (r c) -> p r c", r=4)
        qT = part(2 * HG * SEQ).rearrange("p (g h t) -> p g h t", g=2, h=HG)
        kT = part(2 * HG * SEQ).rearrange("p (g h t) -> p g h t", g=2, h=HG)
        VW = C + 1
        vb = part(2 * TPB * HG * VW).rearrange("p (g t h c) -> p g t h c", g=2, t=TPB, h=HG)
        pt = part(HG * 3 * P).rearrange("p (r c) -> p r c", r=HG)
        qn = lent[:, :].rearrange("p (g u c) -> p g u c", g=2, u=4)
        cosd = part(TPB * HD).rearrange("p (t c) -> p t c", t=TPB)
        sind = part(TPB * HD).rearrange("p (t c) -> p t c", t=TPB)
        ss = sb("ss", [P, 4, HG])
        rms = sb("rms", [P, 4, HG])
        rq = sb("rq", [P, BATCH * NG, 4 * HG])
        rl = sb("rl", [P, 2, TPB])
        off[0] = 0
        selS = part(WS * P // 2).bitcast(F16).rearrange("p (s l) -> p s l", s=WS)
        kwt = part(SG * NT * P // 2).bitcast(F16).rearrange("p (g t) -> p g t", g=SG)
        selW = part(SU * P // 2).bitcast(F16).rearrange("p (s c) -> p s c", s=SU)
        uu = part(UR * CHUNK).rearrange("p (r c) -> p r c", r=UR)
        raww2 = uu.rearrange("p r (u c) -> p (r u) c", c=C)
        kwf = kwt.rearrange("p g t -> p (g t)").bitcast(F32)

        def parts16(region, *sizes):
            at, views = 0, []
            for n in sizes:
                views.append(region[:, at:at + n // 2].bitcast(F16))
                at += n // 2
            assert at <= region.shape[1]
            return views
        oh, oht, h1h, h1l, xnh = parts16(kwf, *[2048] * 5)
        oh = oh.rearrange("p (t e b s) -> p t e b s", t=TPB, e=E1, b=BPC)
        oht = oht.rearrange("p (e t) -> p e t", e=E1)
        h1h, h1l = (v.rearrange("p (r c) -> p r c", c=CHUNK) for v in (h1h, h1l))
        xnl, y1h, y1l = parts16(arena[:, off[0]:ARENA], 2048, 1024, 1024)
        xnh, xnl = (v.rearrange("p (t c) -> p t c", t=NT) for v in (xnh, xnl))
        y1h, y1l = (v.rearrange("p (e c) -> p e c", e=E1) for v in (y1h, y1l))
        selR, upto, ones, slotrow, rankT, taken, takent, gatet, rankt, xgh, xgl = parts16(
            lent[:, :], BATCH // BPC * E1 * P, P, P, TOPK, SEQ, SEQ, TPB * 64, TPB * P, TPB * 64, 1024, 1024)
        selR = selR.rearrange("p (c s) -> p c s", s=P)
        takent, rankt = (v.rearrange("p (t r) -> p t r", t=TPB) for v in (takent, rankt))
        gatet = gatet.rearrange("p (t l b e) -> p t l b e", t=TPB, l=2, b=BATCH)
        xgh, xgl = (v.rearrange("p (e b s) -> p e b s", e=E1, b=BPC) for v in (xgh, xgl))
        y1f = work[:, 2:4, :]
        wsm, prod, sil = work[:, 0:2, :], work[:, 2:4, :], work[:, 4:6, :]
        wacc = [rt[:, k:k + 2].rearrange("p a t e -> p (a t e)") for k in (0, 4)]
        yw = rt[:, 2:4].rearrange("p a t e -> p (a t e)")
        rawkw = sb("rawkw", [P, WK // SU, SU * WH])
        kb = sb("kb", [P, WK // SU])
        wwh = sb("wwh", [P, 2 * WH], F16)
        wwl = sb("wwl", [P, 2 * WH], F16)
        wwr = sb("wwr", [P, 2 * WH])
        wb = sb("wb", [P, 2 * WH])
        ow = sb("ow", [P, C])
        sgrid = sb("sgrid", [P, WS])
        tokpos = sb("tokpos", [P, NT])
        minusj = sb("minusj", [P, 2])
        diffm = sb("diffm", [P, 4, P])
        wdnf = wd16[:, :, :, :].rearrange("p a u c -> p (a u c)").bitcast(F32)
        posT = wdnf[:, 0:NT * P // 2].bitcast(BF16)
        dxs = wdnf[:, NT * P // 2:NT * P // 2 + 2 * BPC * TPB * C].rearrange("p (r b t c) -> p r b t c", r=2, b=BPC, t=TPB)
        guf = guh[:, :, :].rearrange("p a b -> p (a b)")
        kwh = guf[:, 0:SG * P].rearrange("p (g d r) -> p g d r", g=SG, d=2)
        kwl = guf[:, SG * P:2 * SG * P].rearrange("p (g d r) -> p g d r", g=SG, d=2)
        pos = sb("pos", [P, NT, WS])
        xnc = pos[:, :, :].rearrange("p t k -> p (t k)")[:, 0:CHUNK].rearrange("p (t c) -> p t c", t=TPC)
        posr = sb("posr", [P, NT, WS])
        pos16 = sb("pos16", [P, NT, WS], BF16)
        stag = gul[:, :, :].rearrange("p a b -> p (a b)")[:, 0:2 * NT * POSK].bitcast(F32).rearrange("p (t k) -> p t k", t=NT)
        wz = sb("wz", [P, NT, 2, WH])
        wav = sb("wav", [P, 4, NT])
        pT = work[0:64, 2, 0:SEQ]
        pW = work[0:64, 4:6, 0:SEQ]
        pD = work[0:64, 3, 0:SEQ]
        top8 = sb("top8", [64, 8])
        slotcol = sb("slotcol", [P, 1])
        gslot = sb("gslot", [P, E1])

        S = {}

        def s(name):
            if name not in S:
                S[name] = sem(name)
            return S[name]

        block = ctx.enter_context(nc.Block())
        stage_order = a["_stages"]

        def nth(i, per, j=0):
            return i * per + j + 1

        def wait_apart(eng, sem_, value):
            eng.wait_ge(sem_, value)
            eng.sem_inc(s("waited"), 1)

        def matmul3(pe, o, lh, ll, rh, rl_, last=None):
            nc.tensor.matmul(o, ll, rh, start=True, stop=False)
            nc.tensor.matmul(o, lh, rl_, start=False, stop=False)
            return nc.tensor.matmul(o, lh, rh, start=False, stop=True)

        GUP = 3

        @block.sync
        def _(sp):
            def ld(dst, src, name):
                sp.dma_start(dst, src).then_inc(s(name), 16)
            xv = a["L0_attn_x"].rearrange("b (t p) c -> p (b t) c", p=P)
            for c in range(NC):
                ld(x[:, c * TPC:(c + 1) * TPC, :], xv[:, c * TPC:(c + 1) * TPC, :], f"ld_x{c}")
            ld(ident[:, :], a["ident"], "ld_ident")
            ld(rwr[:, :], a["L0_ffn_router_w"], "ld_rw")
            ld(rawgu[:, 0:E0, :], a["L0_ffn_gate_up_w"].rearrange("e c h -> c e h"), "ld_gu")
            ld(rawgu[:, E0:U0, 0:HID], a["L0_ffn_shared_gate_w"].rearrange("c (u h) -> c u h", u=2), "ld_gu")
            ld(rawgu[:, E0:U0, HID:], a["L0_ffn_shared_up_w"].rearrange("c (u h) -> c u h", u=2), "ld_gu")
            ld(sel0[:, :, :], a["sel0"], "ld_sel0")
            ld(rawdn[:, 0:E0, :], a["L0_ffn_down_w"].rearrange("e h c -> h e c"), "ld_dn")
            ld(rawdn[:, E0:U0, :], a["L0_ffn_shared_down_w"].rearrange("(u h) c -> h u c", h=P), "ld_dn")
            ld(rawqk[:, 0, :], a["L0_attn_wq"].rearrange("m h d -> m (h d)"), "ld_qk")
            ld(rawqk[:, 1, :], a["L0_attn_wk"].rearrange("m h d -> m (h d)"), "ld_qk")
            ld(rawvo[:, 0, :], a["L0_attn_wv"].rearrange("d h m -> d (h m)"), "ld_vo")
            ld(rawvo[:, 1, :].rearrange("d (h m) -> d h m", h=NH), a["L0_attn_wo"].rearrange("h d m -> d h m"), "ld_vo")
            ld(cwr[:, :], a["L1_ffn_choice_w"], "ld_cw")
            ld(rawkw[:, :, :], a["L1_attn_kernel_w"], "ld_kw")
            ld(wwr[:, :], a["L1_attn_wave_w"], "ld_ww")
            ld(wb[:, :], a["L1_attn_wave_b"].rearrange("(o w) -> o w", o=1).broadcast_to([P, 2 * WH]), "ld_wb")
            ld(ow[:, :], a["L1_attn_out_w"], "ld_ow")
            ld(sgrid[:, :], a["sgrid"], "ld_sg")
            ld(tokpos[:, :], a["tokpos"], "ld_sg")
            ld(minusj[:, :], a["minusj"], "ld_mj")
            ld(diffm[:, :, :], a["diffm"], "ld_df")
            for d in range(2):
                ld(kb[d * P // 2:(d + 1) * P // 2, :], a["L1_attn_kernel_b"], "ld_kb")
            sp.wait_ge(s("gu_split"), GUP)
            sp.wait_ge(s("dn_split"), 1)
            ld(cosd[:, :, :], a["cosd"], "ld_cos")
            ld(sind[:, :, :], a["sind"], "ld_cos")
            sp.wait_ge(s("qk_split"), NC)
            ld(raww1, a["L1_ffn_w1"].rearrange("e d f -> d e f"), "ld_w1")
            sp.wait_ge(s("at_done"), 1)
            for dst, name in ((selR[0:64, :, :], "selR"), (upto, "upto"), (ones, "ones"), (slotrow, "slotrow"),
                              (slotcol[:, :], "slotcol")):
                ld(dst, a[name], "ld_slots")
            ld(raww2, a["L1_ffn_w2"].rearrange("e (f p) d -> p (e f) d", p=P), "ld_w2")
            ld(selS[0:POSK, :, :], a["selS"], "ld_selS")
            ld(selW, a["selW"], "ld_selS")
            sp.wait_ge(s("x_final"), 1)
            sp.dma_start(out.rearrange("b (t p) c -> p (b t) c", p=P), x[:, :, :]).then_inc(s("stored"), 16)
            sp.wait_ge(s("stored"), 16)

        def chunks_left(puse):
            before = stage_order[puse - 1] if puse else None
            return [(puse * NC + c, c) for c in ([NC - 1] if before in ("F0", "F1", "LA") else range(NC))]

        def tile(v, c, k):
            return v[:, ds(c * TPC + k, 1), :].rearrange("p o c -> p (o c)")

        def slots(c):
            c = c if isinstance(c, int) else 0
            return range(c * TPC, (c + 1) * TPC)

        def statistics(dve, i, c):
            if isinstance(i, int) and i < NC:
                dve.wait_ge(s(f"ld_x{c}"), 16)
            for k, t in enumerate(slots(c)):
                nc.vector.bn_stats(stats[:, t:t + 1, :], x[:, ds(c * TPC + k, 1), :]).then_inc(s("stats"), 1)

        def moments(dve, i, c):
            wait_apart(dve, s("stats"), nth(i, TPC, TPC - 1))
            for t in slots(c):
                last = nc.vector.bn_aggr(mv[:, t, :], stats[:, t, :])
            last.then_inc(s("moments"), 1)

        def keeps(puse):
            return stage_order[puse + 1] in ("LA", "F1")

        def normalise(dve, i, c, dst):
            dve.wait_ge(s("rstd"), nth(i, 1))
            for k, t in enumerate(slots(c)):
                last = nc.vector.tensor_scalar(dst(k), tile(x, c, k), mv[:, t, 0:1], rstd[:, t:t + 1],
                                               ALU.subtract, ALU.mult)
            last.then_inc(s("xn_ready"), 1)

        def low(dve, i, c, b):
            dve.wait_ge(s("xh_ready"), nth(i, 1))
            cs = ds(c * CHUNK, CHUNK)
            nc.vector.tensor_tensor(xTl[:, cs], bank(b), xTh[:, cs], ALU.subtract).then_inc(s("xT_ready"), 1)

        def inverse_deviation(pool, i, c):
            ts = slice(slots(c)[0], slots(c)[-1] + 1)
            wait_apart(pool, s("moments"), nth(i, 1))
            nc.gpsimd.tensor_scalar(rvar[:, ts], mv[:, ts, 1], LN_EPS, None, ALU.add).then_inc(s("rvar"), 1)
            pool.wait_ge(s("rvar"), nth(i, 1))
            nc.gpsimd.tensor_tensor(rstd[:, ts], rvar[:, ts], neghalf[:, 0:TPC], ALU.pow).then_inc(s("rstd"), 1)

        def turn_rows(pe, i, b, src, busy):
            pe.wait_ge(s("xn_ready"), nth(i, 1))
            pe.wait_ge(s("xT_ready"), XT0 + i - busy)
            for k in range(TPC):
                last = nc.tensor.transpose(bank(b)[:, k * P:(k + 1) * P], src(k), ident[:, :])
            last.then_inc(s("tp_ready"), 1)

        def high(act, i, c, b, keep=False):
            act.wait_ge(s("tp_ready"), nth(i, 1))
            if keep:
                nc.scalar.activation(xn[:, ds(c * TPC, TPC), :].rearrange("p t c -> p (t c)"),
                                     xnc[:, :, :].rearrange("p t c -> p (t c)"), ACT.Copy)
            nc.scalar.activation(xTh[:, ds(c * CHUNK, CHUNK)], bank(b), ACT.Copy).then_inc(s("xh_ready"), 1)

        def prep_vector(dve, puse):
            left = chunks_left(puse)
            n = len(left)
            statistics(dve, *left[0])
            for m in range(n + 3):
                if m + 1 < n:
                    statistics(dve, *left[m + 1])
                if m < n:
                    moments(dve, *left[m])
                if 0 <= m - 1 < n:
                    i, c = left[m - 1]
                    normalise(dve, i, c, lambda k: xn[:, c * TPC + k, :])
                if 0 <= m - 3 < n:
                    low(dve, *left[m - 3], 6 + left[m - 3][1] % 2)

        def prep_gpsimd(pool, puse):
            for i, c in chunks_left(puse):
                inverse_deviation(pool, i, c)

        def prep_tensor(pe, puse):
            for i, c in chunks_left(puse):
                turn_rows(pe, i, 6 + c % 2, lambda k: xn[:, c * TPC + k, :], 1)

        def prep_scalar(act, puse):
            for i, c in chunks_left(puse):
                high(act, i, c, 6 + c % 2)

        XT0 = 2

        def all_xT(eng, use):
            eng.wait_ge(s("xT_ready"), XT0 + NC * (use + 1))

        def split_act(act, dst, src, wait, n):
            act.wait_ge(s(wait), n)
            nc.scalar.activation(dst, src, ACT.Copy, scale=WSCALE).then_inc(s("hi_" + wait), 1)

        def split_dve(dve, dst, src, hi, wait, done):
            dve.wait_ge(s("hi_" + wait), 1)
            nc.vector.scalar_tensor_tensor(dst, src, WSCALE, hi, ALU.mult, ALU.subtract).then_inc(s(done), 1)

        def flat(v):
            return v.rearrange("p a b -> p (a b)")

        def route0_tensor(pe, use, puse):
            all_xT(pe, puse)
            if use == 0:
                pe.wait_ge(s("rw_split"), 1)
            for t in range(NT):
                last = matmul3(pe, bank(7)[:, t * E0:(t + 1) * E0], xTh[:, t * P:(t + 1) * P],
                               xTl[:, t * P:(t + 1) * P], rwh[:, :], rwl[:, :])
            last.then_inc(s("logit0"), 1)
            if use == 0:
                pe.wait_ge(s("gu_split"), 1)
            for r in range(2):
                up0(pe, 0, ds(r, 1), r, use * NC * U0 // 2)
            pe.wait_ge(s("identh"), 1)
            pe.wait_ge(s("gate0"), use + 1)
            for c in range(NC):
                for k in range(TPC):
                    last = nc.tensor.matmul(psum[0:64, 4 + c, k * P:(k + 1) * P], gst[:, c * TPC + k, :], identh[:, :],
                                            start=True, stop=True)
                last.then_inc(s("gT0_psum"), 1)

        def route0_scalar(act, use):
            act.wait_ge(s("top2"), use + 1)
            nc.scalar.activation(rs[:, 4:6, :], rs[:, 2:4, :], ACT.Sigmoid, scale=1.0 / WSCALE).then_inc(s("sig2"), 1)
            act.preload_act_table(ACT.Silu)
            if use == 0:
                split_act(act, flat(wd16[:, 0]), flat(rawdn), "ld_dn", 32)
            for c in range(NC):
                act.wait_ge(s("gT0_psum"), nth(use, NC, c))
                nc.scalar.activation(gT0[:, c * CHUNK:(c + 1) * CHUNK], psum[0:64, 4 + c, :],
                                     ACT.Copy).then_inc(s("gT0"), 1)

        def route0_vector(dve, use):
            n = [0]

            def step(ins):
                n[0] += 1
                ins.then_inc(s("route0_step"), 1)
                dve.wait_ge(s("route0_step"), ROUTE0_STEPS * use + n[0])

            def eachtile(v):
                return v.unsqueeze(2).broadcast_to([P, NT, E0])
            L = rt[:, 0]
            dve.wait_ge(s("logit0"), use + 1)
            step(nc.vector.tensor_copy(L, bank(7)[:, 0:NT * E0].rearrange("p (t e) -> p t e", t=NT)))
            for r in range(2):
                m = rs[:, 2 + r, :]
                k = rs[:, r, :]
                key, one = rt[:, 1], rt[:, 2 + r]
                step(nc.vector.tensor_reduce(m, L, AX, ALU.max))
                step(nc.vector.tensor_tensor(key, L, eachtile(m), ALU.is_equal))
                step(nc.vector.tensor_tensor(key, key, revidx[:, :].unsqueeze(1).broadcast_to([P, NT, E0]), ALU.mult))
                step(nc.vector.tensor_reduce(k, key, AX, ALU.max))
                step(nc.vector.tensor_tensor(one, key, eachtile(k), ALU.is_equal))
                if r == 0:
                    step(nc.vector.scalar_tensor_tensor(L, one, -1e30, L, ALU.mult, ALU.add))
            nc.vector.tensor_copy(rs[:, 0, 0:1], rs[:, 2, 0:1]).then_inc(s("top2"), 1)
            dve.wait_ge(s("sig2"), use + 1)
            step(nc.vector.tensor_tensor(rt[:, 4], rt[:, 2], eachtile(rs[:, 4, :]), ALU.mult))
            step(nc.vector.tensor_tensor(rt[:, 5], rt[:, 3], eachtile(rs[:, 5, :]), ALU.mult))
            step(nc.vector.tensor_tensor(rt[:, 1], rt[:, 4], rt[:, 5], ALU.add))
            step(nc.vector.tensor_copy(gst[:, :, 0:E0], rt[:, 1]))
            nc.vector.tensor_tensor(gst[:, :, 32:32 + E0], rt[:, 1], gst[:, :, 0:E0],
                                    ALU.subtract).then_inc(s("gate0"), 1)

        ROUTE0_STEPS = 1 + 6 + 5 + 4

        H0 = 2
        LAG0 = 2
        PREP_AT = 3

        def by_chunk(eng, emit):
            emit(0, True)
            with eng.Fori(1, NC) as c:
                emit(c, False)
            emit(None, False)

        def experts_tensor(pe, n, use, puse, units, lag, up, weigh, down_w):
            def down(u, r, i):
                pe.wait_ge(s(n + "_hl"), H0 + nth(i, 2, r))
                nc.tensor.matmul(bank(6), down_w[:, 0, u, :], hl[:, r, :], start=False, stop=True, skip_group_check=True)
                nc.tensor.matmul(bank(6), down_w[:, 1, u, :], hh[:, r, :], start=False, stop=True, skip_group_check=True)
                nc.tensor.matmul(bank(6), down_w[:, 0, u, :], hh[:, r, :], start=False, stop=True,
                                 skip_group_check=True).then_inc(s(n + "_down"), 1)

            def turn_result(count):
                pe.wait_ge(s(n + "_out"), 1 + count)
                pe.wait_ge(s(n + "_added"), count)
                for k in range(TPC):
                    last = nc.tensor.transpose(bank(7)[:, k * P:(k + 1) * P], outT[:, k * P:(k + 1) * P], ident[:, :])
                last.then_inc(s(n + "_turned"), 1)

            def emit(c, first):
                base = (use * NC + (NC if c is None else c)) * (units // 2)

                def unit(step, pair, slot):
                    if isinstance(pair, int) and pair < 0:
                        step(ds(units + 2 * pair + slot, 1), None, slot, base + pair)
                    else:
                        step(ds(pair * 2 + slot, 1), pair, slot, base + pair)

                def up_(u, pair, slot, i):
                    if not (first and isinstance(pair, int) and pair == 0):
                        up(pe, c, u, slot, i)
                    weigh(c, u, pair, slot, i)

                def down_(u, pair, slot, i):
                    down(u, slot, i)

                def behind_(n):
                    return -((n + 1) // 2), n % 2
                for u in range(lag):
                    if c is not None:
                        unit(up_, u // 2, u % 2)
                    if not first:
                        unit(down_, *behind_(lag - u))
                if c is not None:
                    unit(up_, lag // 2, lag % 2)
                    pe.wait_ge(s(n + "_out"), nth(use * NC + c, 1))
                    nc.tensor.matmul(bank(6), zrow[:, 0:P], zrow[:, :], start=True, stop=False, skip_group_check=True)
                    unit(down_, 0, 0)
                    unit(up_, (lag + 1) // 2, (lag + 1) % 2)
                if not first:
                    turn_result(use * NC + (NC if c is None else c))
                if c is not None:
                    unit(down_, 0, 1)

                    def pairs(k0, k1):
                        with pe.Fori(k0, k1) as k:
                            for r in range(2):
                                unit(up_, k + (lag + r) // 2, (lag + r) % 2)
                                unit(down_, k, r)
                    end = units // 2 - (lag + 1) // 2
                    if not first and puse + 1 < len(stage_order):
                        pairs(1, PREP_AT + 1)
                        turn_rows(pe, (puse + 1) * NC + c - 1, 7, lambda k: xnc[:, k, :], 0)
                        pairs(PREP_AT + 1, end)
                    else:
                        pairs(1, end)
                    if lag % 2:
                        unit(up_, units // 2 - 1, 1)
                        unit(down_, end, 0)
            by_chunk(pe, emit)

        def experts_scalar(act, n, use, puse, units, lag, sg_read, side):
            def silu(r, i):
                act.wait_ge(s(n + "_g"), nth(i, 2, r))
                act.wait_ge(s(sg_read), nth(i, 2, r))
                nc.scalar.activation(sg[:, r, :], bank(r), ACT.Silu, scale=1.0 / WSCALE).then_inc(s(n + "_sg"), 1)

            def high_part(r, i):
                act.wait_ge(s(n + "_hT"), H0 + nth(i, 2, r))
                act.wait_ge(s(n + "_down"), nth(i, 2, r))
                nc.scalar.activation(hh[:, r, :], hT[:, r, :], ACT.Copy).then_inc(s(n + "_hh"), 1)

            def emit(c, first):
                base = (use * NC + (NC if c is None else c)) * (units // 2)
                count = use * NC + (NC if c is None else c)
                def copy_result():
                    act.wait_ge(s(n + "_down"), H0 + count * units)
                    act.wait_ge(s(n + "_turned"), count)
                    nc.scalar.activation(outT, bank(6), ACT.Copy).then_inc(s(n + "_out"), 1)
                if c is None:
                    high_part(1, base - 1)
                    copy_result()
                else:
                    for u in range(4):
                        silu(u % 2, base + u // 2)
                        if u == 2 and lag == 3 and not first:
                            copy_result()
                        if u or not first:
                            high_part((u - 1) % 2, base + (u - 1) // 2)
                        if u == 1 and lag == 2 and not first:
                            copy_result()

                    def pairs(k0, k1):
                        with act.Fori(k0, k1) as k:
                            silu(0, base + k)
                            high_part(1, base + k - 1)
                            silu(1, base + k)
                            high_part(0, base + k)
                    pairs(2, PREP_AT + 2)
                    if not first and puse + 1 < len(stage_order):
                        high(act, (puse + 1) * NC + c - 1, c - 1, 7, keeps(puse))
                    pairs(PREP_AT + 2, units // 2 - 1)
                    side(c)
                    pairs(units // 2 - 1, units // 2)
            by_chunk(act, emit)

        def experts_vector(dve, n, use, puse, units, hidden):
            def emit(c, first):
                base = (use * NC + (NC if c is None else c)) * (units // 2)
                if c is not None:
                    for k in range(2):
                        for r in range(2):
                            hidden(r, base + k)
                if not first:
                    count = use * NC + (NC if c is None else c)
                    dve.wait_ge(s(n + "_turned"), 1 + count)
                    xc = x[:, ds(((NC if c is None else c) - 1) * TPC, TPC), :].rearrange("p t c -> p (t c)")
                    nc.vector.scalar_tensor_tensor(xc, bank(7), HALF / WSCALE, xc, ALU.mult, ALU.add).then_inc(s(n + "_added"), 1)
                if c is not None:
                    def pairs(k0, k1):
                        with dve.Fori(k0, k1) as k:
                            for r in range(2):
                                hidden(r, base + k)
                    if not first and puse + 1 < len(stage_order):
                        i = (puse + 1) * NC + c - 1
                        wait_apart(dve, s(n + "_added"), 1 + use * NC + c)
                        statistics(dve, i, c - 1)
                        hidden(0, base + 2)
                        moments(dve, i, c - 1)
                        hidden(1, base + 2)
                        normalise(dve, i, c - 1, lambda k: xnc[:, k, :])
                        pairs(3, PREP_AT + 3)
                        low(dve, i, c - 1, 7)
                        pairs(PREP_AT + 3, units // 2)
                    else:
                        pairs(2, units // 2)
            by_chunk(dve, emit)
            dve.wait_ge(s(n + "_added"), 1 + NC * (use + 1))

        def experts_gpsimd(pool, n, use, puse, units, side):
            def emit(c, first):
                def pairs(k0, k1):
                    with pool.Fori(k0, k1) as k:
                        for r in range(2):
                            pool.wait_ge(s(n + "_hh"), nth((use * NC + c) * (units // 2) + k, 2, r))
                            nc.gpsimd.tensor_tensor(hl[:, r, :], hT[:, r, :], hh[:, r, :], ALU.subtract).then_inc(s(n + "_hl"), 1)
                if c is None:
                    return
                pairs(0, 2)
                if not first and puse + 1 < len(stage_order):
                    inverse_deviation(pool, (puse + 1) * NC + c - 1, c - 1)
                pairs(2, units // 2 - 1)
                side(c)
                pairs(units // 2 - 1, units // 2)
            by_chunk(pool, emit)

        def pieces(use, n):
            if n == "F0" and use == 0:
                return [(flat(rawqk[:, :, :]), flat(qkh[:, :, :]), flat(qkl[:, :, :]), "qk", 32)]
            if n == "F0" and use == 1:
                return [(flat(raww1), flat(w1h[:, :, :]), flat(w1l[:, :, :]), "w1", 16),
                        (flat(raww2), flat(w216[:, 0]), flat(w216[:, 1]), "w2", 16)]
            return []

        def scale_pieces(act, use, n):
            def side(c):
                cs = ds(c * CHUNK, CHUNK)
                for raw, hi, lo, name, loads in pieces(use, n):
                    if isinstance(c, int):
                        act.wait_ge(s("ld_" + name), loads)
                    nc.scalar.activation(hi[:, cs], raw[:, cs], ACT.Copy, scale=WSCALE)
                    nc.scalar.activation(raw[:, cs], raw[:, cs], ACT.Copy, scale=WSCALE).then_inc(s("hi_" + name), 1)
            return side

        def low_pieces(pool, use, n):
            def side(c):
                cs = ds(c * CHUNK, CHUNK)
                for raw, hi, lo, name, loads in pieces(use, n):
                    pool.wait_ge(s("hi_" + name), nth(c, 1))
                    nc.gpsimd.tensor_tensor(lo[:, cs], raw[:, cs], hi[:, cs], ALU.subtract).then_inc(s(name + "_split"), 1)
            return side

        def up0(pe, c, u, r, i):
            cs = ds(c * CHUNK, CHUNK)
            pe.wait_ge(s("f0_hT"), nth(i, 2, r))
            for half_, b in ((0, 0), (1, 2)):
                ws = ds(half_ * HID, HID)
                last = matmul3(pe, bank(b + r), guh[:, u, ws], gul[:, u, ws], xTh[:, cs], xTl[:, cs])
                if half_ == 0:
                    last.then_inc(s("f0_g"), 1)

        def ffn0_tensor(pe, use, puse):
            if use == 0:
                pe.wait_ge(s("gu_split"), GUP)
                pe.wait_ge(s("ld_sel0"), 16)
                pe.wait_ge(s("dn_split"), 1)
            pe.wait_ge(s("gT0"), NC * (use + 1))

            def weigh(c, u, pair, r, i):
                nc.tensor.matmul(bank(4 + r), sel0[:, u, :], gT0[:, ds(c * CHUNK, CHUNK)], start=True,
                                 stop=True).then_inc(s("f0_u"), 1)
            experts_tensor(pe, "f0", use, puse, U0, LAG0, up0, weigh, wd16)

        def ffn0_scalar(act, use, puse):
            experts_scalar(act, "f0", use, puse, U0, LAG0, "f0_su", scale_pieces(act, use, "F0"))

        def ffn0_vector(dve, use, puse):
            def hidden(r, i):
                dve.wait_ge(s("f0_sg"), nth(i, 2, r))
                dve.wait_ge(s("f0_u"), nth(i, 2, r))
                nc.vector.tensor_tensor(su[:, r, :], sg[:, r, :], bank(2 + r), ALU.mult).then_inc(s("f0_su"), 1)
                dve.wait_ge(s("f0_su"), H0 + nth(i, 2, r))
                dve.wait_ge(s("f0_hl"), nth(i, 2, r))
                nc.vector.tensor_tensor(hT[:, r, :], su[:, r, :], bank(4 + r), ALU.mult).then_inc(s("f0_hT"), 1)
            experts_vector(dve, "f0", use, puse, U0, hidden)

        QKU = 2 * TPB
        AT_ROUNDS = BATCH * NG
        R0 = 2 * QKU

        def at_loop(eng, emit):
            def rd(b, k):
                return (b + k // NG, k % NG, b * NG + k)
            emit(None, None, None, rd(0, 0))
            emit(None, None, rd(0, 0), rd(0, 1))
            emit(None, rd(0, 0), rd(0, 1), rd(0, 2))
            with eng.Fori(0, BATCH - 2) as b:
                for k in range(NG):
                    emit(rd(b, k), rd(b, k + 1), rd(b, k + 2), rd(b, k + 3))
            b = BATCH - 2
            emit(rd(b, 0), rd(b, 1), rd(b, 2), rd(b, 3))
            emit(rd(b, 1), rd(b, 2), rd(b, 3), None)
            emit(rd(b, 2), rd(b, 3), None, None)
            emit(rd(b, 3), None, None, None)

        def behind(last, core, h):
            rnd, hh = (last, h + 2) if h < 2 else (core, h - 2)
            return (rnd, hh) if rnd else None

        def rotation(turn_, proj_, h):
            rnd, u = (turn_, h + 1) if h < HG - 1 else (proj_, 0)
            return (rnd, u) if rnd else None

        def at_tensor(pe, puse):
            pe.wait_ge(s("ld_vo"), 32)
            for h in range(NH):
                hs = slice(h * HD, (h + 1) * HD)
                last = nc.tensor.matmul(psum[:, h // HG, (h % HG) * C:(h % HG + 1) * C], rawvo[:, 0, hs],
                                        rawvo[:, 1, hs], start=True, stop=True)
            last.then_inc(s("vo_psum"), 1)
            prep_tensor(pe, puse)
            all_xT(pe, puse)
            pe.wait_ge(s("qk_split"), NC)
            pe.wait_ge(s("vo_split"), 1)

            def emit(last_, core, turn_, proj_):
                def project(u):
                    b, g, j = proj_
                    pe.wait_ge(s("qn_ready"), nth(j, QKU, u))
                    tok = ds(b * SEQ + (u // 2) * P, P)
                    cols = slice(g * CHUNK, (g + 1) * CHUNK)
                    matmul3(pe, bank(u % 2), xTh[:, tok], xTl[:, tok], qkh[:, u % 2, cols],
                            qkl[:, u % 2, cols]).then_inc(s("pj_ready"), 1)

                def project_v(t):
                    b, g, j = turn_
                    pe.wait_ge(s("vb_ready"), nth(j, TPB, t))
                    tok = ds(b * SEQ + t * P, P)
                    cols = slice(g * CHUNK, (g + 1) * CHUNK)
                    matmul3(pe, bank(2), xTh[:, tok], xTl[:, tok], voh[:, cols], vol[:, cols]).then_inc(s("v_ready"), 1)

                def turn(u):
                    j = turn_[2]
                    pe.wait_ge(s("rot_ready"), R0 + nth(j, QKU, u))
                    pe.wait_ge(s("qkT_ready"), nth(j, QKU, u))
                    for h in range(HG):
                        last = nc.tensor.transpose(bank(3)[:, h * P:(h + 1) * P], qr[:, u, h * HD:(h + 1) * HD], ident[:, :])
                    last.then_inc(s("tr_ready"), 1)

                def scores(h):
                    b, g, i = core
                    pe.wait_ge(s("qkT_ready"), 1 + nth(i, QKU, QKU - 1))
                    pe.wait_ge(s("exp_ready"), nth(i, HG, h))
                    nc.tensor.matmul(bank(4 + h % 2)[:, 0:SEQ], kT[:, g, h, 0:P], qT[:, g, h, :], start=True, stop=True)
                    nc.tensor.matmul(bank(4 + h % 2)[:, SEQ:SEQ + P], kT[:, g, h, P:SEQ], qT[:, g, h, P:SEQ],
                                     start=True, stop=True).then_inc(s("sc_ready"), 1)

                def values(due):
                    (b, g, i), h = due
                    pe.wait_ge(s("mask_ready"), nth(i, HG, h))
                    pe.wait_ge(s("vb_ready"), 1 + nth(i, TPB, TPB - 1))
                    pe.wait_ge(s("pv_taken"), nth(i, HG, h))
                    o = bank(6 + h % 2)
                    nc.tensor.matmul(o[:, 0:VW], pt[:, h, 0:P], vb[:, g, 0, h, :], start=True, stop=True)
                    nc.tensor.matmul(o[:, SEQ:SEQ + VW], pt[:, h, P:SEQ], vb[:, g, 0, h, :], start=True, stop=False)
                    nc.tensor.matmul(o[:, SEQ:SEQ + VW], pt[:, h, SEQ:SEQ + P], vb[:, g, 1, h, :],
                                     start=False, stop=True).then_inc(s("pv_ready"), 1)
                for h in range(HG):
                    if proj_:
                        project(h)
                    if turn_ and h % 2 == 1:
                        project_v(h // 2)
                    if core:
                        scores(h)
                    if behind(last_, core, h):
                        values(behind(last_, core, h))
                    if turn_:
                        turn(h)
            at_loop(pe, emit)

        def at_scalar(act, puse):
            act.wait_ge(s("vo_psum"), 1)
            nc.scalar.activation(voh[:, :], psum[:, 0:2, :].rearrange("p a b -> p (a b)"), ACT.Copy,
                                 scale=WSCALE).then_inc(s("hi_vo"), 1)
            prep_scalar(act, puse)
            act.preload_act_table(ACT.Exp)
            act.wait_ge(s("vb_ones"), 1)

            def emit(last_, core, turn_, proj_):
                def exps(h):
                    b, g, i = core
                    act.wait_ge(s("sc_ready"), nth(i, HG, h))
                    act.wait_ge(s("pv_ready"), nth(i, HG, h))
                    act.wait_ge(s("rq_ready"), nth(i, TPB, TPB - 1))
                    nc.scalar.activation(pt[:, h, 0:SEQ], bank(4 + h % 2)[:, 0:SEQ], ACT.Exp,
                                         scale=rq[:, ds(i, 1), HG + h])
                    nc.scalar.activation(pt[:, h, SEQ:SEQ + P], bank(4 + h % 2)[:, SEQ:SEQ + P], ACT.Exp,
                                         scale=rq[:, ds(i, 1), 3 * HG + h]).then_inc(s("exp_ready"), 1)

                def squares(u):
                    j = proj_[2]
                    act.wait_ge(s("pj_ready"), nth(j, QKU, u))
                    act.wait_ge(s("ss_ready"), nth(j, QKU, u))
                    nc.scalar.activation(sq[:, u % 2, :], bank(u % 2), ACT.Square).then_inc(s("sq_ready"), 1)

                def copy_out(u):
                    b, g, j = proj_
                    act.wait_ge(s("rot_ready"), nth(j, QKU, u))
                    nc.scalar.activation(qn[:, g, u, :], bank(u % 2), ACT.Copy).then_inc(s("qn_ready"), 1)

                def scale_q(rnd, t):
                    b, g, j = rnd
                    act.wait_ge(s("qn_ready"), 2 + nth(j, QKU, 2 * t))
                    act.wait_ge(s("rq_ready"), nth(j, TPB, t))
                    for h in range(HG):
                        hs = slice(h * HD, (h + 1) * HD)
                        last = nc.scalar.activation(qn[:, g, 2 * t, hs], qn[:, g, 2 * t, hs], ACT.Copy,
                                                    scale=rq[:, ds(j, 1), 2 * t * HG + h])
                    last.then_inc(s("qs_ready"), 1)

                def turned(u):
                    b, g, j = turn_
                    act.wait_ge(s("tr_ready"), QKU + nth(j, QKU, u))
                    dst = (qT, kT)[u % 2][:, g, :, (u // 2) * P:(u // 2 + 1) * P]
                    nc.scalar.activation(dst, bank(3).rearrange("p (h t) -> p h t", h=HG),
                                         ACT.Copy).then_inc(s("qkT_ready"), 1)

                def values_out(t):
                    b, g, j = turn_
                    act.wait_ge(s("v_ready"), nth(j, TPB, t))
                    if last_:
                        act.wait_ge(s("pv_ready"), HG + nth(last_[2], HG, HG - 1))
                    nc.scalar.activation(vb[:, g, t, :, 0:C], bank(2).rearrange("p (h c) -> p h c", h=HG),
                                         ACT.Copy).then_inc(s("vb_ready"), 1)
                for h in range(HG):
                    if proj_:
                        squares(h)
                        copy_out(h)
                    if core:
                        exps(h)
                    if turn_ and h >= 2:
                        values_out(h - 2)
                    if turn_:
                        turned(h)
                    if turn_ and h == 0:
                        scale_q(turn_, 1)
                    if proj_ and h == 2:
                        scale_q(proj_, 0)
            at_loop(act, emit)

        def at_vector(dve, puse):
            prep_vector(dve, puse)
            dve.wait_ge(s("hi_vo"), 1)
            nc.vector.scalar_tensor_tensor(vol[:, :], psum[:, 0:2, :].rearrange("p a b -> p (a b)"), WSCALE, voh[:, :],
                                           ALU.mult, ALU.subtract).then_inc(s("vo_split"), 1)
            dve.wait_ge(s("ld_cos"), 32)
            nc.vector.memset(vb[:, :, :, :, C:VW].rearrange("p g t h c -> p (g t h) c"), WSCALE).then_inc(s("vb_ones"), 1)

            def emit(last_, core, turn_, proj_):
                def sums(u):
                    j = proj_[2]
                    dve.wait_ge(s("rms_ready"), nth(j, TPB, u // 2))
                    dve.wait_ge(s("sq_ready"), nth(j, QKU, u))
                    nc.vector.tensor_reduce(ss[:, u, :], sq[:, u % 2, :].rearrange("p (h d) -> p h d", h=HG), AX,
                                            ALU.add).then_inc(s("ss_ready"), 1)

                def cosines(rnd, u):
                    b, g, j = rnd
                    if u % 2 == 0:
                        dve.wait_ge(s("qs_ready"), nth(j, TPB, u // 2))
                    else:
                        dve.wait_ge(s("qn_ready"), 2 + nth(j, QKU, u))
                    dve.wait_ge(s("rot_ready"), R0 - 2 + nth(j, QKU, u))
                    cs = cosd[:, u // 2, :].unsqueeze(1).broadcast_to([P, HG, HD])
                    nc.vector.tensor_tensor(rpA[:, u % 2, :].rearrange("p (h d) -> p h d", h=HG),
                                            qn[:, g, u, :].rearrange("p (h d) -> p h d", h=HG), cs,
                                            ALU.mult).then_inc(s("cos_ready"), 1)

                def rotated(rnd, u):
                    b, g, j = rnd
                    dve.wait_ge(s("cos_ready"), nth(j, QKU, u))
                    dve.wait_ge(s("sin_ready"), nth(j, QKU, u))
                    dve.wait_ge(s("tr_ready"), nth(j, QKU, u))
                    nc.vector.tensor_tensor(qr[:, u, :], rpA[:, u % 2, :], rpB[:, u % 2, :],
                                            ALU.add).then_inc(s("rot_ready"), 1)

                def add_values(due):
                    (b, g, i), h = due
                    o = bank(6 + h % 2)
                    dve.wait_ge(s("pv_ready"), HG + nth(i, HG, h))
                    nc.vector.reciprocal(rl[:, h % 2, :], o.rearrange("p (t c) -> p t c", t=TPB)[:, :, C]).then_inc(s("rl_ready"), 1)
                    dve.wait_ge(s("rl_ready"), nth(i, HG, h))
                    dve.wait_ge(s("pv_taken"), 1 + nth(i, HG, h))
                    for t in range(TPB):
                        xt = x[:, ds(b * TPB + t, 1), :].rearrange("p o c -> p (o c)")
                        last = nc.vector.scalar_tensor_tensor(xt, o[:, t * SEQ:t * SEQ + C], rl[:, h % 2, t:t + 1], xt,
                                                              ALU.mult, ALU.add)
                    last.then_inc(s("pv_taken"), 1)
                for h in range(HG):
                    if rotation(turn_, proj_, h):
                        cosines(*rotation(turn_, proj_, h))
                    if proj_:
                        sums(h)
                    if behind(last_, core, h):
                        add_values(behind(last_, core, h))
                    if rotation(turn_, proj_, h):
                        rotated(*rotation(turn_, proj_, h))
            at_loop(dve, emit)
            dve.wait_ge(s("pv_taken"), 2 + AT_ROUNDS * HG)
            dve.sem_inc(s("at_done"), 1)

        def at_gpsimd(pool, puse):
            prep_gpsimd(pool, puse)

            def emit(last_, core, turn_, proj_):
                def scale(rnd, t):
                    b, g, j = rnd
                    wait_apart(pool, s("ss_ready"), 2 + nth(j, QKU, 2 * t + 1))
                    nc.gpsimd.tensor_scalar(rms[:, 2 * t:2 * t + 2, :], ss[:, 2 * t:2 * t + 2, :], RMS_EPS * HD * WSCALE ** 2,
                                            None, ALU.add).then_inc(s("rms_ready"), 1)
                    pool.wait_ge(s("rms_ready"), TPB + nth(j, TPB, t))
                    nc.gpsimd.tensor_tensor(rq[:, ds(j, 1), 2 * t * HG:(2 * t + 2) * HG],
                                            rms[:, 2 * t:2 * t + 2, :].rearrange("p u h -> p (u h)"), neghalf[:, 0:2 * HG],
                                            ALU.pow).then_inc(s("rq_ready"), 1)

                def sines(rnd, u):
                    b, g, j = rnd
                    if u % 2 == 0:
                        pool.wait_ge(s("qs_ready"), nth(j, TPB, u // 2))
                    else:
                        pool.wait_ge(s("qn_ready"), 2 + nth(j, QKU, u))
                    pool.wait_ge(s("rot_ready"), R0 - 2 + nth(j, QKU, u))
                    sn = sind[:, u // 2, :].unsqueeze(1).broadcast_to([P, HG, HD])
                    half = HD // 2
                    for k in range(2):
                        last = nc.gpsimd.tensor_tensor(
                            rpB[:, u % 2, :].rearrange("p (h d) -> p h d", h=HG)[:, :, k * half:(k + 1) * half],
                            qn[:, g, u, :].rearrange("p (h d) -> p h d", h=HG)[:, :, (1 - k) * half:(2 - k) * half],
                            sn[:, :, k * half:(k + 1) * half], ALU.mult)
                    last.then_inc(s("sin_ready"), 1)

                def mask(h):
                    b, g, i = core
                    wait_apart(pool, s("exp_ready"), 2 + nth(i, HG, h))
                    v = pt[:, h, :].rearrange("p (n t) -> p n t", t=P)[:, 0:3:2, :]
                    nc.gpsimd.affine_select(out=v, in_=v, compare_op=ALU.is_ge, fill=0.0, base=0,
                                            pattern=[[0, 2], [1, P]], channel_multiplier=-1).then_inc(s("mask_ready"), 1)
                for h in range(HG):
                    if proj_ and h == 2:
                        scale(proj_, 0)
                    if turn_ and h == 0:
                        scale(turn_, 1)
                    if rotation(turn_, proj_, h):
                        sines(*rotation(turn_, proj_, h))
                    if core:
                        mask(h)
            at_loop(pool, emit)

        probs = rt[:, 1].rearrange("p t e -> p (t e)")[:, 0:NT * E1]

        def route1_tensor(pe, use, puse):
            all_xT(pe, puse)
            if use == 0:
                pe.wait_ge(s("cw_split"), 1)
            for t in range(NT):
                last = matmul3(pe, bank(7)[:, t * E1:(t + 1) * E1], xTh[:, t * P:(t + 1) * P],
                               xTl[:, t * P:(t + 1) * P], cwh[:, :], cwl[:, :])
            last.then_inc(s("logit1"), 1)
            pe.wait_ge(s("prob1"), use + 1)
            for t in range(TPB):
                last = nc.tensor.transpose(psum[0:64, 6, t * P:(t + 1) * P], probs[:, t * 64:(t + 1) * 64], ident[:, :])
            last.then_inc(s("probT"), 1)

        def route1_scalar(act, use, puse):
            act.wait_ge(s("shift1"), use + 1)
            v = rt[:, 0].rearrange("p t e -> p (t e)")[:, 0:NT * E1]
            nc.scalar.activation(v, v, ACT.Exp, scale=1.0 / WSCALE).then_inc(s("exp1"), 1)
            act.preload_act_table(ACT.Silu)
            for c in range(NC):
                ts = slice(c * TPC, (c + 1) * TPC)
                act.wait_ge(s("xn_ready"), nth((puse + 1) * NC - 1, 1))
                nc.scalar.activation(xnh[:, ts, :], xn[:, ts, :], ACT.Copy).then_inc(s("xnh_ready"), 1)

        ROUTE1_STEPS = 1 + 3 + 1 + 16 + 3

        def route1_vector(dve, use):
            n = [0]

            def step(ins):
                n[0] += 1
                ins.then_inc(s("route1_step"), 1)
                dve.wait_ge(s("route1_step"), ROUTE1_STEPS * use + n[0])

            def tiles(v):
                return v.rearrange("p t e -> p (t e)")[:, 0:NT * E1].rearrange("p (t e) -> p t e", e=E1)

            def eachtile(v):
                return v.unsqueeze(2).broadcast_to([P, NT, E1])
            L = bank(7)[:, 0:NT * E1].rearrange("p (t e) -> p t e", t=NT)
            dve.wait_ge(s("logit1"), use + 1)
            step(nc.vector.tensor_reduce(rs[:, 0, :], L, AX, ALU.max))
            nc.vector.tensor_tensor(tiles(rt[:, 0]), L, eachtile(rs[:, 0, :]), ALU.subtract).then_inc(s("shift1"), 1)
            dve.wait_ge(s("exp1"), use + 1)
            step(nc.vector.tensor_reduce(rs[:, 1, :], tiles(rt[:, 0]), AX, ALU.add))
            step(nc.vector.reciprocal(rs[:, 2, :], rs[:, 1, :]))
            nc.vector.tensor_tensor(probs.rearrange("p (t b e) -> p b t e", t=TPB, b=BATCH),
                                    tiles(rt[:, 0]).rearrange("p (b t) e -> p b t e", t=TPB),
                                    eachtile(rs[:, 2, :]).rearrange("p (b t) e -> p b t e", t=TPB),
                                    ALU.mult).then_inc(s("prob1"), 1)
            dve.wait_ge(s("probT"), use + 1)
            step(nc.vector.tensor_copy(pT, psum[0:64, 6, 0:SEQ]))
            for k in range(TOPK // 8):
                src = pT if k == 0 else pW[:, (k - 1) % 2]
                step(nc.vector.max(top8[:, :], src))
                step(nc.vector.match_replace(pW[:, k % 2], top8[:, :], src, 0.0))
            step(nc.vector.tensor_tensor(pD, pT, pW[:, (TOPK // 8 - 1) % 2], ALU.subtract))
            step(nc.vector.tensor_scalar(taken[0:64, :], pD, 0.0, None, ALU.is_gt))
            step(nc.vector.tensor_copy(gT1[0:64, :], pD))
            step(nc.vector.tensor_tensor(pD, pD, gT1[0:64, :], ALU.subtract))
            nc.vector.tensor_copy(gT1[64:128, :], pD).then_inc(s("gate1"), 1)

        EP = E1 // 2
        SCB = (3, 7)
        RKB = (5, 6)

        def by_chunk1(eng, emit):
            emit(0, True, False)
            with eng.Fori(1, NC - 1) as c:
                emit(c, False, False)
            emit(NC - 1, False, True)

        def ffn1_tensor(pe, use, puse):
            n0 = use * NC
            if use == 0:
                pe.wait_ge(s("w1_split"), NC)
                pe.wait_ge(s("w2_split"), NC)
                pe.wait_ge(s("ld_slots"), 16 * 5)
            pe.wait_ge(s("gate1"), use + 1)
            for t in range(TPB):
                ts = slice(t * P, (t + 1) * P)
                nc.tensor.matmul(bank(6)[:, t * 64:(t + 1) * 64], taken[0:64, ts], identh[0:64, 0:64], start=True, stop=True)
                last = nc.tensor.matmul(bank(5)[:, ts], gT1[:, ts], identh[:, :], start=True, stop=True)
            last.then_inc(s("taken_psum"), 1)
            pe.wait_ge(s("taken_copied"), 2 * use + 2)
            nc.tensor.matmul(bank(4)[:, 0:64], upto, takent[:, 0, :], start=True, stop=True)
            nc.tensor.matmul(bank(4)[:, 64:128], ones, takent[:, 0, :], start=True, stop=False)
            nc.tensor.matmul(bank(4)[:, 64:128], upto, takent[:, 1, :], start=False, stop=True)
            nc.tensor.matmul(psum[0:64, 3, 0:P], takent[:, 0, :], upto, start=True, stop=True)
            nc.tensor.matmul(psum[0:64, 3, P:SEQ], takent[:, 0, :], ones, start=True, stop=False)
            nc.tensor.matmul(psum[0:64, 3, P:SEQ], takent[:, 1, :], upto, start=False, stop=True).then_inc(s("rank_psum"), 1)
            pe.wait_ge(s("xnl_ready"), NC * (use + 1))

            def gather(c):
                n = n0 + c
                pe.wait_ge(s("oh_ready"), nth(n, BPC, BPC - 1))
                pe.wait_ge(s("xg_ready"), nth(n, BPC, BPC - 1))
                for b in range(BPC):
                    for t in range(TPB):
                        for part_ in (xnl, xnh):
                            last = nc.tensor.matmul(
                                bank(4 + b).rearrange("p (e s) -> p e s", e=E1),
                                part_[:, ds(c * TPC + b * TPB + t, 1), :].rearrange("p o c -> p (o c)"), oh[:, t, :, b, :],
                                start=(t == 0 and part_ is xnl), stop=(t == TPB - 1 and part_ is xnh))
                    last.then_inc(s("gathered"), 1)

            def gates(c):
                pe.wait_ge(s("b6_read"), 1 + nth(n0 + c, EP + 1))
                for e in range(E1):
                    for t in range(TPB):
                        last = nc.tensor.matmul(bank(6)[:, e * 4:(e + 1) * 4].rearrange("p (l b) -> p l b", l=2),
                                                oh[:, t, e, :, :].rearrange("p b s -> p (b s)"),
                                                gatet[:, t, :, ds(c * BPC, BPC), e], start=(t == 0), stop=(t == TPB - 1))
                last.then_inc(s("gates_psum"), 1)

            def up(c, p):
                pe.wait_ge(s("xg_ready"), BPC + nth(n0 + c, BPC, BPC - 1))
                pe.wait_ge(s("silu_ready"), nth(n0 + c, EP, p))
                for k in range(4):
                    e, f = 2 * p + k // 2, k % 2
                    fs = slice(f * P, (f + 1) * P)
                    xh, xl = (v[:, e, :, :].rearrange("p b s -> p (b s)") for v in (xgh, xgl))
                    last = matmul3(pe, bank(p % 2)[:, k * P:(k + 1) * P], w1h[:, e, fs], w1l[:, e, fs], xh, xl)
                last.then_inc(s("f1_up"), 1)

            def ranks(c, p):
                pe.wait_ge(s("b6_read"), nth(n0 + c, EP + 1, 1 + p))
                for k in range(2):
                    last = nc.tensor.matmul(bank(RKB[p % 2])[:, k * SEQ:(k + 1) * SEQ],
                                            selR[0:64, ds(c * E1 + 2 * p + k, 1), :].rearrange("p o s -> p (o s)"),
                                            rankT[0:64, :], start=True, stop=True)
                last.then_inc(s("ranks_psum"), 1)

            def down(c, q):
                pe.wait_ge(s("f1_hl"), 2 + nth(n0 + c, EP, 2 * q + 1))
                pe.wait_ge(s("y1_ready"), nth(n0 + c, 2, q))
                for k in range(4):
                    e = 4 * q + k
                    for f in range(F1):
                        hs = slice(((e % 2) * 2 + f) * P, ((e % 2) * 2 + f + 1) * P)
                        o = bank(2)[:, k * P:(k + 1) * P]
                        nc.tensor.matmul(o, h1l[:, e // 2, hs], w216[:, 0, e * F1 + f, :], start=(f == 0), stop=False)
                        nc.tensor.matmul(o, h1h[:, e // 2, hs], w216[:, 1, e * F1 + f, :], start=False, stop=False)
                        last = nc.tensor.matmul(o, h1h[:, e // 2, hs], w216[:, 0, e * F1 + f, :], start=False,
                                                stop=(f == F1 - 1))
                last.then_inc(s("f1_down"), 1)

            def scatter(c):
                pe.wait_ge(s("y1l_ready"), 2 + nth(n0 + c, 2, 1))
                pe.wait_ge(s("b6_read"), 2 + nth(n0 + c, EP + 1, EP))
                pe.wait_ge(s("f1_added"), nth(n0 + c, 1))
                if puse + 1 < len(stage_order):
                    pe.wait_ge(s("xT_ready"), XT0 + (puse + 1) * NC + c)
                for t in range(TPB):
                    for e in range(E1):
                        for part_ in (y1l, y1h):
                            for b in range(BPC):
                                rows = slice(b * TOPK, (b + 1) * TOPK)
                                last = nc.tensor.matmul(bank(SCB[b])[:, t * C:(t + 1) * C],
                                                        oht[rows, e, t * P:(t + 1) * P], part_[rows, e, :],
                                                        start=(e == 0 and part_ is y1l), stop=(e == E1 - 1 and part_ is y1h))
                last.then_inc(s("scattered"), 1)
            gather(0)
            gates(0)

            def emit(c, first, last_):
                job = not first and puse + 1 < len(stage_order)
                i = (puse + 1) * NC + c - 1
                up(c, 0)
                up(c, 1)
                up(c, 2)
                ranks(c, 0)
                if not first:
                    scatter(c - 1)
                up(c, 3)
                ranks(c, 1)
                down(c, 0)
                ranks(c, 2)
                ranks(c, 3)
                down(c, 1)
                if not last_:
                    pe.wait_ge(s("b6_read"), 2 + nth(n0 + c, EP + 1, EP))
                    gather(c + 1)
                    gates(c + 1)
                if job:
                    turn_rows(pe, i, 7, lambda k: xnc[:, k, :], 0)
            by_chunk1(pe, emit)
            scatter(NC - 1)

        def ffn1_scalar(act, use, puse):
            n0 = use * NC
            act.wait_ge(s("taken_psum"), use + 1)
            nc.scalar.activation(takent.rearrange("p t r -> p (t r)"), bank(6)[:, 0:P], ACT.Copy).then_inc(s("taken_copied"), 1)
            nc.scalar.activation(gatet.rearrange("p t l b e -> p (t l b e)"), bank(5)[:, 0:SEQ],
                                 ACT.Copy).then_inc(s("taken_copied"), 1)

            def high_gathered(c):
                for b in range(BPC):
                    act.wait_ge(s("gathered"), nth(n0 + c, BPC, b))
                    nc.scalar.activation(xgh[:, :, b, :], bank(4 + b).rearrange("p (e s) -> p e s", e=E1),
                                         ACT.Copy).then_inc(s("xgh_ready"), 1)

            def silu(c, p):
                act.wait_ge(s("f1_up"), nth(n0 + c, EP, p))
                act.wait_ge(s("f1_down"), nth(n0 + c, 2, p // 2))
                nc.scalar.activation(h1h[:, p, :], bank(p % 2), ACT.Silu, scale=1.0 / WSCALE)
                act.wait_ge(s("f1_hl"), nth(n0 + c, EP, p))
                nc.scalar.activation(sg[:, p % 2, :], bank(p % 2), ACT.Silu, scale=1.0 / WSCALE).then_inc(s("silu_ready"), 1)

            def high_y(c, q):
                act.wait_ge(s("y1_ready"), 1 + nth(n0 + c, 2, q))
                act.wait_ge(s("scattered"), nth(n0 + c, 1))
                nc.scalar.activation(y1h[:, 4 * q:4 * q + 4, :].rearrange("p e c -> p (e c)"), y1f[:, q, :],
                                     ACT.Copy).then_inc(s("y1h_ready"), 1)
            high_gathered(0)

            def emit(c, first, last_):
                for p in range(EP):
                    silu(c, p)
                high_y(c, 0)
                if not last_:
                    act.wait_ge(s("f1_up"), nth(n0 + c, EP, EP - 1))
                    high_gathered(c + 1)
                if not first and puse + 1 < len(stage_order):
                    high(act, (puse + 1) * NC + c - 1, c - 1, 7, keeps(puse))
                high_y(c, 1)
            by_chunk1(act, emit)

        def ffn1_vector(dve, use, puse):
            n0 = use * NC
            dve.wait_ge(s("rank_psum"), use + 1)
            nc.vector.tensor_tensor(rankt.rearrange("p t r -> p (t r)"), bank(4)[:, 0:P],
                                    takent.rearrange("p t r -> p (t r)"), ALU.mult).then_inc(s("rank_ready"), 1)
            nc.vector.tensor_tensor(rankT[0:64, :], psum[0:64, 3, 0:SEQ], taken[0:64, :], ALU.mult).then_inc(s("rank_ready"), 1)
            dve.wait_ge(s("rank_ready"), 2 * use + 2)

            def token_by_slot(c):
                wait_apart(dve, s("gates_psum"), nth(n0 + c, 1))
                for b in range(BPC):
                    rk = rankt[:, :, ds((c * BPC + b) * E1, E1)].unsqueeze(3).broadcast_to([P, TPB, E1, TOPK])
                    sl = slotrow.unsqueeze(1).unsqueeze(1).broadcast_to([P, TPB, E1, TOPK])
                    nc.vector.tensor_tensor(oh[:, :, :, b, :], rk, sl, ALU.is_equal).then_inc(s("oh_ready"), 1)

            def low_gathered(c):
                for b in range(BPC):
                    dve.wait_ge(s("xgh_ready"), nth(n0 + c, BPC, b))
                    nc.vector.tensor_tensor(xgl[:, :, b, :], bank(4 + b).rearrange("p (e s) -> p e s", e=E1), xgh[:, :, b, :],
                                            ALU.subtract).then_inc(s("xg_ready"), 1)

            def gate_by_slot(c):
                wait_apart(dve, s("gates_psum"), 1 + nth(n0 + c, 1))
                for b in range(BPC):
                    rows = slice(b * TOPK, (b + 1) * TOPK)
                    g = psum[rows, 6, 0:4 * E1].rearrange("p (e l b) -> p e l b", e=E1, l=2)
                    nc.vector.tensor_copy(gslot[rows, :], g[:, :, 0, b]).then_inc(s("gslot_step"), 1)
                    wait_apart(dve, s("gslot_step"), nth(n0 + c, BPC, b))
                    last = nc.vector.tensor_tensor(gslot[rows, :], gslot[rows, :], g[:, :, 1, b], ALU.add)
                last.then_inc(s("b6_read"), 1)

            def slot_by_token(c, p):
                dve.wait_ge(s("ranks_psum"), nth(n0 + c, EP, p))
                dve.wait_ge(s("scattered"), nth(n0 + c, 1))
                nc.vector.tensor_scalar(oht[:, 2 * p:2 * p + 2, :].rearrange("p e t -> p (e t)"), bank(RKB[p % 2]), slotcol[:, 0:1],
                                        None, ALU.is_equal).then_inc(s("b6_read"), 1)

            def weigh(c, q):
                dve.wait_ge(s("f1_down"), 2 + nth(n0 + c, 2, q))
                dve.wait_ge(s("y1l_ready"), nth(n0 + c, 2, q))
                g = gslot[:, 4 * q:4 * q + 4].unsqueeze(2).broadcast_to([P, 4, C])
                nc.vector.scalar_tensor_tensor(y1f[:, q, :].rearrange("p (e c) -> p e c", e=4),
                                               bank(2).rearrange("p (e c) -> p e c", e=4), 1.0 / WSCALE, g,
                                               ALU.mult, ALU.mult).then_inc(s("y1_ready"), 1)

            def add(c):
                dve.wait_ge(s("scattered"), 1 + nth(n0 + c, 1))
                for b in range(BPC):
                    xc = x[:, ds(c * TPC + b * TPB, TPB), :].rearrange("p t c -> p (t c)")
                    last = nc.vector.scalar_tensor_tensor(xc, bank(SCB[b])[:, 0:TPB * C], HALF, xc, ALU.mult, ALU.add)
                last.then_inc(s("f1_added"), 1)
            token_by_slot(0)
            gate_by_slot(0)
            low_gathered(0)

            def emit(c, first, last_):
                job = not first and puse + 1 < len(stage_order)
                i = (puse + 1) * NC + c - 1
                if not last_:
                    token_by_slot(c + 1)
                if not first:
                    add(c - 1)
                if job:
                    wait_apart(dve, s("f1_added"), 1 + n0 + c)
                    statistics(dve, i, c - 1)
                slot_by_token(c, 0)
                if job:
                    moments(dve, i, c - 1)
                slot_by_token(c, 1)
                wait_apart(dve, s("b6_read"), 2 + nth(n0 + c, EP + 1))
                weigh(c, 0)
                slot_by_token(c, 2)
                slot_by_token(c, 3)
                if job:
                    normalise(dve, i, c - 1, lambda k: xnc[:, k, :])
                if not last_:
                    low_gathered(c + 1)
                weigh(c, 1)
                if not last_:
                    wait_apart(dve, s("y1_ready"), 1 + nth(n0 + c, 2, 1))
                    gate_by_slot(c + 1)
                if job:
                    low(dve, i, c - 1, 7)
            by_chunk1(dve, emit)
            add(NC - 1)
            dve.wait_ge(s("f1_added"), 1 + NC * (use + 1))

        def ffn1_gpsimd(pool, use, puse):
            n0 = use * NC
            for c in range(NC):
                ts = slice(c * TPC, (c + 1) * TPC)
                pool.wait_ge(s("xnh_ready"), nth(n0 + c, 1))
                nc.gpsimd.tensor_tensor(xnl[:, ts, :], xn[:, ts, :], xnh[:, ts, :], ALU.subtract).then_inc(s("xnl_ready"), 1)

            def emit(c, first, last_):
                def low_part(p):
                    pool.wait_ge(s("silu_ready"), 2 + nth(n0 + c, EP, p))
                    nc.gpsimd.tensor_tensor(h1l[:, p, :], sg[:, p % 2, :], h1h[:, p, :], ALU.subtract).then_inc(s("f1_hl"), 1)

                def low_y(q):
                    pool.wait_ge(s("y1h_ready"), nth(n0 + c, 2, q))
                    nc.gpsimd.tensor_tensor(y1l[:, 4 * q:4 * q + 4, :].rearrange("p e c -> p (e c)"), y1f[:, q, :],
                                            y1h[:, 4 * q:4 * q + 4, :].rearrange("p e c -> p (e c)"),
                                            ALU.subtract).then_inc(s("y1l_ready"), 1)
                for p in range(EP):
                    low_part(p)
                if not first and puse + 1 < len(stage_order):
                    inverse_deviation(pool, (puse + 1) * NC + c - 1, c - 1)
                low_y(0)
                low_y(1)
            by_chunk1(pool, emit)

        def sample(c, k, q):
            return c * WS + k * SU + q + 1

        def half(c, k, q, jt):
            return (c * WS + k * SU + q) * 2 + jt + 1

        def item(c, g):
            return c * SG + g

        KQ = 3

        def group_of(c, k):
            if isinstance(k, int) and k == 0:
                return (c, SG - 1)
            return (c + 1, k - 1) if c + 1 < NC else None

        def first_round(k):
            return isinstance(k, int) and k == 0

        def rounds(eng, emit, between):
            emit(0)
            between(0)
            with eng.Fori(1, SG - 2) as k:
                emit(k)
            between(1)
            emit(SG - 2)
            between(2)

        def la_tensor(pe, puse):
            prep_tensor(pe, puse)
            all_xT(pe, puse)
            pe.wait_ge(s("ww_split"), 1)
            for t in range(NT):
                last = matmul3(pe, bank(0)[:, t * 2 * WH:(t + 1) * 2 * WH], xTh[:, t * P:(t + 1) * P],
                               xTl[:, t * P:(t + 1) * P], wwh[:, :], wwl[:, :])
            last.then_inc(s("wave_ready"), 1)
            pe.wait_ge(s("kw_split"), 2)

            def project(c, g, b, ring):
                pe.wait_ge(s("sil_ready"), 2 + item(c, g) - ring + 1)
                cs = ds(c * CHUNK, CHUNK)
                kh, kl = (v[:, ds(g, 1), :, :].rearrange("p g d r -> p (g d r)") for v in (kwh, kwl))
                matmul3(pe, bank(b), kh, kl, xTh[:, cs], xTl[:, cs]).then_inc(s("kp_ready"), 1)
            for g in range(SG - 1):
                project(0, g, 6 + g % 2, 2)
            pe.wait_ge(s("stag_ready"), 1)
            for c in range(NC):
                for k in range(TPC):
                    last = nc.tensor.transpose(psum[0:POSK, 1 + c, k * P:(k + 1) * P], stag[:, c * TPC + k, :], ident[:, :])
                last.then_inc(s("posT_psum"), 1)
            pe.wait_ge(s("ld_df"), 16)
            pe.wait_ge(s("ld_selS"), 32)
            pe.wait_ge(s("ld_ow"), 16)
            pe.wait_ge(s("posT"), NC)

            def result(c):
                pe.wait_ge(s("acc_sum"), 2 + nth(c, WS, WS - 1))
                pe.wait_ge(s("yw_ready"), nth(c, 1))
                if puse + 1 < len(stage_order):
                    pe.wait_ge(s("xT_ready"), XT0 + (puse + 1) * NC + c)
                for k in range(TPC):
                    last = nc.tensor.matmul(bank(7)[:, k * P:(k + 1) * P], wacc[c % 2][:, k * P:(k + 1) * P], ow[:, :],
                                            start=True, stop=True)
                last.then_inc(s("y_psum"), 1)

            def differences(c):
                pe.wait_ge(s("dx_ready"), nth(c, 1))
                for b in range(BPC):
                    x0 = xn[:, c * TPC + b * TPB, :]
                    x1 = xn[:, c * TPC + b * TPB + 1, :]
                    for jt, (m0, m1) in enumerate(((0, 1), (3, 2))):
                        o = bank(3)[:, (b * TPB + jt) * C:(b * TPB + jt + 1) * C]
                        nc.tensor.matmul(o, diffm[:, m0, :], x0, start=True, stop=False)
                        last = nc.tensor.matmul(o, diffm[:, m1, :], x1, start=False, stop=True)
                last.then_inc(s("dx_psum"), 1)
            differences(0)
            for c in range(NC):
                r = c % 2
                cs = slice(c * CHUNK, (c + 1) * CHUNK)

                def positions(n, g, k, q):
                    pe.wait_ge(s("relu_ready"), half(c, k, q, 1))
                    nc.tensor.matmul(bank((r + q) % PR), selS[0:POSK, n, :], posT[0:POSK, cs],
                                     start=True, stop=True).then_inc(s("pos_ready"), 1)
                    pe.wait_ge(s("ws_ready"), sample(c, k, q))
                    nc.tensor.matmul(bank(6), selW[:, q % SU, :], kwt[:, g, cs], start=True,
                                     stop=True).then_inc(s("w_ready"), 1)

                def samples(k, q):
                    pe.wait_ge(s("prod_ready"), sample(c, k, q))
                    for jt in range(2):
                        v = (2 * (r + q) + jt) % UR
                        pe.wait_ge(s("clip_ready"), half(c, k, q, jt))
                        for b in range(BPC):
                            last = nc.tensor.matmul(bank(4 + (r + q) % 2)[:, b * SEQ:(b + 1) * SEQ], dxs[:, r, b, jt, :],
                                                    uu[:, v, b * SEQ:(b + 1) * SEQ], start=(jt == 0 and b == 0),
                                                    stop=(jt == 1), skip_group_check=True)
                        last.then_inc(s("uu_used"), 1)

                pe.wait_ge(s("kwt_ready"), 2 + item(c, 0) + 1)
                positions(ds(0, 1), ds(0, 1), 0, 0)
                pe.wait_ge(s("dx_ready"), 1 + nth(c, 1))

                def round_(k):
                    for q in range(SU):
                        if q == SU - 1:
                            pe.wait_ge(s("kwt_ready"), 2 + item(c, k + 1) + 1)
                        positions(ds(k * SU + q + 1, 1), ds(k, 1) if q < SU - 1 else ds(k + 1, 1), k, q + 1)
                        samples(k, q)
                        if q == KQ and group_of(c, k):
                            project(*group_of(c, k), 2, 1)
                        if q == KQ + 1 and c and first_round(k):
                            result(c - 1)

                def between(m):
                    if m == 2 and c + 1 < NC:
                        differences(c + 1)
                    if m == 2 and c and puse + 1 < len(stage_order):
                        turn_rows(pe, (puse + 1) * NC + c - 1, 7, lambda k: xnc[:, k, :], 0)
                rounds(pe, round_, between)
                samples(SG - 1, 0)
                if group_of(c, SG - 1):
                    project(*group_of(c, SG - 1), 2, 1)
            result(NC - 1)

        def la_scalar(act, puse):
            act.wait_ge(s("ld_kw"), 16)
            for d in range(2):
                nc.scalar.activation(kwh[:, :, d, :], rawkw[:, 0:SG, :], ACT.Copy, scale=WSCALE).then_inc(s("hi_kw"), 1)
            split_act(act, wwh[:, :], wwr[:, :], "ld_ww", 16)
            prep_scalar(act, puse)
            act.wait_ge(s("wz_ready"), 1)
            wzf = wz[:, :, :, :].rearrange("p t a h -> p (t a h)")
            nc.scalar.activation(wzf, wzf, ACT.Silu).then_inc(s("wave_act"), 1)
            act.wait_ge(s("wave_act"), 1)
            nc.scalar.activation(wz[:, :, 1, :], wz[:, :, 1, :], ACT.Tanh).then_inc(s("wave_act"), 1)
            nc.scalar.activation(wz[:, :, 0, :], wz[:, :, 0, :], ACT.Sigmoid).then_inc(s("wave_act"), 1)
            act.preload_act_table(ACT.Silu)
            act.wait_ge(s("ld_kb"), 32)

            def kernel_high(c, g, b):
                wait_apart(act, s("kp_ready"), 1 + item(c, g))
                nc.scalar.activation(kwt[:, ds(g, 1), ds(c * CHUNK, CHUNK)].rearrange("p g t -> p (g t)"), bank(b),
                                     ACT.Silu, bias=kb[:, ds(g, 1)], scale=1.0 / WSCALE)

            def kernel_full(c, g, b, slot, ring):
                wait_apart(act, s("kwt_ready"), 2 + item(c, g) - ring + 1)
                nc.scalar.activation(sil[:, slot, :], bank(b), ACT.Silu, bias=kb[:, ds(g, 1)], scale=1.0 / WSCALE
                                     ).then_inc(s("sil_ready"), 1)
            for g in range(SG - 1):
                kernel_high(0, g, 6 + g % 2)
                kernel_full(0, g, 6 + g % 2, g % 2, 2)
            for c in range(NC):
                act.wait_ge(s("posT_psum"), c + 1)
                nc.scalar.activation(posT[0:POSK, c * CHUNK:(c + 1) * CHUNK], psum[0:POSK, 1 + c, :],
                                     ACT.Copy).then_inc(s("posT"), 1)
            act.wait_ge(s("ld_mj"), 16)

            def result_silu(c):
                act.wait_ge(s("y_psum"), nth(c, 1))
                act.wait_ge(s("res_done"), nth(c, 1))
                nc.scalar.activation(yw, bank(7), ACT.Silu).then_inc(s("yw_ready"), 1)

            def copy_differences(c):
                act.wait_ge(s("dx_psum"), nth(c, 1))
                nc.scalar.activation(dxs[:, c % 2].rearrange("p b t c -> p (b t c)"), bank(3), ACT.Copy).then_inc(s("dx_ready"), 1)
            copy_differences(0)
            for c in range(NC):
                r = c % 2

                def relus(k, q):
                    act.wait_ge(s("pos_ready"), sample(c, k, q))
                    for jt in range(2):
                        act.wait_ge(s("uu_used"), half(c, k, q, jt))
                        nc.scalar.activation(uu[:, (2 * (r + q) + jt) % UR, :], bank((r + q) % PR), ACT.Relu,
                                             bias=minusj[:, jt:jt + 1]).then_inc(s("relu_ready"), 1)

                def copy_weights(k, q):
                    act.wait_ge(s("w_ready"), sample(c, k, q))
                    act.wait_ge(s("prod_ready"), sample(c, k, q))
                    nc.scalar.activation(wsm[:, (r + q) % 2, :], bank(6), ACT.Copy).then_inc(s("ws_ready"), 1)

                def round_(k):
                    for q in range(SU):
                        relus(k, q)
                        copy_weights(k, q)
                        if q == 0 and c and first_round(k):
                            kernel_high(*group_of(c - 1, SG - 1), 2)
                        if q == 1 and c and first_round(k):
                            kernel_full(*group_of(c - 1, SG - 1), 2, 0, 1)
                        if q == KQ + 1 and group_of(c, k):
                            kernel_high(*group_of(c, k), 2)
                        if q == KQ + 2 and group_of(c, k):
                            kernel_full(*group_of(c, k), 2, 0, 1)
                        if q == KQ + 3 and c and first_round(k):
                            result_silu(c - 1)
                rounds(act, round_, lambda m: None)
                relus(SG - 1, 0)
                copy_weights(SG - 1, 0)
                if c + 1 < NC:
                    copy_differences(c + 1)
                if c and puse + 1 < len(stage_order):
                    high(act, (puse + 1) * NC + c - 1, c - 1, 7, keeps(puse))
            result_silu(NC - 1)

        def la_vector(dve, puse):
            dve.wait_ge(s("hi_kw"), 2)
            for d in range(2):
                nc.vector.scalar_tensor_tensor(kwl[:, :, d, :], rawkw[:, 0:SG, :], WSCALE, kwh[:, :, d, :],
                                               ALU.mult, ALU.subtract).then_inc(s("kw_split"), 1)
            split_dve(dve, wwl[:, :], wwr[:, :], wwh[:, :], "ld_ww", "ww_split")
            prep_vector(dve, puse)
            n = [0]

            def step(ins):
                n[0] += 1
                ins.then_inc(s("wave_step"), 1)
                dve.wait_ge(s("wave_step"), n[0])
            dve.wait_ge(s("wave_ready"), 1)
            dve.wait_ge(s("ld_wb"), 16)
            wzf = wz[:, :, :, :].rearrange("p t a h -> p t (a h)")
            nc.vector.scalar_tensor_tensor(wzf, bank(0)[:, 0:NT * 2 * WH].rearrange("p (t w) -> p t w", t=NT), 1.0 / WSCALE,
                                           wb[:, :].unsqueeze(1).broadcast_to([P, NT, 2 * WH]),
                                           ALU.mult, ALU.add).then_inc(s("wz_ready"), 1)
            dve.wait_ge(s("wave_act"), 3)
            dve.wait_ge(s("ld_sg"), 32)
            nc.vector.tensor_reduce(wav[:, 0, :], wz[:, :, 0, :], AX, ALU.add)
            step(nc.vector.tensor_reduce(wav[:, 1, :], wz[:, :, 1, :], AX, ALU.add))
            nc.vector.tensor_scalar(wav[:, 2, :], wav[:, 0, :], (MAX_FREQ - MIN_FREQ) / WH, MIN_FREQ, ALU.mult, ALU.add)
            step(nc.vector.scalar_tensor_tensor(wav[:, 3, :], wav[:, 1, :], MAX_FREQ / WH, tokpos[:, :], ALU.mult, ALU.add))
            step(nc.vector.tensor_tensor(pos[:, :, :], sgrid[:, :].unsqueeze(1).broadcast_to([P, NT, WS]),
                                         wav[:, 2, :].unsqueeze(2).broadcast_to([P, NT, WS]), ALU.mult))
            step(nc.vector.tensor_tensor(pos[:, :, :], pos[:, :, :], wav[:, 3, :].unsqueeze(2).broadcast_to([P, NT, WS]), ALU.add))
            step(nc.vector.tensor_scalar(pos[:, :, :], pos[:, :, :], 0.0, SEQ - 1.0, ALU.max, ALU.min))
            step(nc.vector.tensor_copy(pos16[:, :, :], pos[:, :, :]))
            nc.vector.tensor_copy(stag[:, :, 0:WS], pos16[:, :, :])
            step(nc.vector.tensor_tensor(posr[:, :, :], pos[:, :, :], pos16[:, :, :], ALU.subtract))
            step(nc.vector.tensor_copy(pos16[:, :, :], posr[:, :, :]))
            nc.vector.tensor_copy(stag[:, :, WS:2 * WS], pos16[:, :, :])
            nc.vector.tensor_tensor(stag[:, :, 2 * WS:POSK], posr[:, :, :], pos16[:, :, :],
                                    ALU.subtract).then_inc(s("stag_ready"), 1)

            def add_result(c):
                dve.wait_ge(s("yw_ready"), 1 + nth(c, 1))
                xc = x[:, c * TPC:(c + 1) * TPC, :].rearrange("p t c -> p (t c)")
                nc.vector.tensor_tensor(xc, xc, yw, ALU.add).then_inc(s("res_done"), 1)
            for c in range(NC):
                r = c % 2

                def clips(k, q):
                    for jt in range(2):
                        v = (2 * (r + q) + jt) % UR
                        dve.wait_ge(s("relu_ready"), 2 * PR + half(c, k, q, jt))
                        nc.vector.tensor_scalar(uu[:, v, :], uu[:, v, :], 1.0, None, ALU.min).then_inc(s("clip_ready"), 1)

                def weigh(k, q):
                    dve.wait_ge(s("uu_used"), UR + half(c, k, q, 1))
                    dve.wait_ge(s("ws_ready"), 1 + sample(c, k, q))
                    dve.wait_ge(s("acc_sum"), sample(c, k, q))
                    nc.vector.tensor_tensor(prod[:, (r + q) % 2, :], wsm[:, (r + q) % 2, :], bank(4 + (r + q) % 2),
                                            ALU.mult).then_inc(s("prod_ready"), 1)
                job = c and puse + 1 < len(stage_order)
                i = (puse + 1) * NC + c - 1

                def round_(k):
                    for q in range(SU):
                        clips(k, q + 1)
                        weigh(k, q)

                def between(m):
                    if m == 0 and c:
                        add_result(c - 1)
                    if m == 0 and job:
                        dve.wait_ge(s("res_done"), 1 + c)
                        statistics(dve, i, c - 1)
                        moments(dve, i, c - 1)
                    if m == 1 and job:
                        normalise(dve, i, c - 1, lambda k: xnc[:, k, :])
                clips(0, 0)
                rounds(dve, round_, between)
                weigh(SG - 1, 0)
                if job:
                    low(dve, i, c - 1, 7)
            add_result(NC - 1)
            dve.wait_ge(s("res_done"), 1 + NC)

        def la_gpsimd(pool, puse):
            prep_gpsimd(pool, puse)

            def kernel_low(c, g, slot):
                pool.wait_ge(s("sil_ready"), 2 + item(c, g) + 1)
                lo = kwt[P // 2:P, ds(g, 1), ds(c * CHUNK, CHUNK)].rearrange("p g t -> p (g t)")
                nc.gpsimd.tensor_tensor(lo, sil[P // 2:P, slot, :], lo, ALU.subtract).then_inc(s("kwt_ready"), 1)
            for g in range(SG - 1):
                kernel_low(0, g, g % 2)
            pool.wait_ge(s("kwt_ready"), 2 + SG - 1)
            for c in range(NC):
                r = c % 2
                if c >= 2:
                    pool.wait_ge(s("yw_ready"), 1 + nth(c - 2, 1))
                nc.gpsimd.memset(wacc[r], 0.0).then_inc(s("wacc0"), 1)
                pool.wait_ge(s("wacc0"), nth(c, 1))

                def add(k, q):
                    pool.wait_ge(s("prod_ready"), 2 + sample(c, k, q))
                    pool.wait_ge(s("acc_sum"), 1 + sample(c, k, q))
                    nc.gpsimd.tensor_tensor(wacc[r], wacc[r], prod[:, (r + q) % 2, :], ALU.add).then_inc(s("acc_sum"), 1)

                def low_apart(group, k, q):
                    if group:
                        pool.wait_ge(s("acc_sum"), 2 + sample(c, k, q))
                        kernel_low(*group, 0)
                        pool.wait_ge(s("kwt_ready"), 2 + item(*group) + 1)

                def round_(k):
                    for q in range(SU):
                        add(k, q)
                        if q == 1 and c and first_round(k):
                            low_apart(group_of(c - 1, SG - 1), k, q)
                        if q == KQ + 2:
                            low_apart(group_of(c, k), k, q)

                def between(m):
                    if m == 0 and c and puse + 1 < len(stage_order):
                        inverse_deviation(pool, (puse + 1) * NC + c - 1, c - 1)
                rounds(pool, round_, between)
                add(SG - 1, 0)

        @block.gpsimd
        def _(pool):
            pool.sem_inc(s("acc_sum"), 2)
            pool.sem_inc(s("f0_hl"), H0)
            pool.sem_inc(s("f1_hl"), 2)
            pool.sem_inc(s("y1l_ready"), 2)
            pool.sem_inc(s("rms_ready"), TPB)
            pool.sem_inc(s("kwt_ready"), 2)
            nc.gpsimd.memset(neghalf[:, :], -0.5)
            nc.gpsimd.memset(zrow[:, :], 0.0).then_inc(s("consts"), 1)
            nc.gpsimd.memset(gst[:, :, :], 0.0).then_inc(s("gst0"), 1)
            pool.wait_ge(s("gst0"), 1)
            nc.gpsimd.memset(gst[:, :, E0:U0], 1.0).then_inc(s("consts"), 1)
            nc.gpsimd.iota(revidx[:, :], pattern=[[-1, E0]], base=E0, channel_multiplier=0,
                           allow_small_or_imprecise_dtypes=True).then_inc(s("consts"), 1)
            pool.wait_ge(s("consts"), 3)
            uses = {}
            for pu, st in enumerate(stage_order):
                use = uses.get(st, 0)
                uses[st] = use + 1
                if st == "AT":
                    at_gpsimd(pool, pu)
                elif st == "LA":
                    la_gpsimd(pool, pu)
                else:
                    prep_gpsimd(pool, pu)
                    if st == "F0" and use == 0:
                        for k in range(GUP):
                            us = slice(k * U0 // GUP, (k + 1) * U0 // GUP)
                            pool.wait_ge(s("hi_gu"), k + 1)
                            nc.gpsimd.tensor_tensor(flat(gul[:, us, :]), flat(rawgu[:, us, :]), flat(guh[:, us, :]),
                                                    ALU.subtract).then_inc(s("gu_split"), 1)
                    if st == "F0":
                        experts_gpsimd(pool, "f0", use, pu, U0, low_pieces(pool, use, st))
                    else:
                        ffn1_gpsimd(pool, use, pu)

        @block.scalar
        def _(act):
            act.sem_inc(s("f0_out"), 1)
            act.sem_inc(s("silu_ready"), 2)
            act.sem_inc(s("vb_ready"), 1)
            act.sem_inc(s("qkT_ready"), 1)
            act.sem_inc(s("qn_ready"), 2)
            act.sem_inc(s("exp_ready"), 2)
            act.sem_inc(s("ws_ready"), 1)
            act.sem_inc(s("relu_ready"), 2 * PR)
            act.sem_inc(s("dx_ready"), 1)
            act.sem_inc(s("sil_ready"), 2)
            act.sem_inc(s("yw_ready"), 1)
            split_act(act, rwh[:, :], rwr[:, :], "ld_rw", 16)
            uses = {}
            for pu, st in enumerate(stage_order):
                use = uses.get(st, 0)
                uses[st] = use + 1
                if st == "AT":
                    at_scalar(act, pu)
                    continue
                if st == "LA":
                    la_scalar(act, pu)
                    continue
                if st == "F1" and use == 0:
                    split_act(act, cwh[:, :], cwr[:, :], "ld_cw", 16)
                prep_scalar(act, pu)
                if st == "F0" and use == 0:
                    act.wait_ge(s("ld_gu"), 48)
                    for k in range(GUP):
                        us = slice(k * U0 // GUP, (k + 1) * U0 // GUP)
                        nc.scalar.activation(flat(guh[:, us, :]), flat(rawgu[:, us, :]), ACT.Copy, scale=WSCALE)
                        nc.scalar.activation(flat(rawgu[:, us, :]), flat(rawgu[:, us, :]), ACT.Copy,
                                             scale=WSCALE).then_inc(s("hi_gu"), 1)
                if st == "F1":
                    route1_scalar(act, use, pu)
                    ffn1_scalar(act, use, pu)
                if st == "F0":
                    route0_scalar(act, use)
                    ffn0_scalar(act, use, pu)

        @block.vector
        def _(dve):
            dve.sem_inc(s("xT_ready"), XT0)
            dve.sem_inc(s("f0_hT"), H0)
            dve.sem_inc(s("f0_su"), H0)
            dve.sem_inc(s("f0_added"), 1)
            dve.sem_inc(s("xg_ready"), BPC)
            dve.sem_inc(s("b6_read"), 2)
            dve.sem_inc(s("y1_ready"), 1)
            dve.sem_inc(s("f1_added"), 1)
            dve.sem_inc(s("ss_ready"), 2)
            dve.sem_inc(s("rot_ready"), R0)
            dve.sem_inc(s("pv_taken"), 2)
            dve.sem_inc(s("prod_ready"), 2)
            dve.sem_inc(s("res_done"), 1)
            split_dve(dve, rwl[:, :], rwr[:, :], rwh[:, :], "ld_rw", "rw_split")
            dve.wait_ge(s("consts"), 3)
            dve.wait_ge(s("ld_ident"), 16)
            nc.vector.tensor_copy(identh[:, :], ident[:, :]).then_inc(s("identh"), 1)
            uses = {}
            for pu, st in enumerate(stage_order):
                use = uses.get(st, 0)
                uses[st] = use + 1
                if st == "AT":
                    at_vector(dve, pu)
                    continue
                if st == "LA":
                    la_vector(dve, pu)
                    continue
                if st == "F1" and use == 0:
                    split_dve(dve, cwl[:, :], cwr[:, :], cwh[:, :], "ld_cw", "cw_split")
                prep_vector(dve, pu)
                if st == "F1":
                    route1_vector(dve, use)
                    ffn1_vector(dve, use, pu)
                if st == "F0":
                    route0_vector(dve, use)
                    if use == 0:
                        split_dve(dve, flat(wd16[:, 1]), flat(rawdn), flat(wd16[:, 0]), "ld_dn", "dn_split")
                    ffn0_vector(dve, use, pu)
            dve.sem_inc(s("x_final"), 1)

        @block.tensor
        def _(pe):
            pe.wait_ge(s("ld_ident"), 16)
            pe.sem_inc(s("f0_down"), H0)
            pe.sem_inc(s("f0_turned"), 1)
            pe.sem_inc(s("f1_down"), 2)
            pe.sem_inc(s("scattered"), 1)
            pe.sem_inc(s("gates_psum"), 1)
            pe.sem_inc(s("tr_ready"), 4)
            pe.sem_inc(s("pv_ready"), HG)
            pe.sem_inc(s("uu_used"), UR)
            pe.wait_ge(s("consts"), 3)
            uses = {}
            for pu, st in enumerate(stage_order):
                use = uses.get(st, 0)
                uses[st] = use + 1
                if st == "AT":
                    at_tensor(pe, pu)
                    continue
                if st == "LA":
                    la_tensor(pe, pu)
                    continue
                prep_tensor(pe, pu)
                if st == "F1":
                    route1_tensor(pe, use, pu)
                    ffn1_tensor(pe, use, pu)
                if st == "F0":
                    route0_tensor(pe, use, pu)
                    ffn0_tensor(pe, use, pu)


def _constants():
    ident = np.eye(P, dtype=np.float32)
    sel0 = np.zeros((64, U0, P), np.float16)
    for u in range(U0):
        sel0[u, u] = 1 / WSCALE
        sel0[32 + u, u] = 1 / WSCALE
    selR = np.zeros((BATCH, E1, NC, E1, BPC, TOPK), np.float16)
    for b in range(BATCH):
        for e in range(E1):
            selR[b, e, b // BPC, e, b % BPC, :] = 1
    upto = np.triu(np.ones((P, P), np.float16))
    ones = np.ones((P, P), np.float16)
    slotrow = np.tile(np.arange(1, TOPK + 1, dtype=np.float16), (P, 1))
    slotcol = (np.arange(P, dtype=np.float32) % TOPK + 1)[:, None]
    j = np.arange(HD // 2, dtype=np.float32)
    freqs = np.power(np.float32(ROPE_BASE), -j / np.float32(HD // 2)).astype(np.float32)
    rad = (np.arange(SEQ, dtype=np.float32)[:, None] * freqs[None, :]).astype(np.float32).astype(np.float64)
    cos, sin = np.cos(rad).astype(np.float32), np.sin(rad).astype(np.float32)
    cosd = np.concatenate([cos, cos], 1).reshape(TPB, P, HD).transpose(1, 0, 2).copy()
    sind = np.concatenate([-sin, sin], 1).reshape(TPB, P, HD).transpose(1, 0, 2).copy()
    selS = np.zeros((POSK, WS, P), np.float16)
    for t in range(WS):
        selS[[p * WS + t for p in range(PIECES)], t] = 1
    minusj = -np.arange(SEQ, dtype=np.float32).reshape(2, P).T.copy()
    minusj[P - 1, 1] = 1
    d = np.zeros((P, 4, P), np.float32)
    for k in range(P):
        d[k, 0, k] = -1
        if k:
            d[k, 0, k - 1] = 1
            d[k, 2, k - 1] = 1
        if k < P - 1:
            d[k, 2, k] = -1
    d[0, 1, P - 1] = 1
    d[0, 3, P - 1] = 1
    selW = np.zeros((2, SU, WH, SU, WH, WD), np.float16)
    for t in range(SU):
        for h in range(WH):
            selW[:, t, h, t, h, :] = 1
    sgrid = np.tile(np.arange(WS, dtype=np.float32) - (WS // 2), (P, 1))
    tokpos = np.zeros((P, NT), np.float32)
    for t in range(NT):
        tokpos[:, t] = np.arange(P) + (t % TPB) * P
    return {"ident": ident, "sel0": sel0, "selR": selR.reshape(BATCH * E1, NC * E1, P), "upto": upto,
            "ones": ones, "slotrow": slotrow, "slotcol": slotcol, "cosd": cosd, "sind": sind,
            "selS": selS, "minusj": minusj, "diffm": d, "selW": selW.reshape(P, SU, P), "sgrid": sgrid, "tokpos": tokpos}


_TRANSPOSED = {"L0_ffn_router_w": (1, 0), "L0_ffn_shared_gate_w": (1, 0), "L0_ffn_shared_up_w": (1, 0),
               "L0_ffn_shared_down_w": (1, 0), "L0_attn_wv": (2, 1, 0), "L1_attn_wave_w": (1, 0),
               "L1_attn_kernel_w": (3, 1, 2, 0), "L1_attn_kernel_b": (2, 0, 1),
               "L1_attn_out_w": (1, 0), "L1_ffn_choice_w": (1, 0)}
_SHAPED = {"L1_attn_kernel_w": (WH, WK // SU, SU, C), "L1_attn_kernel_b": (WH, WK // SU, SU)}
_MERGED = {"L1_attn_kernel_w": (C, WK // SU, SU * WH), "L1_attn_kernel_b": (SU * WH, WK // SU)}
_STAGES = ["F0", "AT", "F0", "F1", "LA", "F1"]


def _laid_out(name, v):
    v = v.reshape(_SHAPED.get(name, v.shape))
    v = v.transpose(_TRANSPOSED.get(name, range(v.ndim)))
    return np.ascontiguousarray(v.reshape(_MERGED.get(name, v.shape)))


def kernel(**inputs):
    import concourse.bacc as _bacc
    from concourse.bass_utils import run_bass_kernel_spmd as _run

    nc = _bacc.Bacc("TRN2", target_bir_lowering=False, num_devices=1)
    host = dict(_constants())
    for name, v in inputs.items():
        v = np.asarray(v)
        host[name] = _laid_out(name, v)
    arrays, aps = {}, {"_stages": _STAGES}
    for name, v in host.items():
        arrays[f"in_{name}"] = v
        aps[name] = nc.dram_tensor(f"in_{name}", v.shape, mybir.dt.from_np(v.dtype), kind="ExternalInput").ap()
    out = nc.dram_tensor("out_x", (BATCH, SEQ, C), F32, kind="ExternalOutput").ap()
    macaron_kernel(nc, aps, out)
    r = _run(nc, [arrays], core_ids=[0])
    return r.results[0]["out_x"]
```
